# Optimizing a Trainium2 kernel written in Bass

```python
import numpy as np
import jax
import jax.numpy as jnp

def _softmax(x, axis=-1):
    return jax.nn.softmax(x, axis=axis)

def _gelu(x):
    return jax.nn.gelu(x, approximate=True)

def _silu(x):
    return jax.nn.silu(x)

def _sigmoid(x):
    return jax.nn.sigmoid(x)

def _layernorm(x, axis=-1, eps=1e-05):
    m = jnp.mean(x, axis=axis, keepdims=True)
    v = jnp.var(x, axis=axis, keepdims=True)
    return (x - m) / jnp.sqrt(v + eps)

def _scatter_add(tgt, idx, src, axis=0):
    return tgt.at[idx].add(src)

def _segment_sum(src, seg, n):
    return jax.ops.segment_sum(src, seg, n)
kernel_name = 'mk_xattn_ffn_d2_seqx_r8_ef681f'

def setup_inputs(seed: int=0):
    np.random.seed(seed)
    _w = jnp.asarray

    def _rec_inputs():
        import jax
        import jax.numpy as jnp
        _rk = jax.random.key(seed)
        x = -0.0003929 + 0.9999 * jax.random.normal(jax.random.fold_in(_rk, 1), (32, 128, 128), jnp.float32)
        _lenS = 128 - jax.random.randint(jax.random.fold_in(_rk, 7), (32,), 0, max(1, 128 // 4) + 1, jnp.int32)
        _lenS2 = 77 - jax.random.randint(jax.random.fold_in(_rk, 8), (32,), 0, max(1, 77 // 4) + 1, jnp.int32)
        _ctx_768P = jax.random.normal(jax.random.fold_in(_rk, 11), (32, 16, 96), jnp.float32)
        _ctx_768c = jax.random.dirichlet(jax.random.fold_in(_rk, 511), 0.3 * jnp.ones((16,), jnp.float32), (32, 77))
        _ctx_768t = jnp.einsum('bsk,bkd->bsd', _ctx_768c, _ctx_768P)
        _ctx_768t = _ctx_768t * jax.lax.rsqrt(jnp.mean(jnp.square(_ctx_768t)) + 1e-12) * 0.953939
        ctx_768 = 2.09791e-05 + 1.00001 * (_ctx_768t + 0.3 * jax.random.normal(jax.random.fold_in(_rk, 611), (32, 77, 96), jnp.float32))
        return (x, ctx_768)
    x, ctx_768 = _rec_inputs()

    def _L0_xattn_setup():
        import jax, jax.numpy as jnp
        import numpy as np
        HEADS = 16
        DIM_HEAD = 64
        SCALE = DIM_HEAD ** (-0.5)
        key = jax.random.key(seed)
        ks = jax.random.split(key, 7)
        B, SQ, SKV, QD, CD, ID = (4, 512, 128, 128, 96, HEADS * DIM_HEAD)
        s = lambda d: 1.0 / np.sqrt(d)
        return {'x': jax.random.normal(ks[0], (B, SQ, QD), jnp.float32), 'context': jax.random.normal(ks[1], (B, SKV, CD), jnp.float32), 'Wq': jax.random.normal(ks[2], (QD, ID), jnp.float32) * s(QD), 'Wk': jax.random.normal(ks[3], (CD, ID), jnp.float32) * s(CD), 'Wv': jax.random.normal(ks[4], (CD, ID), jnp.float32) * s(CD), 'Wo': jax.random.normal(ks[5], (ID, QD), jnp.float32) * s(ID), 'bo': jnp.zeros((QD,), jnp.float32)}
    _L0_xattn_all = _L0_xattn_setup()
    _L0_xattn_in = {k: v for k, v in _L0_xattn_all.items() if k in ('Wq', 'Wk', 'Wv', 'Wo', 'bo')}
    del _L0_xattn_all

    def _L0_ffn_setup():
        import jax, jax.numpy as jnp
        import numpy as np
        DIM = 128
        N_EXPERTS = 16
        TOP_K = 4
        N_GROUP = 4
        TOPK_GROUP = 2
        MOE_INTER = 64
        SHARED_INTER = 256
        ROUTED_SCALE = 2.5

        def relu2(x):
            return jnp.square(jax.nn.relu(x))

        def _router(x2, gate_w, bias_e):
            T = x2.shape[0]
            logits = x2 @ gate_w.T
            scores = jax.nn.sigmoid(logits)
            sc = jax.lax.stop_gradient(scores + bias_e[None, :])
            grp = sc.reshape(T, N_GROUP, N_EXPERTS // N_GROUP)
            top2, _ = jax.lax.top_k(grp, 2)
            group_scores = top2.sum(-1)
            _, gidx = jax.lax.top_k(group_scores, TOPK_GROUP)
            rows = jnp.arange(T)[:, None]
            gmask = jnp.zeros((T, N_GROUP), dtype=sc.dtype).at[rows, gidx].set(1.0)
            smask = jnp.repeat(gmask, N_EXPERTS // N_GROUP, axis=1)
            masked = jnp.where(smask > 0, sc, 0.0)
            _, topk_idx = jax.lax.top_k(masked, TOP_K)
            topk_w = jnp.take_along_axis(scores, topk_idx, axis=1)
            topk_w = topk_w / (topk_w.sum(-1, keepdims=True) + 1e-20)
            topk_w = topk_w * ROUTED_SCALE
            return (topk_idx, topk_w)
        key = jax.random.key(seed)
        ks = jax.random.split(key, 6)
        hidden_states = jax.random.normal(ks[0], (2, 256, DIM), dtype=jnp.float32)
        gate_w = jax.random.normal(ks[1], (N_EXPERTS, DIM), dtype=jnp.float32) * 0.02
        bias_e = jnp.zeros((N_EXPERTS,), dtype=jnp.float32)
        up_w = jax.random.normal(ks[2], (N_EXPERTS, MOE_INTER, DIM), dtype=jnp.float32) * 0.02
        down_w = jax.random.normal(ks[3], (N_EXPERTS, DIM, MOE_INTER), dtype=jnp.float32) * 0.02
        shared_up = jax.random.normal(ks[4], (SHARED_INTER, DIM), dtype=jnp.float32) * 0.02
        shared_down = jax.random.normal(ks[5], (DIM, SHARED_INTER), dtype=jnp.float32) * 0.02
        return {'hidden_states': hidden_states, 'gate_w': gate_w, 'bias_e': bias_e, 'up_w': up_w, 'down_w': down_w, 'shared_up': shared_up, 'shared_down': shared_down}
    _L0_ffn_all = _L0_ffn_setup()
    _L0_ffn_in = {k: v for k, v in _L0_ffn_all.items() if k in ('gate_w', 'bias_e', 'up_w', 'down_w', 'shared_up', 'shared_down')}
    del _L0_ffn_all

    def _L1_xattn_setup():
        import jax, jax.numpy as jnp
        import numpy as np
        HEADS = 16
        DIM_HEAD = 64
        SCALE = DIM_HEAD ** (-0.5)
        QUERY_DIM = 128
        CONTEXT_DIM = 96
        INNER_DIM = HEADS * DIM_HEAD
        key = jax.random.key(seed)
        ks = jax.random.split(key, 7)
        B, Nq, Nk = (8, 512, 77)
        x = jax.random.normal(ks[0], (B, Nq, QUERY_DIM), dtype=jnp.float32)
        context = jax.random.normal(ks[1], (B, Nk, CONTEXT_DIM), dtype=jnp.float32)
        Wq = jax.random.normal(ks[2], (QUERY_DIM, INNER_DIM), dtype=jnp.float32) * QUERY_DIM ** (-0.5)
        Wk = jax.random.normal(ks[3], (CONTEXT_DIM, INNER_DIM), dtype=jnp.float32) * CONTEXT_DIM ** (-0.5)
        Wv = jax.random.normal(ks[4], (CONTEXT_DIM, INNER_DIM), dtype=jnp.float32) * CONTEXT_DIM ** (-0.5)
        Wo = jax.random.normal(ks[5], (INNER_DIM, QUERY_DIM), dtype=jnp.float32) * INNER_DIM ** (-0.5)
        bo = jnp.zeros((QUERY_DIM,), dtype=jnp.float32)
        return {'x': x, 'context': context, 'Wq': Wq, 'Wk': Wk, 'Wv': Wv, 'Wo': Wo, 'bo': bo}
    _L1_xattn_all = _L1_xattn_setup()
    _L1_xattn_in = {k: v for k, v in _L1_xattn_all.items() if k in ('Wq', 'Wk', 'Wv', 'Wo', 'bo')}
    del _L1_xattn_all

    def _L1_ffn_setup():
        import jax, jax.numpy as jnp
        import numpy as np
        B, S, H, D, E = (4, 128, 128, 512, 8)
        key = jax.random.key(seed)
        ks = jax.random.split(key, 12)

        def init(k, shape, fan_in):
            return jax.random.normal(k, shape, jnp.float32) / np.float32(np.sqrt(fan_in))
        return {'x': jax.random.normal(ks[0], (B, S, H), jnp.float32), 'Wq': init(ks[1], (H, H), H), 'bq': jnp.zeros((H,), jnp.float32), 'Wk': init(ks[2], (H, H), H), 'bk': jnp.zeros((H,), jnp.float32), 'Wv': init(ks[3], (H, H), H), 'bv': jnp.zeros((H,), jnp.float32), 'Wo': init(ks[4], (H, H), H), 'bo': jnp.zeros((H,), jnp.float32), 'Wg': init(ks[5], (H, E), H), 'bg': jnp.zeros((E,), jnp.float32), 'W1': init(ks[6], (E, H, D), H), 'b1': jnp.zeros((E, D), jnp.float32), 'W2': init(ks[7], (E, D, H), D), 'b2': jnp.zeros((E, H), jnp.float32)}
    _L1_ffn_all = _L1_ffn_setup()
    _L1_ffn_in = {k: v for k, v in _L1_ffn_all.items() if k in ('Wq', 'bq', 'Wk', 'bk', 'Wv', 'bv', 'Wo', 'bo', 'Wg', 'bg', 'W1', 'b1', 'W2', 'b2')}
    del _L1_ffn_all
    return {'x': x, 'ctx_768': ctx_768, 'L0_xattn_Wq': _L0_xattn_in['Wq'], 'L0_xattn_Wk': _L0_xattn_in['Wk'], 'L0_xattn_Wv': _L0_xattn_in['Wv'], 'L0_xattn_Wo': _L0_xattn_in['Wo'], 'L0_xattn_bo': _L0_xattn_in['bo'], 'L0_ffn_gate_w': _L0_ffn_in['gate_w'], 'L0_ffn_bias_e': _L0_ffn_in['bias_e'], 'L0_ffn_up_w': _L0_ffn_in['up_w'], 'L0_ffn_down_w': _L0_ffn_in['down_w'], 'L0_ffn_shared_up': _L0_ffn_in['shared_up'], 'L0_ffn_shared_down': _L0_ffn_in['shared_down'], 'L1_xattn_Wq': _L1_xattn_in['Wq'], 'L1_xattn_Wk': _L1_xattn_in['Wk'], 'L1_xattn_Wv': _L1_xattn_in['Wv'], 'L1_xattn_Wo': _L1_xattn_in['Wo'], 'L1_xattn_bo': _L1_xattn_in['bo'], 'L1_ffn_Wq': _L1_ffn_in['Wq'], 'L1_ffn_bq': _L1_ffn_in['bq'], 'L1_ffn_Wk': _L1_ffn_in['Wk'], 'L1_ffn_bk': _L1_ffn_in['bk'], 'L1_ffn_Wv': _L1_ffn_in['Wv'], 'L1_ffn_bv': _L1_ffn_in['bv'], 'L1_ffn_Wo': _L1_ffn_in['Wo'], 'L1_ffn_bo': _L1_ffn_in['bo'], 'L1_ffn_Wg': _L1_ffn_in['Wg'], 'L1_ffn_bg': _L1_ffn_in['bg'], 'L1_ffn_W1': _L1_ffn_in['W1'], 'L1_ffn_b1': _L1_ffn_in['b1'], 'L1_ffn_W2': _L1_ffn_in['W2'], 'L1_ffn_b2': _L1_ffn_in['b2']}

def reference(x, ctx_768, L0_xattn_Wq, L0_xattn_Wk, L0_xattn_Wv, L0_xattn_Wo, L0_xattn_bo, L0_ffn_gate_w, L0_ffn_bias_e, L0_ffn_up_w, L0_ffn_down_w, L0_ffn_shared_up, L0_ffn_shared_down, L1_xattn_Wq, L1_xattn_Wk, L1_xattn_Wv, L1_xattn_Wo, L1_xattn_bo, L1_ffn_Wq, L1_ffn_bq, L1_ffn_Wk, L1_ffn_bk, L1_ffn_Wv, L1_ffn_bv, L1_ffn_Wo, L1_ffn_bo, L1_ffn_Wg, L1_ffn_bg, L1_ffn_W1, L1_ffn_b1, L1_ffn_W2, L1_ffn_b2):
    import jax
    import jax.numpy as jnp

    def _L0_xattn_ref(x, context, Wq, Wk, Wv, Wo, bo):
        import jax, jax.numpy as jnp
        import numpy as np
        HEADS = 16
        DIM_HEAD = 64
        SCALE = DIM_HEAD ** (-0.5)
        b, sq, _ = x.shape

        def split_heads(t):
            return t.reshape(b, -1, HEADS, DIM_HEAD).transpose(0, 2, 1, 3)
        q = split_heads(x @ Wq)
        k = split_heads(context @ Wk)
        v = split_heads(context @ Wv)
        sim = jnp.einsum('bhid,bhjd->bhij', q, k) * SCALE
        attn = jax.nn.softmax(sim, axis=-1)
        out = jnp.einsum('bhij,bhjd->bhid', attn, v)
        out = out.transpose(0, 2, 1, 3).reshape(b, sq, HEADS * DIM_HEAD)
        return out @ Wo + bo

    def _L0_ffn_ref(hidden_states, gate_w, bias_e, up_w, down_w, shared_up, shared_down):
        import jax, jax.numpy as jnp
        import numpy as np
        DIM = 128
        N_EXPERTS = 16
        TOP_K = 4
        N_GROUP = 4
        TOPK_GROUP = 2
        MOE_INTER = 64
        SHARED_INTER = 256
        ROUTED_SCALE = 2.5

        def relu2(x):
            return jnp.square(jax.nn.relu(x))

        def _router(x2, gate_w, bias_e):
            T = x2.shape[0]
            logits = x2 @ gate_w.T
            scores = jax.nn.sigmoid(logits)
            sc = jax.lax.stop_gradient(scores + bias_e[None, :])
            grp = sc.reshape(T, N_GROUP, N_EXPERTS // N_GROUP)
            top2, _ = jax.lax.top_k(grp, 2)
            group_scores = top2.sum(-1)
            _, gidx = jax.lax.top_k(group_scores, TOPK_GROUP)
            rows = jnp.arange(T)[:, None]
            gmask = jnp.zeros((T, N_GROUP), dtype=sc.dtype).at[rows, gidx].set(1.0)
            smask = jnp.repeat(gmask, N_EXPERTS // N_GROUP, axis=1)
            masked = jnp.where(smask > 0, sc, 0.0)
            _, topk_idx = jax.lax.top_k(masked, TOP_K)
            topk_w = jnp.take_along_axis(scores, topk_idx, axis=1)
            topk_w = topk_w / (topk_w.sum(-1, keepdims=True) + 1e-20)
            topk_w = topk_w * ROUTED_SCALE
            return (topk_idx, topk_w)
        B, S, D = hidden_states.shape
        x2 = hidden_states.reshape(-1, D)
        T = x2.shape[0]
        topk_idx, topk_w = _router(x2, gate_w, bias_e)
        rows = jnp.arange(T)[:, None]
        combine = jnp.zeros((T, N_EXPERTS), dtype=topk_w.dtype).at[rows, topk_idx].add(topk_w)

        def body(acc, inp):
            wu, wd, cw = inp
            y = relu2(x2 @ wu.T) @ wd.T
            return (acc + cw[:, None] * y, None)
        routed, _ = jax.lax.scan(body, jnp.zeros_like(x2), (up_w, down_w, combine.T))
        shared = relu2(x2 @ shared_up.T) @ shared_down.T
        out = routed + shared
        return out.reshape(B, S, D)

    def _L1_xattn_ref(x, context, Wq, Wk, Wv, Wo, bo):
        import jax, jax.numpy as jnp
        import numpy as np
        HEADS = 16
        DIM_HEAD = 64
        SCALE = DIM_HEAD ** (-0.5)
        QUERY_DIM = 128
        CONTEXT_DIM = 96
        INNER_DIM = HEADS * DIM_HEAD
        B, Nq, _ = x.shape
        Nk = context.shape[1]
        q = x @ Wq
        k = context @ Wk
        v = context @ Wv
        q = q.reshape(B, Nq, HEADS, DIM_HEAD).transpose(0, 2, 1, 3)
        k = k.reshape(B, Nk, HEADS, DIM_HEAD).transpose(0, 2, 1, 3)
        v = v.reshape(B, Nk, HEADS, DIM_HEAD).transpose(0, 2, 1, 3)
        sim = jnp.einsum('bhid,bhjd->bhij', q, k) * SCALE
        attn = jax.nn.softmax(sim, axis=-1)
        out = jnp.einsum('bhij,bhjd->bhid', attn, v)
        out = out.transpose(0, 2, 1, 3).reshape(B, Nq, INNER_DIM)
        return out @ Wo + bo

    def _L1_ffn_ref(x, Wq, bq, Wk, bk, Wv, bv, Wo, bo, Wg, bg, W1, b1, W2, b2):
        import jax, jax.numpy as jnp
        import numpy as np
        B, S, H, D, E = (4, 128, 128, 512, 8)
        q = x @ Wq + bq
        k = x @ Wk + bk
        v = x @ Wv + bv
        scale = jnp.asarray(1.0 / np.sqrt(H), x.dtype)
        scores = jnp.einsum('bqh,bkh->bqk', q, k) * scale
        attn = jax.nn.softmax(scores, axis=-1)
        a = jnp.einsum('bqk,bkh->bqh', attn, v) @ Wo + bo
        x = x + a
        gates = jax.nn.softmax(x @ Wg + bg, axis=-1)
        hmid = jax.nn.relu(jnp.einsum('bsh,ehd->bsed', x, W1) + b1)
        eout = jnp.einsum('bsed,edh->bseh', hmid, W2) + b2
        y = jnp.einsum('bse,bseh->bsh', gates, eout)
        return x + y
    x = x + _L0_xattn_ref(_layernorm(x, axis=-1), ctx_768, L0_xattn_Wq, L0_xattn_Wk, L0_xattn_Wv, L0_xattn_Wo, L0_xattn_bo)
    x = x + _L0_ffn_ref(_layernorm(x, axis=-1), L0_ffn_gate_w, L0_ffn_bias_e, L0_ffn_up_w, L0_ffn_down_w, L0_ffn_shared_up, L0_ffn_shared_down)
    x = x + _L1_xattn_ref(_layernorm(x, axis=-1), ctx_768, L1_xattn_Wq, L1_xattn_Wk, L1_xattn_Wv, L1_xattn_Wo, L1_xattn_bo)
    x = x + _L1_ffn_ref(_layernorm(x, axis=-1), L1_ffn_Wq, L1_ffn_bq, L1_ffn_Wk, L1_ffn_bk, L1_ffn_Wv, L1_ffn_bv, L1_ffn_Wo, L1_ffn_bo, L1_ffn_Wg, L1_ffn_bg, L1_ffn_W1, L1_ffn_b1, L1_ffn_W2, L1_ffn_b2)
    return x

_drawn_inputs = setup_inputs


def setup_inputs(seed=0):
    import zlib

    import numpy as np

    out = dict(_drawn_inputs(seed))
    spreads = {'L0_xattn_bo': (0.0, 0.1),
     'L0_ffn_bias_e': (0.0, 0.8),
     'L1_xattn_bo': (0.0, 0.45),
     'L1_ffn_bq': (0.0, 2.0),
     'L1_ffn_bk': (0.0, 2.0),
     'L1_ffn_bv': (0.0, 0.477),
     'L1_ffn_bo': (0.0, 0.476),
     'L1_ffn_bg': (0.0, 0.625),
     'L1_ffn_b1': (0.0, 0.562),
     'L1_ffn_b2': (0.0, 0.393)}
    factors = {'L0_ffn_gate_w': 8.0,
     'L0_ffn_up_w': 7.476,
     'L0_ffn_down_w': 6.865,
     'L0_ffn_shared_up': 4.602,
     'L0_ffn_shared_down': 4.059}
    for name, (base, spread) in spreads.items():
        noise = np.random.default_rng([zlib.crc32(name.encode()), seed]).standard_normal(out[name].shape)
        drawn = base * np.exp(spread * noise) if base else spread * noise
        out[name] = jnp.asarray(drawn.astype(out[name].dtype))
    for name, factor in factors.items():
        out[name] = (out[name] * factor).astype(out[name].dtype)
    return out
```

```python
from contextlib import ExitStack

import concourse.bass as bass
from concourse import mybir

F32 = mybir.dt.float32
F32R = mybir.dt.float32r
ALU = mybir.AluOpType
ACT = mybir.ActivationFunctionType
AX_X = mybir.AxisListType.X

P = 128
BANK = 512
NB = 32
G = 4
NG = NB // G
NK = 77
CD = 96
H = 16
DH = 64
INNER = H * DH
NC = INNER // P
HS = [(0, 6), (6, 12), (12, 16)]
EPS = 1e-5


def need(eng, sem, value):
    if isinstance(value, int) and value <= 0:
        return
    eng.wait_ge(sem, value)


def split3(pe, out, pairs, first=True, last=True, **kw):
    n = 0
    for a_hi, a_lo, b_hi, b_lo in pairs:
        for a, b in ((a_hi, b_hi), (a_hi, b_lo), (a_lo, b_hi)):
            n += 1
            ins = pe.matmul(out, a, b, start=first and n == 1, stop=last and n == 3 * len(pairs), **kw)
    return ins


def cap(value, most):
    return min(value, most) if isinstance(value, int) else value


class Step:

    def __init__(self, g, i):
        self.g, self.i, self.n = g, i, g * G + i

    def has(self, off):
        return not isinstance(self.n, int) or 0 <= self.n + off < NB


def run_steps(eng, step):
    for n in range(-3, G):
        step(Step(n // G, n % G))
    with eng.Fori(1, NG - 1) as g:
        for i in range(G):
            step(Step(g, i))
    for n in range(NB - G, NB + 1):
        step(Step(n // G, n % G))


class Chip:

    def __init__(self, nc, ctx):
        self.nc, self.ctx = nc, ctx
        self.x = self.sb("x_res", [P, NB * P])
        self.ident = self.sb("identity", [P, P])
        self.fused_hi = self.sb("fused_hi", [CD, H * P], F32R)
        self.fused_lo = self.sb("fused_lo", [CD, H * P], F32R)
        self.wv_hi = self.sb("wv_hi", [CD, INNER], F32R)
        self.wv_lo = self.sb("wv_lo", [CD, INNER], F32R)
        self.wo = self.sb("wo", [P, NC * P])
        self.bo = self.sb("bo", [P, P])
        self.w_hi = self.sb("w_hi", [P, 4096], F32R)
        self.w_lo = self.sb("w_lo", [P, 4096], F32R)
        self.ps = ctx.enter_context(nc.psum_tensor("banks", [P, 8 * BANK], F32))

    def sb(self, name, shape, dt=F32):
        return self.ctx.enter_context(self.nc.sbuf_tensor(name, shape, dt))

    def sem(self, name):
        return self.ctx.enter_context(self.nc.semaphore(name))

    def xt(self, n, k=1):
        return self.x[:, bass.ds(n * P, k * P)]

    def bank(self, b, rows, width, at=0):
        return self.ps[0:rows, b * BANK + at:b * BANK + at + width]


def prepare_xattn(nc, chip, L, a, sems, loads=()):
    pre = f"p{L}_"
    names = "w_loaded o_loaded wT_psum wT_act wT_dve f_psum f_hi f_lo v_hi v_lo".split()
    if not sems:
        sems.update({n: chip.sem("p_" + n) for n in names})
    w_loaded, o_loaded, wT_psum, wT_act, wT_dve, f_psum, f_hi, f_lo, v_hi, v_lo = (sems[n] for n in names)
    base = {n: k * L for n, k in (("w_loaded", 64), ("o_loaded", 48), ("wT_psum", 4), ("wT", 2), ("f", 4), ("v", 1))}
    with ExitStack() as own:
        def sb(name, shape, dt=F32):
            return own.enter_context(nc.sbuf_tensor(pre + name, shape, dt))

        wq = sb("wq", [P, INNER])
        wk = sb("wk", [CD, INNER])
        wv = sb("wv", [CD, INNER])
        wqT = sb("wqT", [P, NC * P])
        wkT = sb("wkT", [P, NC * CD])
        block = own.enter_context(nc.Block())

        def heads(t, q):
            return t[:].rearrange("c (m r d) -> c r m d", r=2, d=P)[:, q // 2, 4 * (q % 2):4 * (q % 2) + 4]

        @block.sync
        def _(sp):
            if L == 0:
                sp.dma_start(chip.ident[:], a["ident"]).then_inc(w_loaded, 16)
            sp.dma_start(wq[:], a["Wq"]).then_inc(w_loaded, 16)
            sp.dma_start(wk[:], a["Wk"]).then_inc(w_loaded, 16)
            sp.dma_start(wv[:], a["Wv"]).then_inc(w_loaded, 16)
            sp.dma_start(chip.wo[:].rearrange("p (c d) -> p c d", c=NC),
                         a["Wo"].rearrange("(c p) d -> p c d", p=P)).then_inc(o_loaded, 16)
            sp.dma_start(chip.bo[:], a["bo"].rearrange("(o d) -> o d", o=1).broadcast_to([P, P])).then_inc(o_loaded, 16)
            for dst, src in loads:
                sp.dma_start(dst, src).then_inc(o_loaded, 16)
            sp.wait_ge(o_loaded, base["o_loaded"] + 16 * (2 + len(loads)))

        @block.tensor
        def _(pe):
            pe.wait_ge(w_loaded, base["w_loaded"] + 16 * (4 if L == 0 else 3))
            for w, rows, at in ((wq, P, 0), (wk, CD, 2)):
                for c in range(NC):
                    t = nc.tensor.transpose(chip.bank(at + c // 4, P, rows, (c % 4) * rows),
                                            w[:, c * P:(c + 1) * P], chip.ident[0:rows, 0:rows])
                    if c % 4 == 3:
                        t.then_inc(wT_psum, 1)
            pe.wait_ge(wT_act, base["wT"] + 2)
            pe.wait_ge(wT_dve, base["wT"] + 2)
            for odd in range(2):
                for m in range(NC):
                    r = slice(DH * odd, DH * (odd + 1))
                    f = nc.tensor.matmul(chip.bank(4 + 2 * odd + m // 4, CD, P, (m % 4) * P),
                                         wkT[r, m * CD:(m + 1) * CD], wqT[r, m * P:(m + 1) * P], start=True, stop=True)
                    if m % 4 == 3:
                        f.then_inc(f_psum, 1)

        @block.scalar
        def _(act):
            for q in range(2):
                act.wait_ge(wT_psum, base["wT_psum"] + q + 1)
                nc.scalar.copy(wqT[:, q * BANK:(q + 1) * BANK], chip.bank(q, P, BANK)).then_inc(wT_act, 1)
            nc.scalar.copy(chip.wv_hi[:], wv[:]).then_inc(v_hi, 1)
            for q in range(4):
                act.wait_ge(f_psum, base["f"] + q + 1)
                nc.scalar.copy(heads(chip.fused_hi, q), chip.bank(4 + q, CD, BANK).rearrange("c (m d) -> c m d", m=4)).then_inc(f_hi, 1)

        @block.vector
        def _(dve):
            for q in range(2):
                dve.wait_ge(wT_psum, base["wT_psum"] + q + 3)
                nc.vector.tensor_copy(wkT[:, q * 4 * CD:(q + 1) * 4 * CD], chip.bank(2 + q, P, 4 * CD)).then_inc(wT_dve, 1)
            dve.wait_ge(v_hi, base["v"] + 1)
            nc.vector.tensor_tensor(chip.wv_lo[:], wv[:], chip.wv_hi[:].bitcast(F32), ALU.subtract).then_inc(v_lo, 1)
            for q in range(4):
                dve.wait_ge(f_hi, base["f"] + q + 1)
                nc.vector.tensor_tensor(heads(chip.fused_lo, q), chip.bank(4 + q, CD, BANK).rearrange("c (m d) -> c m d", m=4),
                                        heads(chip.fused_hi, q).bitcast(F32), ALU.subtract).then_inc(f_lo, 1)


def xattn_stage(nc, chip, L, context, sems):
    pre = f"x{L}_"
    names = ("ctx_loaded bn_done stats_done eps_done rstd_done xn_done xnT_psum xnT_hi xnT_lo bo_added "
             "ctxT_psum ctxT_hi ctxT_lo kp_psum kp_hi kp_lo sim_done max_done sub_done exp_done sum_done recip_done "
             "norm_done v_psum v_sb t_psum t_sb pv_psum oT_sb wo_psum x_upd half").split()
    if not sems:
        sems.update({n: chip.sem("x_" + n) for n in names})
    (ctx_loaded, bn_done, stats_done, eps_done, rstd_done, xn_done, xnT_psum, xnT_hi, xnT_lo, bo_added,
     ctxT_psum, ctxT_hi, ctxT_lo, kp_psum, kp_hi, kp_lo, sim_done, max_done, sub_done, exp_done, sum_done, recip_done,
     norm_done, v_psum, v_sb, t_psum, t_sb, pv_psum, oT_sb, wo_psum, x_upd, half_set) = (sems[n] for n in names)
    KW = G * NK
    with ExitStack() as own:
        def sb(name, shape, dt=F32):
            return own.enter_context(nc.sbuf_tensor(pre + name, shape, dt))

        ctx_raw = sb("ctx_raw", [NK, G, CD])
        ctxT_h = sb("ctxT_h", [CD, KW], F32R)
        ctxT_l = sb("ctxT_l", [CD, KW], F32R)
        kp_h = sb("kp_h", [P, G, H * NK], F32R)
        kp_l = sb("kp_l", [P, G, H * NK], F32R)
        bn = sb("bn", [P, 2, 6])
        mv = sb("mv", [P, 4, 2])
        rstd = sb("rstd", [P, 4])
        var_eps = sb("var_eps", [P, 4])
        minus_half = sb("minus_half", [P, 1])
        eps = sb("eps", [P, 1])
        xn = sb("xn", [P, 2, P])
        xnT_h = sb("xnT_h", [P, 2, P], F32R)
        xnT_l = sb("xnT_l", [P, 2, P], F32R)
        prob = sb("prob", [P, 2, H, NK])
        mx = sb("mx", [P, 2, H])
        rs = sb("rs", [P, 2, H])
        ri = sb("ri", [P, 2, H])
        v = sb("v", [NK, 2, INNER])
        pT = sb("pT", [NK, H, P])
        oT = sb("oT", [P, NC, P])
        SIM, MISC = 0, 7
        V_BANK, T_BANK, PV_BANK = (3, 4), (5, 6, 3, 4), (5, 6)
        KP_BANK = (3, 5, 0)
        CTX_AT, WO_AT = P, BANK - P

        def sim_ps(part):
            if part == 0:
                return chip.ps[:, 0:2 * BANK].rearrange("p (b c) -> p b c", b=2)[:, :, 0:6 * NK].rearrange(
                    "p b (h k) -> p b h k", h=6)
            return chip.bank(2, P, 4 * NK).rearrange("p (h k) -> p h k", h=4)

        def pair_ps(p):
            at = KP_BANK[p % 3] * BANK
            return chip.ps[:, at:at + 2 * BANK].rearrange("p (h c) -> p h c", h=2)[:, :, 0:KW].rearrange(
                "p h (b k) -> p h b k", b=G)

        def pair_sb(t, p):
            return t[:, :, 2 * p * NK:2 * (p + 1) * NK].rearrange("p b (h k) -> p h b k", h=2)

        def part_of(t, par, part):
            if part == 0:
                return t[:, par, 0:12].rearrange("p (b h) k -> p b h k", b=2) if len(t.shape) == 4 else \
                    t[:, par, 0:12].rearrange("p (b h) -> p b h", b=2)
            return t[:, par, 12:16]

        block = own.enter_context(nc.Block())

        @block.sync
        def _(sp):
            sp.dma_start(ctx_raw[:], context[0:G].rearrange("b k d -> k b d")).then_inc(ctx_loaded, 16)
            with sp.Fori(1, NG) as g:
                sp.wait_ge(ctxT_psum, g + NG * L)
                sp.dma_start(ctx_raw[:], context[bass.ds(g * G, G)].rearrange("b k d -> k b d")).then_inc(ctx_loaded, 16)

        @block.gpsimd
        def _(pool):
            nc.gpsimd.memset(minus_half[:], -0.5).then_inc(half_set, 1)
            nc.gpsimd.memset(eps[:], EPS).then_inc(half_set, 1)
            pool.wait_ge(half_set, 2 * L + 2)

            def step(s):
                n, i = s.n, s.i
                m = n + NB * L
                if s.has(2):
                    need(pool, xn_done, m + 3)
                    xb = chip.xt(n + 2)
                    nc.gpsimd.tensor_tensor(xb, xb, chip.bo[:], ALU.add).then_inc(bo_added, 1)
                if s.has(3):
                    b = (i + 3) % 4
                    need(pool, stats_done, m + 4)
                    need(pool, xn_done, m)
                    nc.gpsimd.tensor_tensor(var_eps[:, b:b + 1], mv[:, b, 1:2], eps[:], ALU.add).then_inc(eps_done, 1)
                    need(pool, eps_done, m + 4)
                    nc.gpsimd.tensor_tensor(rstd[:, b:b + 1], var_eps[:, b:b + 1], minus_half[:], ALU.pow).then_inc(rstd_done, 1)
                if s.has(1):
                    b = (i + 1) % 2
                    need(pool, recip_done, m + 2)
                    for q in range(4):
                        hq = slice(4 * q, 4 * q + 4)
                        nc.gpsimd.tensor_tensor(prob[:, b, hq], prob[:, b, hq],
                                                ri[:, b, hq].unsqueeze(2).broadcast_to([P, 4, NK]),
                                                ALU.mult).then_inc(norm_done, 1)
            run_steps(pool, step)

        @block.tensor
        def _(pe):
            def step(s):
                n, g, i = s.n, s.g, s.i
                m, gm = n + NB * L, g + NG * L
                b1 = (i + 1) % 2

                def weights(j):
                    if j < 2:
                        need(pe, oT_sb, 2 * m - 1 + j)
                    else:
                        need(pe, v_sb, cap(2 * m + 1 + j, 2 * NB * (L + 1)))
                    need(pe, norm_done, 4 * m + j + 1)
                    for h in range(4 * j, 4 * j + 4):
                        last = nc.tensor.transpose(chip.bank(T_BANK[j], NK, P, (h % 4) * P), prob[:, i % 2, h], chip.ident[:])
                    last.then_inc(t_psum, 1)

                def outputs(j):
                    need(pe, v_sb, 2 * m + 2)
                    need(pe, t_sb, 4 * m + 2 * j + 2)
                    for r in range(4):
                        for half in range(2):
                            h = 8 * j + 2 * r + half
                            at = PV_BANK[j] * BANK + r * P
                            last = nc.tensor.matmul(chip.ps[DH * half:DH * (half + 1), at:at + P],
                                                    v[:, i % 2, h * DH:(h + 1) * DH], pT[:, h], start=True, stop=True)
                    last.then_inc(pv_psum, 1)

                if i == 3 and s.has(1):
                    need(pe, ctxT_hi, gm + 2)
                    need(pe, ctxT_lo, gm + 2)
                    for p in range(H // 2):
                        if p >= 3:
                            need(pe, kp_lo, 8 * gm + 8 + p - 2)
                        elif p == 1:
                            need(pe, oT_sb, 2 * m)
                        elif p == 2:
                            need(pe, sub_done, 2 * m + 2)
                        for h in (2 * p, 2 * p + 1):
                            hs = slice(h * P, (h + 1) * P)
                            last = split3(nc.tensor, chip.bank(KP_BANK[p % 3] + h % 2, P, KW),
                                          [(chip.fused_hi[:, hs], chip.fused_lo[:, hs], ctxT_h[:], ctxT_l[:])])
                        last.then_inc(kp_psum, 1)
                if s.has(1):
                    need(pe, xnT_hi, m + 2)
                    need(pe, xnT_lo, m + 2)
                    need(pe, sub_done, 2 * m + 2)
                    if i == 3:
                        need(pe, kp_lo, 8 * gm + 16)
                    for q, (h0, h1) in enumerate(HS):
                        c = slice(h0 * NK, h1 * NK)
                        last = split3(nc.tensor, chip.bank(SIM + q, P, (h1 - h0) * NK),
                                      [(xnT_h[:, b1], xnT_l[:, b1], kp_h[:, (i + 1) % G, c], kp_l[:, (i + 1) % G, c])])
                    last.then_inc(sim_done, 1)
                if s.has(-1):
                    need(pe, oT_sb, 2 * m)
                    need(pe, xnT_lo, cap(m + 2, NB * (L + 1)))
                    if i == 3 and s.has(1):
                        need(pe, ctxT_lo, gm + 2)
                    for c in range(NC):
                        last = nc.tensor.matmul(chip.bank(MISC, P, P, WO_AT), oT[:, c], chip.wo[:, c * P:(c + 1) * P],
                                                start=c == 0, stop=c == NC - 1)
                    last.then_inc(wo_psum, 1)
                if s.has(1):
                    cs = slice(((i + 1) % G) * NK, ((i + 1) % G + 1) * NK)
                    need(pe, t_sb, 4 * m)
                    for q in range(2):
                        c = slice(q * BANK, (q + 1) * BANK)
                        split3(nc.tensor, chip.bank(V_BANK[q], NK, BANK),
                               [(ctxT_h[:, cs], ctxT_l[:, cs], chip.wv_hi[:, c], chip.wv_lo[:, c])]).then_inc(v_psum, 1)
                if s.has(0):
                    for j in range(4):
                        weights(j)
                if s.has(2):
                    need(pe, xn_done, m + 3)
                    need(pe, x_upd, m)
                    nc.tensor.transpose(chip.bank(MISC, P, P), xn[:, i % 2], chip.ident[:]).then_inc(xnT_psum, 1)
                if s.has(0):
                    outputs(0)
                if i == 2 and s.has(2):
                    need(pe, ctx_loaded, 16 * gm + 32)
                    need(pe, xnT_lo, m + 3)
                    for b in range(G):
                        last = nc.tensor.transpose(chip.bank(MISC, CD, NK, CTX_AT + b * NK), ctx_raw[:, b],
                                                   chip.ident[0:NK, 0:NK])
                    last.then_inc(ctxT_psum, 1)
                if s.has(0):
                    outputs(1)
            run_steps(pe, step)

        @block.scalar
        def _(act):
            def step(s):
                n, g, i = s.n, s.g, s.i
                m, gm = n + NB * L, g + NG * L
                b1 = (i + 1) % 2

                def exps(part):
                    need(act, sub_done, 2 * m + 3 + part)
                    hp = slice(0, 12) if part == 0 else slice(12, 16)
                    nc.scalar.activation(prob[:, b1, hp], prob[:, b1, hp], ACT.Exp, scale=DH ** -0.5).then_inc(exp_done, 1)

                def weights(j):
                    need(act, t_psum, 4 * m + j + 1)
                    nc.scalar.copy(pT[:, 4 * j:4 * j + 4], chip.bank(T_BANK[j], NK, BANK)).then_inc(t_sb, 1)

                if i == 3 and s.has(1):
                    for p in range(H // 2):
                        need(act, kp_psum, 8 * gm + 9 + p)
                        nc.scalar.copy(pair_sb(kp_h, p), pair_ps(p)).then_inc(kp_hi, 1)
                if s.has(1):
                    for q in range(2):
                        need(act, v_psum, 2 * m + 3 + q)
                        nc.scalar.copy(v[:, b1, q * BANK:(q + 1) * BANK], chip.bank(V_BANK[q], NK, BANK)).then_inc(v_sb, 1)
                if s.has(0):
                    weights(0)
                    weights(1)
                if s.has(1):
                    exps(0)
                if s.has(0):
                    weights(2)
                    weights(3)
                if s.has(2):
                    need(act, xnT_psum, m + 3)
                    nc.scalar.copy(xnT_h[:, i % 2], chip.bank(MISC, P, P)).then_inc(xnT_hi, 1)
                if s.has(1):
                    exps(1)
                if i == 2 and s.has(2):
                    need(act, ctxT_psum, gm + 2)
                    nc.scalar.copy(ctxT_h[:], chip.bank(MISC, CD, KW, CTX_AT)).then_inc(ctxT_hi, 1)
            run_steps(act, step)

        @block.vector
        def _(dve):
            def step(s):
                n, g, i = s.n, s.g, s.i
                m, gm = n + NB * L, g + NG * L
                b1 = (i + 1) % 2

                def sums(off):
                    b = (i + off) % 2
                    need(dve, exp_done, 2 * (m + off) + 2)
                    nc.vector.tensor_reduce(rs[:, b], prob[:, b], AX_X, ALU.add).then_inc(sum_done, 1)
                    need(dve, sum_done, m + off + 1)
                    nc.vector.reciprocal(ri[:, b], rs[:, b]).then_inc(recip_done, 1)

                def outputs(j):
                    need(dve, pv_psum, 2 * m + j + 1)
                    nc.vector.tensor_copy(oT[:, 4 * j:4 * j + 4], chip.bank(PV_BANK[j], P, BANK)).then_inc(oT_sb, 1)

                if i == 3 and s.has(1):
                    for p in range(H // 2):
                        need(dve, kp_hi, 8 * gm + 9 + p)
                        nc.vector.tensor_tensor(pair_sb(kp_l, p), pair_ps(p), pair_sb(kp_h, p).bitcast(F32),
                                                ALU.subtract).then_inc(kp_lo, 1)
                    if s.has(0):
                        sums(0)
                if s.has(2):
                    b = (i + 2) % 4
                    need(dve, rstd_done, m + 3)
                    need(dve, xnT_psum, m + 1)
                    nc.vector.tensor_scalar(xn[:, i % 2], chip.xt(n + 2), mv[:, b, 0:1], rstd[:, b:b + 1],
                                            ALU.subtract, ALU.mult).then_inc(xn_done, 1)
                if s.has(1):
                    need(dve, sim_done, m + 2)
                    need(dve, t_psum, 4 * m)
                    for part in range(2):
                        nc.vector.tensor_reduce(part_of(mx, b1, part), sim_ps(part), AX_X, ALU.max).then_inc(max_done, 1)
                    for part in range(2):
                        sp_ = sim_ps(part)
                        need(dve, max_done, 2 * m + 3 + part)
                        nc.vector.tensor_tensor(part_of(prob, b1, part), sp_,
                                                part_of(mx, b1, part).unsqueeze(len(sp_.shape) - 1).broadcast_to(list(sp_.shape)),
                                                ALU.subtract).then_inc(sub_done, 1)
                if s.has(3):
                    nc.vector.bn_stats(bn[:, b1], chip.xt(n + 3)).then_inc(bn_done, 1)
                    need(dve, bn_done, m + 4)
                if s.has(-1):
                    need(dve, wo_psum, m)
                    need(dve, bo_added, m)
                    xb = chip.xt(n - 1)
                    nc.vector.tensor_tensor(xb, xb, chip.bank(MISC, P, P, WO_AT), ALU.add).then_inc(x_upd, 1)
                if s.has(3):
                    nc.vector.bn_aggr(mv[:, (i + 3) % 4], bn[:, b1]).then_inc(stats_done, 1)
                if s.has(2):
                    need(dve, xnT_hi, m + 3)
                    nc.vector.tensor_tensor(xnT_l[:, i % 2], chip.bank(MISC, P, P), xnT_h[:, i % 2].bitcast(F32),
                                            ALU.subtract).then_inc(xnT_lo, 1)
                if s.has(0):
                    outputs(0)
                if i == 2 and s.has(2):
                    need(dve, ctxT_hi, gm + 2)
                    nc.vector.tensor_tensor(ctxT_l[:], chip.bank(MISC, CD, KW, CTX_AT), ctxT_h[:].bitcast(F32),
                                            ALU.subtract).then_inc(ctxT_lo, 1)
                if s.has(0):
                    outputs(1)
                if s.has(1) and not (i == 2 and s.has(2)):
                    sums(1)
            run_steps(dve, step)



NE = 16
FI = 64
TOP = 4
NGRP = 4
CR = NE * FI // P
CS = 2
CF = CR + CS
ROUTED_SCALE = 2.5
GP = G * P


class GroupStep:

    def __init__(self, g):
        self.g = g

    def has(self, off):
        return not isinstance(self.g, int) or 0 <= self.g + off < NG


def run_groups(eng, step):
    step(GroupStep(-1))
    step(GroupStep(0))
    with eng.Fori(1, NG - 1) as g:
        step(GroupStep(g))
    step(GroupStep(NG - 1))
    step(GroupStep(NG))


class Chain:

    def __init__(self, eng, sem, per_group):
        self.eng, self.sem, self.per = eng, sem, per_group

    def begin(self, g):
        self.base, self.n = self.per * g, 0

    def link(self, ins):
        self.n += 1
        ins.then_inc(self.sem, 1)
        self.eng.wait_ge(self.sem, self.base + self.n)

    def end(self):
        assert self.n == self.per, self.n


def prepare_moe0(nc, chip, a, keep):
    up_loaded, dn_loaded, wt_psum, wt_hi, wt_lo, small, gate_sb = (
        chip.sem("m0_" + n) for n in "up_loaded dn_loaded wt_psum wt_hi wt_lo small gate_sb".split())
    with ExitStack() as own:
        def sb(name, shape, dt=F32):
            return own.enter_context(nc.sbuf_tensor("m0_" + name, shape, dt))

        up = sb("up", [P, CF, P])
        dn = sb("dn", [P, CF, P])
        gw = sb("gw", [NE, P])
        sel = sb("sel", [NE, CR * P])
        block = own.enter_context(nc.Block())
        NQ = 2 * CF // 4

        @block.sync
        def _(sp):
            sp.dma_start(up[:, 0:CR], a["up_w"].rearrange("(c e) f d -> (e f) c d", e=2)).then_inc(up_loaded, 16)
            sp.dma_start(up[:, CR:CF], a["shared_up"].rearrange("(c f) d -> f c d", f=P)).then_inc(up_loaded, 16)
            sp.dma_start(gw[:], a["gate_w"]).then_inc(up_loaded, 16)
            sp.dma_start(dn[:, 0:CR].rearrange("d c (e f) -> d (c e) f", e=2),
                         a["down_w"].rearrange("e d f -> d e f")).then_inc(dn_loaded, 16)
            sp.dma_start(dn[:, CR:CF].rearrange("d c f -> d (c f)"), a["shared_down"]).then_inc(dn_loaded, 16)
            sp.dma_start(sel[:], a["pairs"]).then_inc(small, 16)
            sp.dma_start(keep["bias"][:], a["bias_e"].rearrange("(o d) -> o d", o=1).broadcast_to([P, NE])).then_inc(small, 16)
            sp.dma_start(keep["before"][:], a["before"].rearrange("(o d) -> o d", o=1).broadcast_to([P, 2 * NGRP * NGRP])).then_inc(small, 16)
            sp.wait_ge(small, 48)

        @block.tensor
        def _(pe):
            pe.wait_ge(up_loaded, 48)
            for c in range(2 * CF):
                if c == CF:
                    pe.wait_ge(dn_loaded, 32)
                src = up[:, c] if c < CF else dn[:, c - CF]
                t = nc.tensor.transpose(chip.bank(c // 4, P, P, (c % 4) * P), src, chip.ident[:])
                if c % 4 == 3:
                    t.then_inc(wt_psum, 1)
            nc.tensor.transpose(chip.bank(7, P, NE), gw[:], chip.ident[0:NE, 0:NE]).then_inc(wt_psum, 1)

        @block.scalar
        def _(act):
            for q in range(NQ):
                act.wait_ge(wt_psum, q + 1)
                nc.scalar.copy(chip.w_hi[:, q * BANK:(q + 1) * BANK], chip.bank(q, P, BANK)).then_inc(wt_hi, 1)
            act.wait_ge(wt_psum, NQ + 1)
            nc.scalar.copy(keep["gate"][:], chip.bank(7, P, NE)).then_inc(gate_sb, 1)

        @block.vector
        def _(dve):
            for q in range(NQ):
                dve.wait_ge(wt_hi, q + 1)
                c = slice(q * BANK, (q + 1) * BANK)
                nc.vector.tensor_tensor(chip.w_lo[:, c], chip.bank(q, P, BANK), chip.w_hi[:, c].bitcast(F32),
                                        ALU.subtract).then_inc(wt_lo, 1)
            dve.wait_ge(small, 48)
            nc.vector.tensor_copy(keep["pairs"][:], sel[:]).then_inc(wt_lo, 1)


def moe0_stage(nc, chip, a):
    names = ("bn_done stats_done eps_done rstd_done xn_done xnT_psum xT_sb xT_hi xT_lo logit_psum act_sc router cw_done "
             "cwT_psum cwT_hi cwT_lo up_psum bc_psum relu_done q_done h_done h_hi h_lo down_done yT_sb yo_psum "
             "x_upd half scan_zero").split()
    (bn_done, stats_done, eps_done, rstd_done, xn_done, xnT_psum, xT_sb, xT_hi, xT_lo, logit_psum, act_sc, router, cw_done,
     cwT_psum, cwT_hi, cwT_lo, up_psum, bc_psum, relu_done, q_done, h_done, h_hi, h_lo, down_done, yT_sb, yo_psum,
     x_upd, half_set, scan_zero) = (chip.sem("f0_" + n) for n in names)
    RING, LAG = 5, 2
    U, B, Y, XT, YT, LG = 0, 2, 4, 5, 6, 7
    with ExitStack() as own:
        def sb(name, shape, dt=F32):
            return own.enter_context(nc.sbuf_tensor("f0_" + name, shape, dt))

        keep = {"gate": sb("gate", [P, NE]), "bias": sb("bias", [P, NE]), "pairs": sb("pairs", [NE, CR * P], F32R),
                "before": sb("before", [P, 2 * NGRP * NGRP])}
        prepare_moe0(nc, chip, a, keep)
        bn = sb("bn", [P, G, 6])
        mv = sb("mv", [P, G, 2])
        rstd = sb("rstd", [P, G])
        var_eps = sb("var_eps", [P, G])
        minus_half = sb("minus_half", [P, G])
        eps = sb("eps", [P, G])
        xn = sb("xn", [P, G, P])
        xT = sb("xT", [P, GP])
        xh = sb("xh", [P, 2 * GP], F32R)
        xl = sb("xl", [P, 2 * GP], F32R)
        th = sb("th", [P, G, NE])
        ex = sb("ex", [P, G, NE])
        cwT_h = sb("cwT_h", [NE, 2 * GP], F32R)
        cwT_l = sb("cwT_l", [NE, 2 * GP], F32R)
        r = sb("r", [P, RING, GP])
        q = sb("q", [P, RING, GP])
        h = sb("h", [P, RING, GP])
        hh = sb("hh", [P, RING, GP], F32R)
        hl = sb("hl", [P, RING, GP], F32R)
        yT = sb("yT", [P, GP])
        sc = sb("sc", [P, G, NE])
        sig = sb("sig", [P, G, NE])
        pair_max = sb("pair_max", [P, G * NGRP, 2])
        pair_min = sb("pair_min", [P, G * NGRP, 2])
        best = sb("best", [P, G * NGRP])
        second = sb("second", [P, G * NGRP])
        other = sb("other", [P, G * NGRP])
        gs = sb("gs", [P, G, NGRP])
        ge = sb("ge", [P, G, NGRP, NGRP])
        gt4 = sb("gt4", [P, G, NGRP, NGRP])
        rank = sb("rank", [P, G, NGRP])
        masked = sb("masked", [P, G, NE])
        top8 = sb("top8", [P, G, 8])
        over = sb("over", [P, G, NE])
        n_over = sb("n_over", [P, G])
        PAD = 8
        scan = sb("scan", [P, 2, G, PAD + NE])
        same = sb("same", [P, G, NE])
        w_sum = sb("w_sum", [P, G])
        w_inv = sb("w_inv", [P, G])
        cw = sb("cw", [P, G, NE])
        gate, bias, pairs, before = keep["gate"], keep["bias"], keep["pairs"], keep["before"]
        block = own.enter_context(nc.Block())

        def chunk(s, c, late):
            return (s.has(0) if c >= late else s.has(-1)), (c - late) % CF, CF * s.g + c - late + 1

        @block.gpsimd
        def _(pool):
            nc.gpsimd.memset(minus_half[:], -0.5).then_inc(half_set, 1)
            nc.gpsimd.memset(eps[:], EPS).then_inc(half_set, 1)
            pool.wait_ge(half_set, 2)

            def step(s):
                g = s.g
                for c in range(CF):
                    if c == 1 and s.has(1):
                        need(pool, stats_done, G * (g + 2))
                        nc.gpsimd.tensor_tensor(var_eps[:], mv[:, :, 1], eps[:], ALU.add).then_inc(eps_done, 1)
                        need(pool, eps_done, g + 2)
                        need(pool, xn_done, G * (g + 1))
                        nc.gpsimd.tensor_tensor(rstd[:], var_eps[:], minus_half[:], ALU.pow).then_inc(rstd_done, 1)
                    ok, cc, t = chunk(s, c, 0)
                    if ok:
                        b = cc % RING
                        need(pool, relu_done, t)
                        if cc < CR:
                            need(pool, q_done, CR * g + cc + 1)
                        need(pool, h_lo, t - RING)
                        nc.gpsimd.tensor_tensor(h[:, b], q[:, b] if cc < CR else r[:, b], r[:, b], ALU.mult).then_inc(h_done, 1)
            run_groups(pool, step)

        @block.tensor
        def _(pe):
            def step(s):
                g = s.g
                at = (g % 2) * GP if s.has(0) else 0
                for c in range(CF):
                    ok, cc, t = chunk(s, c, 0)
                    if ok:
                        if c == 0:
                            need(pe, xT_hi, g + 1)
                            need(pe, xT_lo, g + 1)
                        if c < CR:
                            if c == 0:
                                need(pe, cwT_hi, g + 1)
                                need(pe, cwT_lo, g + 1)
                            need(pe, q_done, CR * g + c - 1)
                        need(pe, relu_done, t - 2)
                        ws = slice(c * P, (c + 1) * P)
                        xs = (xh[:, bass.ds(at, GP)], xl[:, bass.ds(at, GP)])
                        split3(nc.tensor, chip.bank(U + c % 2, P, GP), [(chip.w_hi[:, ws], chip.w_lo[:, ws], *xs)]).then_inc(up_psum, 1)
                        if c < CR:
                            nc.tensor.matmul(chip.bank(B + c % 2, P, GP), pairs[:, ws], cwT_h[:, bass.ds(at, GP)], start=True, stop=False)
                            nc.tensor.matmul(chip.bank(B + c % 2, P, GP), pairs[:, ws], cwT_l[:, bass.ds(at, GP)],
                                             start=False, stop=True).then_inc(bc_psum, 1)
                    ok, cc, t = chunk(s, c, LAG)
                    if ok:
                        b = cc % RING
                        need(pe, h_hi, t)
                        need(pe, h_lo, t)
                        if cc == 0:
                            need(pe, yT_sb, g)
                        ws = slice((CF + cc) * P, (CF + cc + 1) * P)
                        last = split3(nc.tensor, chip.bank(Y, P, GP), [(chip.w_hi[:, ws], chip.w_lo[:, ws], hh[:, b], hl[:, b])],
                                      first=cc == 0, last=cc == CF - 1)
                        last.then_inc(down_done, 1)
                    if c == 3 and s.has(1):
                        need(pe, xn_done, G * (g + 2))
                        need(pe, xT_sb, g + 1)
                        for b in range(G):
                            last = nc.tensor.transpose(chip.bank(XT, P, P, b * P), xn[:, b], chip.ident[:])
                        last.then_inc(xnT_psum, 1)
                    if c == 3 and s.has(-1):
                        need(pe, yT_sb, g)
                        for b in range(G):
                            last = nc.tensor.transpose(chip.bank(YT, P, P, b * P), yT[:, b * P:(b + 1) * P], chip.ident[:])
                        last.then_inc(yo_psum, 1)
                    if c == 4 and s.has(1):
                        need(pe, xT_sb, g + 2)
                        need(pe, cwT_lo, g + 1)
                        for b in range(G):
                            last = nc.tensor.matmul(chip.bank(LG, P, NE, b * NE), xT[:, b * P:(b + 1) * P], gate[:], start=True, stop=True)
                        last.then_inc(logit_psum, 1)
                    if c == 8 and s.has(-1):
                        need(pe, x_upd, g)
                    if c == 8 and s.has(1):
                        need(pe, cw_done, g + 2)
                        need(pe, act_sc, 2 * g + 4)
                        for b in range(G):
                            last = nc.tensor.transpose(chip.bank(LG, NE, P, b * P), cw[:, b], chip.ident[:])
                        last.then_inc(cwT_psum, 1)
            run_groups(pe, step)

        @block.scalar
        def _(act):
            def step(s):
                g = s.g
                nxt = ((g + 1) % 2) * GP
                for c in range(CF):
                    ok, cc, t = chunk(s, c, 0)
                    if ok:
                        need(act, up_psum, t)
                        need(act, h_done, t - RING)
                        nc.scalar.activation(r[:, cc % RING], chip.bank(U + c % 2, P, GP), ACT.Relu).then_inc(relu_done, 1)
                    ok, cc, t = chunk(s, c, 1)
                    if ok:
                        need(act, h_done, t)
                        need(act, down_done, t - RING)
                        nc.scalar.copy(hh[:, cc % RING], h[:, cc % RING]).then_inc(h_hi, 1)
                    if c == 2 and s.has(-1):
                        need(act, down_done, CF * g)
                        nc.scalar.copy(yT[:], chip.bank(Y, P, GP)).then_inc(yT_sb, 1)
                    if c == 3 and s.has(1):
                        need(act, xnT_psum, g + 2)
                        need(act, logit_psum, g + 1)
                        need(act, xT_lo, g + 1)
                        nc.scalar.copy(xT[:], chip.bank(XT, P, GP)).then_inc(xT_sb, 1)
                    if c == 4 and s.has(1):
                        need(act, logit_psum, g + 2)
                        need(act, cw_done, g + 1)
                        lg = chip.bank(LG, P, G * NE).rearrange("p (b e) -> p b e", b=G)
                        nc.scalar.activation(th[:], lg, ACT.Tanh, scale=0.5).then_inc(act_sc, 1)
                        nc.scalar.activation(ex[:], lg, ACT.Exp, scale=-1.0).then_inc(act_sc, 1)
                    if c == 8 and s.has(-1):
                        need(act, yo_psum, g)
                    if c == 8 and s.has(1):
                        need(act, cwT_psum, g + 2)
                        need(act, bc_psum, CR * g)
                        nc.scalar.copy(cwT_h[:, bass.ds(nxt, GP)], chip.bank(LG, NE, GP)).then_inc(cwT_hi, 1)
            run_groups(act, step)

        @block.vector
        def _(dve):
            for k in range(2):
                nc.vector.memset(scan[:, k], 0.0).then_inc(scan_zero, 1)
            dve.wait_ge(scan_zero, 2)
            chain = Chain(dve, router, 31)
            V = nc.vector

            def over_experts(t):
                return t.unsqueeze(2).broadcast_to([P, G, NE])

            def router_groups():
                chain.link(V.tensor_scalar(sc[:], th[:], 0.5, 0.5, ALU.mult, ALU.add))
                chain.link(V.tensor_scalar(ex[:], ex[:], 1.0, None, ALU.add))
                chain.link(V.tensor_tensor(sc[:], sc[:], bias[:].unsqueeze(1).broadcast_to([P, G, NE]), ALU.add))
                s4 = sc[:].rearrange("p b (i e) -> p (b i) e", e=4)
                chain.link(V.tensor_tensor(pair_max[:], s4[:, :, 0:2], s4[:, :, 2:4], ALU.max))
                chain.link(V.tensor_tensor(pair_min[:], s4[:, :, 0:2], s4[:, :, 2:4], ALU.min))
                V.tensor_tensor(best[:], pair_max[:, :, 0], pair_max[:, :, 1], ALU.max)
                chain.link(V.tensor_tensor(second[:], pair_max[:, :, 0], pair_max[:, :, 1], ALU.min))
                chain.link(V.tensor_tensor(other[:], pair_min[:, :, 0], pair_min[:, :, 1], ALU.max))
                chain.link(V.tensor_tensor(second[:], second[:], other[:], ALU.max))
                chain.link(V.tensor_tensor(gs[:].rearrange("p b i -> p (b i)"), best[:], second[:], ALU.add))

            def router_choice():
                gi = gs[:].unsqueeze(3).broadcast_to([P, G, NGRP, NGRP])
                gj = gs[:].unsqueeze(2).broadcast_to([P, G, NGRP, NGRP])
                m = before[:].rearrange("p (k i j) -> p k i j", k=2, i=NGRP)
                V.tensor_tensor(ge[:], gj, gi, ALU.is_ge)
                chain.link(V.tensor_tensor(gt4[:], gj, gi, ALU.is_gt))
                chain.link(V.tensor_tensor(ge[:], ge[:], m[:, 0].unsqueeze(1).broadcast_to([P, G, NGRP, NGRP]), ALU.mult))
                chain.link(V.tensor_tensor(gt4[:], gt4[:], m[:, 1].unsqueeze(1).broadcast_to([P, G, NGRP, NGRP]), ALU.mult))
                chain.link(V.tensor_tensor(ge[:], ge[:], gt4[:], ALU.add))
                chain.link(V.tensor_reduce(rank[:], ge[:], AX_X, ALU.add))
                chain.link(V.tensor_scalar(rank[:], rank[:], 1.5, None, ALU.is_lt))
                chain.link(V.tensor_tensor(masked[:].rearrange("p b (i e) -> p b i e", e=4), sc[:].rearrange("p b (i e) -> p b i e", e=4),
                                           rank[:].unsqueeze(3).broadcast_to([P, G, NGRP, 4]), ALU.mult))
                V.reciprocal(sig[:], ex[:])
                for b in range(G):
                    last = V.max(top8[:, b], masked[:, b])
                chain.link(last)

            def router_weights():
                fourth = over_experts(top8[:, :, TOP - 1])
                V.tensor_tensor(over[:], masked[:], fourth, ALU.is_gt)
                chain.link(V.tensor_tensor(scan[:, 0, :, PAD:], masked[:], fourth, ALU.is_equal))
                V.tensor_copy(same[:], scan[:, 0, :, PAD:])
                chain.link(V.tensor_reduce(n_over[:], over[:], AX_X, ALU.add))
                for k, d in enumerate((1, 2, 4, 8)):
                    src, dst = scan[:, k % 2], scan[:, 1 - k % 2]
                    chain.link(V.tensor_tensor(dst[:, :, PAD:], src[:, :, PAD:], src[:, :, PAD - d:PAD + NE - d], ALU.add))
                chain.link(V.tensor_tensor(masked[:], scan[:, 0, :, PAD:], over_experts(n_over[:]), ALU.add))
                chain.link(V.scalar_tensor_tensor(same[:], masked[:], TOP + 0.5, same[:], ALU.is_lt, ALU.mult))
                chain.link(V.tensor_tensor(over[:], over[:], same[:], ALU.add))
                chain.link(V.tensor_tensor(sig[:], sig[:], over[:], ALU.mult))
                V_sum = V.tensor_reduce(w_sum[:], sig[:], AX_X, ALU.add)
                return V_sum

            def step(s):
                g = s.g
                nxt = ((g + 1) % 2) * GP
                for c in range(CF):
                    if c == 1 and s.has(1):
                        need(dve, bn_done, G * (g + 2))
                    ok, cc, t = chunk(s, c, 0)
                    if ok and cc < CR:
                        need(dve, bc_psum, CR * g + cc + 1)
                        need(dve, relu_done, t)
                        need(dve, h_done, t - RING)
                        V.tensor_tensor(q[:, cc % RING], r[:, cc % RING], chip.bank(B + c % 2, P, GP), ALU.mult).then_inc(q_done, 1)
                    ok, cc, t = chunk(s, c, 1)
                    if ok:
                        b = cc % RING
                        need(dve, h_hi, t)
                        V.tensor_tensor(hl[:, b], h[:, b], hh[:, b].bitcast(F32), ALU.subtract).then_inc(h_lo, 1)
                    if c == 0 and s.has(1):
                        for b in range(G):
                            V.bn_stats(bn[:, b], chip.xt(G * (g + 1) + b)).then_inc(bn_done, 1)
                    if c == 1 and s.has(1):
                        for b in range(G):
                            V.bn_aggr(mv[:, b], bn[:, b]).then_inc(stats_done, 1)
                    if c == 2 and s.has(1):
                        need(dve, rstd_done, g + 2)
                        need(dve, xnT_psum, g + 1)
                        for b in range(G):
                            V.tensor_scalar(xn[:, b], chip.xt(G * (g + 1) + b), mv[:, b, 0:1], rstd[:, b:b + 1],
                                            ALU.subtract, ALU.mult).then_inc(xn_done, 1)
                    if c == 3 and s.has(1):
                        need(dve, xT_sb, g + 2)
                        need(dve, up_psum, CF * g)
                        V.tensor_copy(xh[:, bass.ds(nxt, GP)], xT[:]).then_inc(xT_hi, 1)
                        need(dve, xT_hi, g + 2)
                        V.tensor_tensor(xl[:, bass.ds(nxt, GP)], xT[:], xh[:, bass.ds(nxt, GP)].bitcast(F32), ALU.subtract).then_inc(xT_lo, 1)
                    if c == 4 and s.has(-1):
                        need(dve, yo_psum, g)
                        xg = chip.xt(G * (g - 1), G)
                        V.tensor_tensor(xg, xg, chip.bank(YT, P, GP), ALU.add).then_inc(x_upd, 1)
                    if c == 5 and s.has(1):
                        need(dve, act_sc, 2 * g + 4)
                        chain.begin(g + 1)
                        router_groups()
                    if c == 6 and s.has(1):
                        router_choice()
                    if c == 7 and s.has(1):
                        chain.link(router_weights())
                        chain.link(V.tensor_scalar(w_sum[:], w_sum[:], 1e-20, None, ALU.add))
                        chain.link(V.reciprocal(w_inv[:], w_sum[:]))
                        chain.link(V.tensor_tensor(sig[:], sig[:], over_experts(w_inv[:]), ALU.mult))
                        need(dve, cwT_psum, g + 1)
                        V.tensor_scalar(cw[:], sig[:], ROUTED_SCALE, None, ALU.mult).then_inc(cw_done, 1)
                        chain.end()
                    if c == 8 and s.has(1):
                        need(dve, cwT_hi, g + 2)
                        V.tensor_tensor(cwT_l[:, bass.ds(nxt, GP)], chip.bank(LG, NE, GP), cwT_h[:, bass.ds(nxt, GP)].bitcast(F32),
                                        ALU.subtract).then_inc(cwT_lo, 1)
            run_groups(dve, step)



E1 = 8
D1 = 512
C1 = D1 // P
CI = E1 * C1


def prepare_moe1(nc, chip, a, w):
    big, small, t_psum, t_sb, hi_a, hi_b, lo = (chip.sem("m1_" + n) for n in "big small t_psum t_sb hi_a hi_b lo".split())
    big2 = chip.sem("m1_big2")
    with ExitStack() as own:
        def sb(name, shape, dt=F32):
            return own.enter_context(nc.sbuf_tensor("m1_" + name, shape, dt))

        w1 = sb("w1", [P, E1, D1])
        w2 = sb("w2", [P, CI, P])
        rows = sb("rows", [CI + 2, P])
        qk = sb("qk", [P, 2 * P])
        b2 = sb("b2", [E1, P])
        sel = sb("sel", [E1, E1 * P])
        block = own.enter_context(nc.Block())

        def row(name, n):
            return a[name].rearrange("(o d) -> o d", o=1).broadcast_to([n, a[name].shape[0]])

        @block.sync
        def _(sp):
            for dst, src in ((rows[0:CI], a["b1"].rearrange("e (c p) -> (e c) p", p=P)), (rows[CI:CI + 1], row("bq", 1)),
                             (rows[CI + 1:CI + 2], row("bk", 1)), (qk[:, 0:P], a["Wq"]), (qk[:, P:], a["Wk"]),
                             (w["wv"][:], a["Wv"]), (w["wo"][:], a["Wo"]), (w["wg"][:], a["Wg"]), (w["bv"][:], row("bv", P)),
                             (w["bo"][:], row("bo", P)), (w["bg"][:], row("bg", P)), (b2[:], a["b2"]), (sel[:], a["ones_rows"])):
                sp.dma_start(dst, src).then_inc(small, 16)
            sp.dma_start(w1[:], a["W1"].rearrange("e h d -> h e d")).then_inc(big, 16)
            sp.dma_start(w2[:], a["W2"].rearrange("e (c p) h -> p (e c) h", p=P)).then_inc(big2, 16)
            sp.wait_ge(small, 16 * 13)

        @block.tensor
        def _(pe):
            pe.wait_ge(small, 16 * 13)
            nc.tensor.transpose(chip.bank(0, P, CI + 2), rows[:], chip.ident[0:CI + 2, 0:CI + 2]).then_inc(t_psum, 1)

        @block.scalar
        def _(act):
            act.wait_ge(t_psum, 1)
            nc.scalar.copy(w["cols"][:], chip.bank(0, P, CI + 2)).then_inc(t_sb, 1)
            act.wait_ge(big, 16)
            nc.scalar.copy(chip.w_hi[:, 0:CI * P // 2], w1[:, 0:E1 // 2]).then_inc(hi_a, 1)
            nc.scalar.copy(chip.w_hi[:, CI * P // 2:], w1[:, E1 // 2:]).then_inc(hi_a, 1)
            act.wait_ge(big2, 16)
            nc.scalar.copy(w["w2h"][:, 0:CI // 2], w2[:, 0:CI // 2]).then_inc(hi_a, 1)
            nc.scalar.copy(w["w2h"][:, CI // 2:], w2[:, CI // 2:]).then_inc(hi_a, 1)

        @block.vector
        def _(dve):
            dve.wait_ge(small, 16 * 13)
            nc.vector.tensor_copy(w["qk_h"][:], qk[:]).then_inc(hi_b, 1)
            nc.vector.tensor_copy(w["b2h"][:], b2[:]).then_inc(hi_b, 1)
            nc.vector.tensor_copy(w["sel"][:], sel[:]).then_inc(hi_b, 1)
            dve.wait_ge(hi_b, 3)
            nc.vector.tensor_tensor(w["qk_l"][:], qk[:], w["qk_h"][:].bitcast(F32), ALU.subtract).then_inc(lo, 1)
            nc.vector.tensor_tensor(w["b2l"][:], b2[:], w["b2h"][:].bitcast(F32), ALU.subtract).then_inc(lo, 1)
            for k, (dst, src, hi) in enumerate((
                    (chip.w_lo[:, 0:CI * P // 2], w1[:, 0:E1 // 2].rearrange("p e d -> p (e d)"), chip.w_hi[:, 0:CI * P // 2]),
                    (chip.w_lo[:, CI * P // 2:], w1[:, E1 // 2:].rearrange("p e d -> p (e d)"), chip.w_hi[:, CI * P // 2:]),
                    (w["w2l"][:, 0:CI // 2], w2[:, 0:CI // 2], w["w2h"][:, 0:CI // 2]),
                    (w["w2l"][:, CI // 2:], w2[:, CI // 2:], w["w2h"][:, CI // 2:]))):
                dve.wait_ge(hi_a, k + 1)
                nc.vector.tensor_tensor(dst, src, hi.bitcast(F32), ALU.subtract).then_inc(lo, 1)


def ffn1_stage(nc, chip, a, out):
    names = ("bn_done stats_done eps_done rstd_done xn_done xnb_done xT_psum xT_sb xT_hi xT_lo q_psum k_psum v_psum qT_sb kT_sb v_sb "
             "s_psum s_max s_sub s_exp s_sum s_inv w_done wT_psum wT_sb aT_psum aT_sb o_psum x2_done res_done x2T_psum x2T_sb "
             "x2T_hi x2T_lo g_psum g_logit g_max g_sub g_exp g_sum g_inv gate_done gT_psum gT_hi gT_lo gb_psum gb_sb b2_psum acc_set "
             "up_psum relu_done hi_act hi_dve h_lo down_done scaled acc_done y_done yo_psum x_upd out_done half").split()
    S = {n: chip.sem("f1_" + n) for n in names}
    (bn_done, stats_done, eps_done, rstd_done, xn_done, xnb_done, xT_psum, xT_sb, xT_hi, xT_lo, q_psum, k_psum, v_psum, qT_sb,
     kT_sb, v_sb, s_psum, s_max, s_sub, s_exp, s_sum, s_inv, w_done, wT_psum, wT_sb, aT_psum, aT_sb, o_psum, x2_done, res_done,
     x2T_psum, x2T_sb, x2T_hi, x2T_lo, g_psum, g_logit, g_max, g_sub, g_exp, g_sum, g_inv, gate_done, gT_psum, gT_hi, gT_lo,
     gb_psum, gb_sb, b2_psum, acc_set, up_psum, relu_done, hi_act, hi_dve, h_lo, down_done, scaled, acc_done, y_done,
     yo_psum, x_upd, out_done, half_set) = (S[n] for n in names)
    RING, LAG = 4, 2
    U, Y, GB, A, B, C = 0, 2, 4, 5, 6, 7
    with ExitStack() as own:
        def sb(name, shape, dt=F32):
            return own.enter_context(nc.sbuf_tensor("f1_" + name, shape, dt))

        w = {"wv": sb("wv", [P, P]), "wo": sb("wo", [P, P]), "wg": sb("wg", [P, E1]), "bv": sb("bv", [P, P]), "bo": sb("bo", [P, P]),
             "bg": sb("bg", [P, E1]), "cols": sb("cols", [P, CI + 2]), "qk_h": sb("qk_h", [P, 2 * P], F32R),
             "qk_l": sb("qk_l", [P, 2 * P], F32R), "b2h": sb("b2h", [E1, P], F32R), "b2l": sb("b2l", [E1, P], F32R),
             "sel": sb("sel", [E1, E1 * P], F32R), "w2h": sb("w2h", [P, CI, P], F32R), "w2l": sb("w2l", [P, CI, P], F32R)}
        prepare_moe1(nc, chip, a, w)
        bn = sb("bn", [P, G, 6])
        mv = sb("mv", [P, G, 2])
        rstd = sb("rstd", [P, G])
        var_eps = sb("var_eps", [P, G])
        minus_half = sb("minus_half", [P, G])
        eps = sb("eps", [P, G])
        xn = sb("xn", [P, G, P])
        xnb = sb("xnb", [P, G, P])
        xT = sb("xT", [P, GP])
        xTh = sb("xTh", [P, GP], F32R)
        xTl = sb("xTl", [P, GP], F32R)
        qT = sb("qT", [P, GP])
        kT = sb("kT", [P, GP])
        v = sb("v", [P, G, P])
        att = sb("att", [P, G, P])
        smax = sb("smax", [P, G])
        ssum = sb("ssum", [P, G])
        sinv = sb("sinv", [P, G])
        attT = sb("attT", [P, GP])
        aT = sb("aT", [P, GP])
        x2 = sb("x2", [P, G, P])
        x2T = sb("x2T", [P, GP])
        x2h = sb("x2h", [P, 2 * GP], F32R)
        x2l = sb("x2l", [P, 2 * GP], F32R)
        gates = sb("gates", [P, G, E1])
        gmax = sb("gmax", [P, G])
        gsum = sb("gsum", [P, G])
        ginv = sb("ginv", [P, G])
        gTh = sb("gTh", [E1, 2 * GP], F32R)
        gTl = sb("gTl", [E1, 2 * GP], F32R)
        gb = sb("gb", [P, 2, GP])
        h = sb("h", [P, RING, GP])
        hh = sb("hh", [P, RING, GP], F32R)
        hl = sb("hl", [P, RING, GP], F32R)
        part = sb("part", [P, 2, GP])
        acc = sb("acc", [P, GP])
        yT = sb("yT", [P, GP])
        block = own.enter_context(nc.Block())

        def item(s, u, late):
            return (s.has(0) if u >= late else s.has(-1)), (u - late) % CI, CI * s.g + u - late + 1

        def four(t):
            return t.rearrange("p (b d) -> p b d", b=G)

        def per_batch(t):
            return t.unsqueeze(2).broadcast_to([P, G, P])

        def all_batches(t, width):
            return t.unsqueeze(1).broadcast_to([P, G, width])

        @block.sync
        def _(sp):
            with sp.Fori(0, NG) as g:
                sp.wait_ge(x_upd, g + 1)
                sp.dma_start(out[bass.ds(g * G, G)].rearrange("b t d -> t b d"), four(chip.xt(g * G, G))).then_inc(out_done, 16)
            sp.wait_ge(out_done, 16 * NG)

        @block.gpsimd
        def _(pool):
            nc.gpsimd.memset(minus_half[:], -0.5).then_inc(half_set, 1)
            nc.gpsimd.memset(eps[:], EPS).then_inc(half_set, 1)
            pool.wait_ge(half_set, 2)

            def step(s):
                g = s.g
                for u in range(CI):
                    if u % 4 == 2:
                        e = (u - 6) // 4 % E1
                        if s.has(0) if u >= 6 else s.has(-1):
                            m = E1 * g + (u - 6) // 4 + 1
                            need(pool, scaled, m)
                            if e == 0:
                                need(pool, acc_set, g + 1)
                            else:
                                need(pool, acc_done, (E1 - 1) * (g if u >= 6 else g - 1) + e)
                            if e < E1 - 1:
                                nc.gpsimd.tensor_tensor(acc[:], acc[:], part[:, e % 2], ALU.add).then_inc(acc_done, 1)
                            else:
                                nc.gpsimd.tensor_tensor(yT[:], acc[:], part[:, e % 2], ALU.add).then_inc(y_done, 1)
                    if u == 8 and s.has(-1):
                        need(pool, yo_psum, g)
                    if u == 1 and s.has(1):
                        need(pool, stats_done, G * (g + 2))
                        nc.gpsimd.tensor_tensor(var_eps[:], mv[:, :, 1], eps[:], ALU.add).then_inc(eps_done, 1)
                        need(pool, eps_done, g + 2)
                        need(pool, xn_done, G * (g + 1))
                        nc.gpsimd.tensor_tensor(rstd[:], var_eps[:], minus_half[:], ALU.pow).then_inc(rstd_done, 1)
                    if u == 3 and s.has(1):
                        need(pool, xn_done, G * (g + 2))
                        need(pool, x2_done, g + 1)
                        nc.gpsimd.tensor_tensor(xnb[:], xn[:], all_batches(w["bo"][:], P), ALU.add).then_inc(xnb_done, 1)
                    if u == 19 and s.has(1):
                        need(pool, x2_done, g + 2)
                        xg = four(chip.xt(G * (g + 1), G))
                        nc.gpsimd.tensor_tensor(xg, xg, x2[:], ALU.add).then_inc(res_done, 1)
            run_groups(pool, step)

        @block.tensor
        def _(pe):
            T = nc.tensor

            def step(s):
                g = s.g
                at = (g % 2) * GP
                for u in range(CI):
                    ok, cc, t = item(s, u, 0)
                    if ok:
                        if u == 0:
                            need(pe, x2T_hi, g + 1)
                            need(pe, x2T_lo, g + 1)
                        if u % 4 == 3:
                            if u == 3:
                                need(pe, gT_hi, g + 1)
                                need(pe, gT_lo, g + 1)
                            need(pe, gb_sb, E1 * g + u // 4)
                            if u == 7:
                                need(pe, acc_set, g + 1)
                        if u == 5:
                            need(pe, gb_sb, E1 * g + 1)
                        need(pe, relu_done, t - 2)
                        ws = slice(u * P, (u + 1) * P)
                        split3(T, chip.bank(U + u % 2, P, GP),
                               [(chip.w_hi[:, ws], chip.w_lo[:, ws], x2h[:, bass.ds(at, GP)], x2l[:, bass.ds(at, GP)])]).then_inc(up_psum, 1)
                        if u % 4 == 3:
                            e = u // 4
                            es = slice(e * P, (e + 1) * P)
                            T.matmul(chip.bank(GB, P, GP), w["sel"][:, es], gTh[:, bass.ds(at, GP)], start=True, stop=False)
                            T.matmul(chip.bank(GB, P, GP), w["sel"][:, es], gTl[:, bass.ds(at, GP)], start=False, stop=True).then_inc(gb_psum, 1)
                        if u == 5:
                            split3(T, chip.bank(GB, P, GP), [(w["b2h"][:], w["b2l"][:], gTh[:, bass.ds(at, GP)], gTl[:, bass.ds(at, GP)])]).then_inc(b2_psum, 1)
                    ok, cc, t = item(s, u, LAG)
                    if ok:
                        b = cc % RING
                        need(pe, h_lo, t)
                        if cc % 4 == 0:
                            need(pe, scaled, E1 * (g if u >= LAG else g - 1) + cc // 4 - 1)
                        split3(T, chip.bank(Y + cc // 4 % 2, P, GP), [(w["w2h"][:, cc], w["w2l"][:, cc], hh[:, b], hl[:, b])],
                               first=cc % 4 == 0, last=cc % 4 == 3).then_inc(down_done, 1)
                    if u == 3 and s.has(1):
                        need(pe, xn_done, G * (g + 2))
                        need(pe, x2T_sb, g + 1)
                        for b in range(G):
                            last = T.transpose(chip.bank(A, P, P, b * P), xn[:, b], chip.ident[:])
                        last.then_inc(xT_psum, 1)
                    if u == 4 and s.has(1):
                        need(pe, xT_lo, g + 2)
                        need(pe, g_logit, g + 1)
                        split3(T, chip.bank(B, P, GP), [(w["qk_h"][:, 0:P], w["qk_l"][:, 0:P], xTh[:], xTl[:])]).then_inc(q_psum, 1)
                        need(pe, gT_lo, g + 1)
                        split3(T, chip.bank(C, P, GP), [(w["qk_h"][:, P:], w["qk_l"][:, P:], xTh[:], xTl[:])]).then_inc(k_psum, 1)
                    if u == 5 and s.has(1):
                        need(pe, xT_sb, g + 2)
                        for b in range(G):
                            last = T.matmul(chip.bank(A, P, P, b * P), xT[:, b * P:(b + 1) * P], w["wv"][:], start=True, stop=True)
                        last.then_inc(v_psum, 1)
                    if u == 7 and s.has(-1):
                        need(pe, y_done, g)
                        if s.has(1):
                            need(pe, qT_sb, g + 2)
                        for b in range(G):
                            last = T.transpose(chip.bank(B, P, P, b * P), yT[:, b * P:(b + 1) * P], chip.ident[:])
                        last.then_inc(yo_psum, 1)
                    if u == 8 and s.has(1):
                        need(pe, qT_sb, g + 2)
                        need(pe, kT_sb, g + 2)
                        for b in range(G):
                            bs = slice(b * P, (b + 1) * P)
                            last = T.matmul(chip.bank(C, P, P, b * P), qT[:, bs], kT[:, bs], start=True, stop=True)
                        last.then_inc(s_psum, 1)
                    if u == 13 and s.has(1):
                        need(pe, w_done, g + 2)
                        need(pe, v_sb, g + 2)
                        for b in range(G):
                            last = T.transpose(chip.bank(A, P, P, b * P), att[:, b], chip.ident[:])
                        last.then_inc(wT_psum, 1)
                    if u == 15 and s.has(1):
                        need(pe, wT_sb, g + 2)
                        need(pe, x_upd, g)
                        for b in range(G):
                            last = T.matmul(chip.bank(B, P, P, b * P), v[:, b], attT[:, b * P:(b + 1) * P], start=True, stop=True)
                        last.then_inc(aT_psum, 1)
                    if u == 17 and s.has(1):
                        need(pe, aT_sb, g + 2)
                        need(pe, s_sub, g + 2)
                        for b in range(G):
                            last = T.matmul(chip.bank(C, P, P, b * P), aT[:, b * P:(b + 1) * P], w["wo"][:], start=True, stop=True)
                        last.then_inc(o_psum, 1)
                    if u == 19 and s.has(1):
                        need(pe, x2_done, g + 2)
                        need(pe, wT_sb, g + 2)
                        for b in range(G):
                            last = T.transpose(chip.bank(A, P, P, b * P), x2[:, b], chip.ident[:])
                        last.then_inc(x2T_psum, 1)
                    if u == 21 and s.has(1):
                        need(pe, x2T_sb, g + 2)
                        need(pe, aT_sb, g + 2)
                        for b in range(G):
                            last = T.matmul(chip.bank(B, P, E1, b * E1), x2T[:, b * P:(b + 1) * P], w["wg"][:], start=True, stop=True)
                        last.then_inc(g_psum, 1)
                    if u == 26 and s.has(1):
                        need(pe, gate_done, g + 2)
                        need(pe, x2_done, g + 2)
                        for b in range(G):
                            last = T.transpose(chip.bank(C, E1, P, b * P), gates[:, b], chip.ident[:])
                        last.then_inc(gT_psum, 1)
            run_groups(pe, step)

        @block.scalar
        def _(act):
            cols = w["cols"]

            def step(s):
                g = s.g
                nxt = ((g + 1) % 2) * GP
                for u in range(CI):
                    ok, cc, t = item(s, u, 0)
                    if ok:
                        need(act, up_psum, t)
                        need(act, h_lo, t - RING)
                        nc.scalar.activation(h[:, cc % RING], chip.bank(U + u % 2, P, GP), ACT.Relu,
                                             bias=cols[:, cc:cc + 1]).then_inc(relu_done, 1)
                        if u % 2 == 0:
                            need(act, relu_done, t)
                            need(act, down_done, t - RING)
                            nc.scalar.copy(hh[:, cc % RING], h[:, cc % RING]).then_inc(hi_act, 1)
                        if u % 4 == 3:
                            e = u // 4
                            need(act, gb_psum, E1 * g + e + 1)
                            need(act, scaled, E1 * g + e - 1)
                            nc.scalar.copy(gb[:, e % 2], chip.bank(GB, P, GP)).then_inc(gb_sb, 1)
                        if u == 5:
                            need(act, b2_psum, g + 1)
                            need(act, y_done, g)
                            nc.scalar.copy(acc[:], chip.bank(GB, P, GP)).then_inc(acc_set, 1)
                    if not s.has(1):
                        continue
                    if u == 3:
                        need(act, xT_psum, g + 2)
                        need(act, xT_lo, g + 1)
                        need(act, v_psum, g + 1)
                        nc.scalar.copy(xT[:], chip.bank(A, P, GP)).then_inc(xT_sb, 1)
                    if u == 4:
                        need(act, q_psum, g + 2)
                        need(act, s_psum, g + 1)
                        nc.scalar.activation(qT[:], chip.bank(B, P, GP), ACT.Identity, bias=cols[:, CI:CI + 1]).then_inc(qT_sb, 1)
                        need(act, k_psum, g + 2)
                        nc.scalar.activation(kT[:], chip.bank(C, P, GP), ACT.Identity, bias=cols[:, CI + 1:CI + 2]).then_inc(kT_sb, 1)
                    if u == 10:
                        need(act, s_sub, g + 2)
                        nc.scalar.activation(att[:], att[:], ACT.Exp, scale=P ** -0.5).then_inc(s_exp, 1)
                    if u == 13:
                        need(act, wT_psum, g + 2)
                        need(act, aT_psum, g + 1)
                        nc.scalar.copy(attT[:], chip.bank(A, P, GP)).then_inc(wT_sb, 1)
                    if u == 15:
                        need(act, aT_psum, g + 2)
                        need(act, o_psum, g + 1)
                        nc.scalar.copy(aT[:], chip.bank(B, P, GP)).then_inc(aT_sb, 1)
                    if u == 19:
                        need(act, x2T_psum, g + 2)
                        need(act, g_psum, g + 1)
                        need(act, x2T_lo, g + 1)
                        nc.scalar.copy(x2T[:], chip.bank(A, P, GP)).then_inc(x2T_sb, 1)
                    if u == 23:
                        need(act, g_sub, g + 2)
                        nc.scalar.activation(gates[:], gates[:], ACT.Exp).then_inc(g_exp, 1)
                    if u == 26:
                        need(act, gT_psum, g + 2)
                        need(act, gb_psum, E1 * g)
                        need(act, b2_psum, g)
                        nc.scalar.copy(gTh[:, bass.ds(nxt, GP)], chip.bank(C, E1, GP)).then_inc(gT_hi, 1)
            run_groups(act, step)

        @block.vector
        def _(dve):
            V = nc.vector

            def step(s):
                g = s.g
                nxt = ((g + 1) % 2) * GP
                for u in range(CI):
                    if u == 1 and s.has(1):
                        need(dve, bn_done, G * (g + 2))
                    ok, cc, t = item(s, u, 0)
                    if ok:
                        b = cc % RING
                        if u % 2 == 0:
                            need(dve, hi_act, CI // 2 * g + u // 2 + 1)
                        else:
                            need(dve, relu_done, t)
                            need(dve, down_done, t - RING)
                            V.tensor_copy(hh[:, b], h[:, b]).then_inc(hi_dve, 1)
                            need(dve, hi_dve, CI // 2 * g + u // 2 + 1)
                        V.tensor_tensor(hl[:, b], h[:, b], hh[:, b].bitcast(F32), ALU.subtract).then_inc(h_lo, 1)
                    if u % 4 == 1 and (s.has(0) if u >= 5 else s.has(-1)):
                        e = (u - 5) // 4 % E1
                        m = E1 * g + (u - 5) // 4
                        need(dve, down_done, 4 * m + 4)
                        need(dve, gb_sb, m + 1)
                        if e >= 2:
                            need(dve, acc_done, (E1 - 1) * (g if u >= 5 else g - 1) + e - 1)
                        elif e == 1:
                            need(dve, y_done, g)
                        else:
                            need(dve, acc_done, (E1 - 1) * g)
                        V.tensor_tensor(part[:, e % 2], chip.bank(Y + e % 2, P, GP), gb[:, e % 2], ALU.mult).then_inc(scaled, 1)
                    if u == 8 and s.has(-1):
                        need(dve, yo_psum, g)
                        need(dve, res_done, g)
                        xg = chip.xt(G * (g - 1), G)
                        V.tensor_tensor(xg, xg, chip.bank(B, P, GP), ALU.add).then_inc(x_upd, 1)
                    if not s.has(1):
                        continue
                    if u == 0:
                        for b in range(G):
                            V.bn_stats(bn[:, b], chip.xt(G * (g + 1) + b)).then_inc(bn_done, 1)
                    if u == 1:
                        for b in range(G):
                            V.bn_aggr(mv[:, b], bn[:, b]).then_inc(stats_done, 1)
                    if u == 2:
                        need(dve, rstd_done, g + 2)
                        need(dve, xT_psum, g + 1)
                        need(dve, xnb_done, g + 1)
                        for b in range(G):
                            V.tensor_scalar(xn[:, b], chip.xt(G * (g + 1) + b), mv[:, b, 0:1], rstd[:, b:b + 1],
                                            ALU.subtract, ALU.mult).then_inc(xn_done, 1)
                    if u == 3:
                        need(dve, xT_sb, g + 2)
                        need(dve, k_psum, g + 1)
                        V.tensor_copy(xTh[:], xT[:]).then_inc(xT_hi, 1)
                        need(dve, xT_hi, g + 2)
                        V.tensor_tensor(xTl[:], xT[:], xTh[:].bitcast(F32), ALU.subtract).then_inc(xT_lo, 1)
                    if u == 5:
                        need(dve, v_psum, g + 2)
                        need(dve, aT_psum, g + 1)
                        V.tensor_tensor(v[:], four(chip.bank(A, P, GP)), all_batches(w["bv"][:], P), ALU.add).then_inc(v_sb, 1)
                    if u == 9:
                        need(dve, s_psum, g + 2)
                        V.tensor_reduce(smax[:], four(chip.bank(C, P, GP)), AX_X, ALU.max).then_inc(s_max, 1)
                        need(dve, s_max, g + 2)
                        need(dve, wT_psum, g + 1)
                        V.tensor_tensor(att[:], four(chip.bank(C, P, GP)), per_batch(smax[:]), ALU.subtract).then_inc(s_sub, 1)
                    if u == 11:
                        need(dve, s_exp, g + 2)
                        V.tensor_reduce(ssum[:], att[:], AX_X, ALU.add).then_inc(s_sum, 1)
                        need(dve, s_sum, g + 2)
                        V.reciprocal(sinv[:], ssum[:]).then_inc(s_inv, 1)
                        need(dve, s_inv, g + 2)
                        V.tensor_tensor(att[:], att[:], per_batch(sinv[:]), ALU.mult).then_inc(w_done, 1)
                    if u == 17:
                        need(dve, o_psum, g + 2)
                        need(dve, xnb_done, g + 2)
                        need(dve, x2T_psum, g + 1)
                        need(dve, res_done, g + 1)
                        V.tensor_tensor(x2[:], xnb[:], four(chip.bank(C, P, GP)), ALU.add).then_inc(x2_done, 1)
                    if u == 20:
                        need(dve, x2T_sb, g + 2)
                        need(dve, up_psum, CI * g)
                        V.tensor_copy(x2h[:, bass.ds(nxt, GP)], x2T[:]).then_inc(x2T_hi, 1)
                        need(dve, x2T_hi, g + 2)
                        V.tensor_tensor(x2l[:, bass.ds(nxt, GP)], x2T[:], x2h[:, bass.ds(nxt, GP)].bitcast(F32), ALU.subtract).then_inc(x2T_lo, 1)
                    if u == 22:
                        gl = chip.bank(B, P, G * E1).rearrange("p (b e) -> p b e", b=G)
                        need(dve, g_psum, g + 2)
                        need(dve, gT_psum, g + 1)
                        V.tensor_tensor(gates[:], gl, all_batches(w["bg"][:], E1), ALU.add).then_inc(g_logit, 1)
                        need(dve, g_logit, g + 2)
                        V.tensor_reduce(gmax[:], gates[:], AX_X, ALU.max).then_inc(g_max, 1)
                        need(dve, g_max, g + 2)
                        V.tensor_tensor(gates[:], gates[:], gmax[:].unsqueeze(2).broadcast_to([P, G, E1]), ALU.subtract).then_inc(g_sub, 1)
                    if u == 24:
                        need(dve, g_exp, g + 2)
                        V.tensor_reduce(gsum[:], gates[:], AX_X, ALU.add).then_inc(g_sum, 1)
                        need(dve, g_sum, g + 2)
                        V.reciprocal(ginv[:], gsum[:]).then_inc(g_inv, 1)
                        need(dve, g_inv, g + 2)
                        V.tensor_tensor(gates[:], gates[:], ginv[:].unsqueeze(2).broadcast_to([P, G, E1]), ALU.mult).then_inc(gate_done, 1)
                    if u == 26:
                        need(dve, gT_hi, g + 2)
                        V.tensor_tensor(gTl[:, bass.ds(nxt, GP)], chip.bank(C, E1, GP), gTh[:, bass.ds(nxt, GP)].bitcast(F32),
                                        ALU.subtract).then_inc(gT_lo, 1)
            run_groups(dve, step)


def network(nc, a, out):
    with ExitStack() as ctx:
        chip = Chip(nc, ctx)
        x_in = (chip.x[:].rearrange("p (b d) -> p b d", b=NB), a["x"].rearrange("b t d -> t b d"))
        prep_sems, xattn_sems = {}, {}
        for L in range(2):
            names = {n: a[f"L{L}_xattn_{n}"] for n in ("Wq", "Wk", "Wv", "Wo", "bo")}
            prepare_xattn(nc, chip, L, {**names, "ident": a["ident"]}, prep_sems, loads=[x_in] if L == 0 else [])
            xattn_stage(nc, chip, L, a["ctx_768"], xattn_sems)
            ffn = {n[len("L0_ffn_"):]: t for n, t in a.items() if n.startswith(f"L{L}_ffn_")}
            if L == 0:
                moe0_stage(nc, chip, {**ffn, "pairs": a["pairs"], "before": a["before"]})
            else:
                ffn1_stage(nc, chip, {**ffn, "ones_rows": a["ones_rows"]}, out)


_OUT = (NB, P, P)


def kernel(**inputs):
    import numpy as np
    import concourse.bacc as bacc
    from concourse import mybir as _mybir
    from concourse.bass_utils import run_bass_kernel_spmd

    f = np.float32
    rows = np.arange(NGRP)[:, None], np.arange(NGRP)[None]
    constants = {
        "ident": np.eye(P, dtype=f),
        "pairs": (np.arange(NE)[:, None] == np.arange(CR * P)[None] // FI).astype(f),
        "ones_rows": (np.arange(E1)[:, None] == np.arange(E1 * P)[None] // P).astype(f),
        "before": np.stack([rows[1] < rows[0], rows[1] > rows[0]]).astype(f).reshape(-1),
    }
    nc = bacc.Bacc("TRN2", target_bir_lowering=False, num_devices=1)
    arrays, a = {}, {}
    for name, t in {**inputs, **constants}.items():
        t = np.ascontiguousarray(t)
        arrays[f"in_{name}"] = t
        a[name] = nc.dram_tensor(f"in_{name}", t.shape, _mybir.dt.from_np(t.dtype), kind="ExternalInput").ap()
    out = nc.dram_tensor("out_0", _OUT, F32, kind="ExternalOutput").ap()
    network(nc, a, out)
    r = run_bass_kernel_spmd(nc, [arrays], core_ids=[0])
    return r.results[0]["out_0"]
```

```python
from contextlib import ExitStack

import concourse.bass as bass
from concourse import mybir

F32 = mybir.dt.float32
F32R = mybir.dt.float32r
ALU = mybir.AluOpType
ACT = mybir.ActivationFunctionType
AX_X = mybir.AxisListType.X

P = 128
BANK = 512
NB = 32
G = 4
NG = NB // G
NK = 77
CD = 96
H = 16
DH = 64
INNER = H * DH
NC = INNER // P
HS = [(0, 6), (6, 12), (12, 16)]
EPS = 1e-5


def need(eng, sem, value):
    if isinstance(value, int) and value <= 0:
        return
    eng.wait_ge(sem, value)


def split3(pe, out, pairs, first=True, last=True, **kw):
    n = 0
    for a_hi, a_lo, b_hi, b_lo in pairs:
        for a, b in ((a_hi, b_hi), (a_hi, b_lo), (a_lo, b_hi)):
            n += 1
            ins = pe.matmul(out, a, b, start=first and n == 1, stop=last and n == 3 * len(pairs), **kw)
    return ins


def cap(value, most):
    return min(value, most) if isinstance(value, int) else value


class Step:

    def __init__(self, g, i):
        self.g, self.i, self.n = g, i, g * G + i

    def has(self, off):
        return not isinstance(self.n, int) or 0 <= self.n + off < NB


def run_steps(eng, step):
    for n in range(-3, G):
        step(Step(n // G, n % G))
    with eng.Fori(1, NG - 1) as g:
        for i in range(G):
            step(Step(g, i))
    for n in range(NB - G, NB + 1):
        step(Step(n // G, n % G))


class Chip:

    def __init__(self, nc, ctx):
        self.nc, self.ctx = nc, ctx
        self.x = self.sb("x_res", [P, NB * P])
        self.ident = self.sb("identity", [P, P])
        self.fused_hi = self.sb("fused_hi", [CD, H * P], F32R)
        self.fused_lo = self.sb("fused_lo", [CD, H * P], F32R)
        self.wv_hi = self.sb("wv_hi", [CD, INNER], F32R)
        self.wv_lo = self.sb("wv_lo", [CD, INNER], F32R)
        self.wo = self.sb("wo", [P, NC * P])
        self.bo = self.sb("bo", [P, P])
        self.w_hi = self.sb("w_hi", [P, 4096], F32R)
        self.w_lo = self.sb("w_lo", [P, 4096], F32R)
        self.ps = ctx.enter_context(nc.psum_tensor("banks", [P, 8 * BANK], F32))

    def sb(self, name, shape, dt=F32):
        return self.ctx.enter_context(self.nc.sbuf_tensor(name, shape, dt))

    def sem(self, name):
        return self.ctx.enter_context(self.nc.semaphore(name))

    def xt(self, n, k=1):
        return self.x[:, bass.ds(n * P, k * P)]

    def bank(self, b, rows, width, at=0):
        return self.ps[0:rows, b * BANK + at:b * BANK + at + width]


def prepare_xattn(nc, chip, L, a, sems, loads=()):
    pre = f"p{L}_"
    names = "w_loaded o_loaded wT_psum wT_act wT_dve f_psum f_hi f_lo v_hi v_lo".split()
    if not sems:
        sems.update({n: chip.sem("p_" + n) for n in names})
    w_loaded, o_loaded, wT_psum, wT_act, wT_dve, f_psum, f_hi, f_lo, v_hi, v_lo = (sems[n] for n in names)
    base = {n: k * L for n, k in (("w_loaded", 64), ("o_loaded", 48), ("wT_psum", 4), ("wT", 2), ("f", 4), ("v", 1))}
    with ExitStack() as own:
        def sb(name, shape, dt=F32):
            return own.enter_context(nc.sbuf_tensor(pre + name, shape, dt))

        wq = sb("wq", [P, INNER])
        wk = sb("wk", [CD, INNER])
        wv = sb("wv", [CD, INNER])
        wqT = sb("wqT", [P, NC * P])
        wkT = sb("wkT", [P, NC * CD])
        block = own.enter_context(nc.Block())

        def heads(t, q):
            return t[:].rearrange("c (m r d) -> c r m d", r=2, d=P)[:, q // 2, 4 * (q % 2):4 * (q % 2) + 4]

        @block.sync
        def _(sp):
            if L == 0:
                sp.dma_start(chip.ident[:], a["ident"]).then_inc(w_loaded, 16)
            sp.dma_start(wq[:], a["Wq"]).then_inc(w_loaded, 16)
            sp.dma_start(wk[:], a["Wk"]).then_inc(w_loaded, 16)
            sp.dma_start(wv[:], a["Wv"]).then_inc(w_loaded, 16)
            sp.dma_start(chip.wo[:].rearrange("p (c d) -> p c d", c=NC),
                         a["Wo"].rearrange("(c p) d -> p c d", p=P)).then_inc(o_loaded, 16)
            sp.dma_start(chip.bo[:], a["bo"].rearrange("(o d) -> o d", o=1).broadcast_to([P, P])).then_inc(o_loaded, 16)
            for dst, src in loads:
                sp.dma_start(dst, src).then_inc(o_loaded, 16)
            sp.wait_ge(o_loaded, base["o_loaded"] + 16 * (2 + len(loads)))

        @block.tensor
        def _(pe):
            pe.wait_ge(w_loaded, base["w_loaded"] + 16 * (4 if L == 0 else 3))
            for w, rows, at in ((wq, P, 0), (wk, CD, 2)):
                for c in range(NC):
                    t = nc.tensor.transpose(chip.bank(at + c // 4, P, rows, (c % 4) * rows),
                                            w[:, c * P:(c + 1) * P], chip.ident[0:rows, 0:rows])
                    if c % 4 == 3:
                        t.then_inc(wT_psum, 1)
            pe.wait_ge(wT_act, base["wT"] + 2)
            pe.wait_ge(wT_dve, base["wT"] + 2)
            for odd in range(2):
                for m in range(NC):
                    r = slice(DH * odd, DH * (odd + 1))
                    f = nc.tensor.matmul(chip.bank(4 + 2 * odd + m // 4, CD, P, (m % 4) * P),
                                         wkT[r, m * CD:(m + 1) * CD], wqT[r, m * P:(m + 1) * P], start=True, stop=True)
                    if m % 4 == 3:
                        f.then_inc(f_psum, 1)

        @block.scalar
        def _(act):
            for q in range(2):
                act.wait_ge(wT_psum, base["wT_psum"] + q + 1)
                nc.scalar.copy(wqT[:, q * BANK:(q + 1) * BANK], chip.bank(q, P, BANK)).then_inc(wT_act, 1)
            nc.scalar.copy(chip.wv_hi[:], wv[:]).then_inc(v_hi, 1)
            for q in range(4):
                act.wait_ge(f_psum, base["f"] + q + 1)
                nc.scalar.copy(heads(chip.fused_hi, q), chip.bank(4 + q, CD, BANK).rearrange("c (m d) -> c m d", m=4)).then_inc(f_hi, 1)

        @block.vector
        def _(dve):
            for q in range(2):
                dve.wait_ge(wT_psum, base["wT_psum"] + q + 3)
                nc.vector.tensor_copy(wkT[:, q * 4 * CD:(q + 1) * 4 * CD], chip.bank(2 + q, P, 4 * CD)).then_inc(wT_dve, 1)
            dve.wait_ge(v_hi, base["v"] + 1)
            nc.vector.tensor_tensor(chip.wv_lo[:], wv[:], chip.wv_hi[:].bitcast(F32), ALU.subtract).then_inc(v_lo, 1)
            for q in range(4):
                dve.wait_ge(f_hi, base["f"] + q + 1)
                nc.vector.tensor_tensor(heads(chip.fused_lo, q), chip.bank(4 + q, CD, BANK).rearrange("c (m d) -> c m d", m=4),
                                        heads(chip.fused_hi, q).bitcast(F32), ALU.subtract).then_inc(f_lo, 1)


def xattn_stage(nc, chip, L, context, sems):
    pre = f"x{L}_"
    names = ("ctx_loaded bn_done stats_done eps_done rstd_done xn_done xnT_psum xnT_hi xnT_lo bo_added "
             "ctxT_psum ctxT_hi ctxT_lo kp_psum kp_hi kp_lo sim_done max_done sub_done exp_done sum_done recip_done "
             "norm_done v_psum v_sb t_psum t_sb pv_psum oT_sb wo_psum x_upd half").split()
    if not sems:
        sems.update({n: chip.sem("x_" + n) for n in names})
    (ctx_loaded, bn_done, stats_done, eps_done, rstd_done, xn_done, xnT_psum, xnT_hi, xnT_lo, bo_added,
     ctxT_psum, ctxT_hi, ctxT_lo, kp_psum, kp_hi, kp_lo, sim_done, max_done, sub_done, exp_done, sum_done, recip_done,
     norm_done, v_psum, v_sb, t_psum, t_sb, pv_psum, oT_sb, wo_psum, x_upd, half_set) = (sems[n] for n in names)
    KW = G * NK
    with ExitStack() as own:
        def sb(name, shape, dt=F32):
            return own.enter_context(nc.sbuf_tensor(pre + name, shape, dt))

        ctx_raw = sb("ctx_raw", [NK, G, CD])
        ctxT_h = sb("ctxT_h", [CD, KW], F32R)
        ctxT_l = sb("ctxT_l", [CD, KW], F32R)
        kp_h = sb("kp_h", [P, G, H * NK], F32R)
        kp_l = sb("kp_l", [P, G, H * NK], F32R)
        bn = sb("bn", [P, 2, 6])
        mv = sb("mv", [P, 4, 2])
        rstd = sb("rstd", [P, 4])
        var_eps = sb("var_eps", [P, 4])
        minus_half = sb("minus_half", [P, 1])
        eps = sb("eps", [P, 1])
        xn = sb("xn", [P, 2, P])
        xnT_h = sb("xnT_h", [P, 2, P], F32R)
        xnT_l = sb("xnT_l", [P, 2, P], F32R)
        prob = sb("prob", [P, 2, H, NK])
        mx = sb("mx", [P, 2, H])
        rs = sb("rs", [P, 2, H])
        ri = sb("ri", [P, 2, H])
        v = sb("v", [NK, 2, INNER])
        pT = sb("pT", [NK, H, P])
        oT = sb("oT", [P, NC, P])
        SIM, MISC = 0, 7
        V_BANK, T_BANK, PV_BANK = (3, 4), (5, 6, 3, 4), (5, 6)
        KP_BANK = (3, 5, 0)
        CTX_AT, WO_AT = P, BANK - P

        def sim_ps(part):
            if part == 0:
                return chip.ps[:, 0:2 * BANK].rearrange("p (b c) -> p b c", b=2)[:, :, 0:6 * NK].rearrange(
                    "p b (h k) -> p b h k", h=6)
            return chip.bank(2, P, 4 * NK).rearrange("p (h k) -> p h k", h=4)

        def pair_ps(p):
            at = KP_BANK[p % 3] * BANK
            return chip.ps[:, at:at + 2 * BANK].rearrange("p (h c) -> p h c", h=2)[:, :, 0:KW].rearrange(
                "p h (b k) -> p h b k", b=G)

        def pair_sb(t, p):
            return t[:, :, 2 * p * NK:2 * (p + 1) * NK].rearrange("p b (h k) -> p h b k", h=2)

        def part_of(t, par, part):
            if part == 0:
                return t[:, par, 0:12].rearrange("p (b h) k -> p b h k", b=2) if len(t.shape) == 4 else \
                    t[:, par, 0:12].rearrange("p (b h) -> p b h", b=2)
            return t[:, par, 12:16]

        block = own.enter_context(nc.Block())

        @block.sync
        def _(sp):
            sp.dma_start(ctx_raw[:], context[0:G].rearrange("b k d -> k b d")).then_inc(ctx_loaded, 16)
            with sp.Fori(1, NG) as g:
                sp.wait_ge(ctxT_psum, g + NG * L)
                sp.dma_start(ctx_raw[:], context[bass.ds(g * G, G)].rearrange("b k d -> k b d")).then_inc(ctx_loaded, 16)

        @block.gpsimd
        def _(pool):
            nc.gpsimd.memset(minus_half[:], -0.5).then_inc(half_set, 1)
            nc.gpsimd.memset(eps[:], EPS).then_inc(half_set, 1)
            pool.wait_ge(half_set, 2 * L + 2)

            def step(s):
                n, i = s.n, s.i
                m = n + NB * L
                if s.has(2):
                    pool.wait_ge(xn_done, m + 3)
                    xb = chip.xt(n + 2)
                    nc.gpsimd.tensor_tensor(xb, xb, chip.bo[:], ALU.add).then_inc(bo_added, 1)
                if s.has(3):
                    b = (i + 3) % 4
                    pool.wait_ge(stats_done, m + 4)
                    need(pool, xn_done, m)
                    nc.gpsimd.tensor_tensor(var_eps[:, b:b + 1], mv[:, b, 1:2], eps[:], ALU.add).then_inc(eps_done, 1)
                    pool.wait_ge(eps_done, m + 4)
                    nc.gpsimd.tensor_tensor(rstd[:, b:b + 1], var_eps[:, b:b + 1], minus_half[:], ALU.pow).then_inc(rstd_done, 1)
                if s.has(1):
                    b = (i + 1) % 2
                    pool.wait_ge(recip_done, m + 2)
                    for q in range(4):
                        hq = slice(4 * q, 4 * q + 4)
                        nc.gpsimd.tensor_tensor(prob[:, b, hq], prob[:, b, hq],
                                                ri[:, b, hq].unsqueeze(2).broadcast_to([P, 4, NK]),
                                                ALU.mult).then_inc(norm_done, 1)
            run_steps(pool, step)

        @block.tensor
        def _(pe):
            def step(s):
                n, g, i = s.n, s.g, s.i
                m, gm = n + NB * L, g + NG * L
                b1 = (i + 1) % 2

                def weights(j):
                    if j < 2:
                        need(pe, oT_sb, 2 * m - 1 + j)
                    else:
                        pe.wait_ge(v_sb, cap(2 * m + 1 + j, 2 * NB * (L + 1)))
                    pe.wait_ge(norm_done, 4 * m + j + 1)
                    for h in range(4 * j, 4 * j + 4):
                        last = nc.tensor.transpose(chip.bank(T_BANK[j], NK, P, (h % 4) * P), prob[:, i % 2, h], chip.ident[:])
                    last.then_inc(t_psum, 1)

                def outputs(j):
                    pe.wait_ge(v_sb, 2 * m + 2)
                    pe.wait_ge(t_sb, 4 * m + 2 * j + 2)
                    for r in range(4):
                        for half in range(2):
                            h = 8 * j + 2 * r + half
                            at = PV_BANK[j] * BANK + r * P
                            last = nc.tensor.matmul(chip.ps[DH * half:DH * (half + 1), at:at + P],
                                                    v[:, i % 2, h * DH:(h + 1) * DH], pT[:, h], start=True, stop=True)
                    last.then_inc(pv_psum, 1)

                def scores():
                    pe.wait_ge(xnT_hi, m + 2)
                    pe.wait_ge(xnT_lo, m + 2)
                    need(pe, sub_done, 2 * m + 2)
                    if i == 3:
                        pe.wait_ge(kp_lo, 8 * gm + 16)
                    for q, (h0, h1) in enumerate(HS):
                        c = slice(h0 * NK, h1 * NK)
                        last = split3(nc.tensor, chip.bank(SIM + q, P, (h1 - h0) * NK),
                                      [(xnT_h[:, b1], xnT_l[:, b1], kp_h[:, (i + 1) % G, c], kp_l[:, (i + 1) % G, c])])
                    last.then_inc(sim_done, 1)

                def projection():
                    pe.wait_ge(oT_sb, 2 * m)
                    pe.wait_ge(xnT_lo, cap(m + 2, NB * (L + 1)))
                    if i == 3 and s.has(1):
                        pe.wait_ge(ctxT_lo, gm + 2)
                    for c in range(NC):
                        last = nc.tensor.matmul(chip.bank(MISC, P, P, WO_AT), oT[:, c], chip.wo[:, c * P:(c + 1) * P],
                                                start=c == 0, stop=c == NC - 1)
                    last.then_inc(wo_psum, 1)

                if i == 3 and s.has(1):
                    pe.wait_ge(ctxT_hi, gm + 2)
                    pe.wait_ge(ctxT_lo, gm + 2)
                    for p in range(H // 2):
                        if p >= 3:
                            pe.wait_ge(kp_lo, 8 * gm + 8 + p - 2)
                        elif p == 1:
                            need(pe, oT_sb, 2 * m)
                        elif p == 2:
                            need(pe, sub_done, 2 * m + 2)
                        for h in (2 * p, 2 * p + 1):
                            hs = slice(h * P, (h + 1) * P)
                            last = split3(nc.tensor, chip.bank(KP_BANK[p % 3] + h % 2, P, KW),
                                          [(chip.fused_hi[:, hs], chip.fused_lo[:, hs], ctxT_h[:], ctxT_l[:])])
                        last.then_inc(kp_psum, 1)
                if s.has(1) and i != 3:
                    scores()
                if s.has(-1):
                    projection()
                if s.has(1) and i == 3:
                    scores()
                if s.has(1):
                    cs = slice(((i + 1) % G) * NK, ((i + 1) % G + 1) * NK)
                    need(pe, t_sb, 4 * m)
                    for q in range(2):
                        c = slice(q * BANK, (q + 1) * BANK)
                        split3(nc.tensor, chip.bank(V_BANK[q], NK, BANK),
                               [(ctxT_h[:, cs], ctxT_l[:, cs], chip.wv_hi[:, c], chip.wv_lo[:, c])]).then_inc(v_psum, 1)
                if s.has(0):
                    for j in range(4):
                        weights(j)
                if s.has(2):
                    pe.wait_ge(xn_done, m + 3)
                    need(pe, x_upd, m)
                    nc.tensor.transpose(chip.bank(MISC, P, P), xn[:, i % 2], chip.ident[:]).then_inc(xnT_psum, 1)
                if s.has(0):
                    outputs(0)
                if i == 2 and s.has(2):
                    pe.wait_ge(ctx_loaded, 16 * gm + 32)
                    pe.wait_ge(xnT_lo, m + 3)
                    for b in range(G):
                        last = nc.tensor.transpose(chip.bank(MISC, CD, NK, CTX_AT + b * NK), ctx_raw[:, b],
                                                   chip.ident[0:NK, 0:NK])
                    last.then_inc(ctxT_psum, 1)
                if s.has(0):
                    outputs(1)
            run_steps(pe, step)

        @block.scalar
        def _(act):
            def step(s):
                n, g, i = s.n, s.g, s.i
                m, gm = n + NB * L, g + NG * L
                b1 = (i + 1) % 2

                def exps(part):
                    act.wait_ge(sub_done, 2 * m + 3 + part)
                    hp = slice(0, 12) if part == 0 else slice(12, 16)
                    nc.scalar.activation(prob[:, b1, hp], prob[:, b1, hp], ACT.Exp, scale=DH ** -0.5).then_inc(exp_done, 1)

                def weights(j):
                    act.wait_ge(t_psum, 4 * m + j + 1)
                    nc.scalar.copy(pT[:, 4 * j:4 * j + 4], chip.bank(T_BANK[j], NK, BANK)).then_inc(t_sb, 1)

                if i == 3 and s.has(1):
                    for p in range(H // 2):
                        act.wait_ge(kp_psum, 8 * gm + 9 + p)
                        nc.scalar.copy(pair_sb(kp_h, p), pair_ps(p)).then_inc(kp_hi, 1)
                if s.has(1):
                    for q in range(2):
                        act.wait_ge(v_psum, 2 * m + 3 + q)
                        nc.scalar.copy(v[:, b1, q * BANK:(q + 1) * BANK], chip.bank(V_BANK[q], NK, BANK)).then_inc(v_sb, 1)
                if s.has(0):
                    weights(0)
                    weights(1)
                    weights(2)
                    weights(3)
                if s.has(2):
                    act.wait_ge(xnT_psum, m + 3)
                    nc.scalar.copy(xnT_h[:, i % 2], chip.bank(MISC, P, P)).then_inc(xnT_hi, 1)
                if s.has(1):
                    exps(0)
                    exps(1)
                if i == 2 and s.has(2):
                    act.wait_ge(ctxT_psum, gm + 2)
                    nc.scalar.copy(ctxT_h[:], chip.bank(MISC, CD, KW, CTX_AT)).then_inc(ctxT_hi, 1)
            run_steps(act, step)

        @block.vector
        def _(dve):
            def step(s):
                n, g, i = s.n, s.g, s.i
                m, gm = n + NB * L, g + NG * L
                b1 = (i + 1) % 2

                def sums(off):
                    b = (i + off) % 2
                    dve.wait_ge(exp_done, 2 * (m + off) + 2)
                    nc.vector.tensor_reduce(rs[:, b], prob[:, b], AX_X, ALU.add).then_inc(sum_done, 1)
                    dve.wait_ge(sum_done, m + off + 1)
                    nc.vector.reciprocal(ri[:, b], rs[:, b]).then_inc(recip_done, 1)

                def outputs(j):
                    dve.wait_ge(pv_psum, 2 * m + j + 1)
                    nc.vector.tensor_copy(oT[:, 4 * j:4 * j + 4], chip.bank(PV_BANK[j], P, BANK)).then_inc(oT_sb, 1)

                if i == 3 and s.has(1):
                    for p in range(H // 2):
                        dve.wait_ge(kp_hi, 8 * gm + 9 + p)
                        nc.vector.tensor_tensor(pair_sb(kp_l, p), pair_ps(p), pair_sb(kp_h, p).bitcast(F32),
                                                ALU.subtract).then_inc(kp_lo, 1)
                    if s.has(0):
                        sums(0)
                if s.has(2):
                    b = (i + 2) % 4
                    dve.wait_ge(rstd_done, m + 3)
                    need(dve, xnT_psum, m + 1)
                    nc.vector.tensor_scalar(xn[:, i % 2], chip.xt(n + 2), mv[:, b, 0:1], rstd[:, b:b + 1],
                                            ALU.subtract, ALU.mult).then_inc(xn_done, 1)
                if s.has(1):
                    dve.wait_ge(sim_done, m + 2)
                    need(dve, t_psum, 4 * m)
                    for part in range(2):
                        nc.vector.tensor_reduce(part_of(mx, b1, part), sim_ps(part), AX_X, ALU.max).then_inc(max_done, 1)
                if s.has(3):
                    nc.vector.bn_stats(bn[:, b1], chip.xt(n + 3)).then_inc(bn_done, 1)
                    dve.wait_ge(bn_done, m + 4)
                if s.has(-1):
                    dve.wait_ge(wo_psum, m)
                    dve.wait_ge(bo_added, m)
                    xb = chip.xt(n - 1)
                    nc.vector.tensor_tensor(xb, xb, chip.bank(MISC, P, P, WO_AT), ALU.add).then_inc(x_upd, 1)
                if s.has(1):
                    for part in range(2):
                        sp_ = sim_ps(part)
                        dve.wait_ge(max_done, 2 * m + 3 + part)
                        nc.vector.tensor_tensor(part_of(prob, b1, part), sp_,
                                                part_of(mx, b1, part).unsqueeze(len(sp_.shape) - 1).broadcast_to(list(sp_.shape)),
                                                ALU.subtract).then_inc(sub_done, 1)
                if s.has(3):
                    nc.vector.bn_aggr(mv[:, (i + 3) % 4], bn[:, b1]).then_inc(stats_done, 1)
                if s.has(2):
                    dve.wait_ge(xnT_hi, m + 3)
                    nc.vector.tensor_tensor(xnT_l[:, i % 2], chip.bank(MISC, P, P), xnT_h[:, i % 2].bitcast(F32),
                                            ALU.subtract).then_inc(xnT_lo, 1)
                if s.has(0):
                    outputs(0)
                if i == 2 and s.has(2):
                    dve.wait_ge(ctxT_hi, gm + 2)
                    nc.vector.tensor_tensor(ctxT_l[:], chip.bank(MISC, CD, KW, CTX_AT), ctxT_h[:].bitcast(F32),
                                            ALU.subtract).then_inc(ctxT_lo, 1)
                if s.has(0):
                    outputs(1)
                if s.has(1) and not (i == 2 and s.has(2)):
                    sums(1)
            run_steps(dve, step)



NE = 16
FI = 64
TOP = 4
NGRP = 4
CR = NE * FI // P
CS = 2
CF = CR + CS
ROUTED_SCALE = 2.5
GP = G * P


class GroupStep:

    def __init__(self, g):
        self.g = g

    def has(self, off):
        return not isinstance(self.g, int) or 0 <= self.g + off < NG


def run_groups(eng, step, ahead=1):
    step(GroupStep(-1))
    step(GroupStep(0))
    with eng.Fori(1, NG - ahead) as g:
        step(GroupStep(g))
    for g in range(NG - ahead, NG + 1):
        step(GroupStep(g))


class Chain:

    def __init__(self, eng, sem, per_group):
        self.eng, self.sem, self.per = eng, sem, per_group

    def begin(self, g, done=0):
        self.base, self.n = self.per * g, done

    def link(self, ins):
        self.n += 1
        ins.then_inc(self.sem, 1)
        self.eng.wait_ge(self.sem, self.base + self.n)

    def end(self):
        assert self.n == self.per, self.n


def prepare_moe0(nc, chip, a, keep):
    up_loaded, dn_loaded, wt_psum, wt_hi, wt_lo, small, gate_sb = (
        chip.sem("m0_" + n) for n in "up_loaded dn_loaded wt_psum wt_hi wt_lo small gate_sb".split())
    with ExitStack() as own:
        def sb(name, shape, dt=F32):
            return own.enter_context(nc.sbuf_tensor("m0_" + name, shape, dt))

        up = sb("up", [P, CF, P])
        dn = sb("dn", [P, CF, P])
        gw = sb("gw", [NE, P])
        sel = sb("sel", [NE, CR * P])
        block = own.enter_context(nc.Block())
        NQ = 2 * CF // 4

        @block.sync
        def _(sp):
            sp.dma_start(up[:, 0:CR], a["up_w"].rearrange("(c e) f d -> (e f) c d", e=2)).then_inc(up_loaded, 16)
            sp.dma_start(up[:, CR:CF], a["shared_up"].rearrange("(c f) d -> f c d", f=P)).then_inc(up_loaded, 16)
            sp.dma_start(gw[:], a["gate_w"]).then_inc(up_loaded, 16)
            sp.dma_start(dn[:, 0:CR].rearrange("d c (e f) -> d (c e) f", e=2),
                         a["down_w"].rearrange("e d f -> d e f")).then_inc(dn_loaded, 16)
            sp.dma_start(dn[:, CR:CF].rearrange("d c f -> d (c f)"), a["shared_down"]).then_inc(dn_loaded, 16)
            sp.dma_start(sel[:], a["pairs"]).then_inc(small, 16)
            sp.dma_start(keep["bias"][:], a["bias_e"].rearrange("(o d) -> o d", o=1).broadcast_to([P, NE])).then_inc(small, 16)
            sp.dma_start(keep["before"][:], a["before"].rearrange("(o d) -> o d", o=1).broadcast_to([P, 2 * NGRP * NGRP])).then_inc(small, 16)
            sp.wait_ge(small, 48)

        @block.tensor
        def _(pe):
            pe.wait_ge(up_loaded, 48)
            for c in range(2 * CF):
                if c == CF:
                    pe.wait_ge(dn_loaded, 32)
                src = up[:, c] if c < CF else dn[:, c - CF]
                t = nc.tensor.transpose(chip.bank(c // 4, P, P, (c % 4) * P), src, chip.ident[:])
                if c % 4 == 3:
                    t.then_inc(wt_psum, 1)
            nc.tensor.transpose(chip.bank(7, P, NE), gw[:], chip.ident[0:NE, 0:NE]).then_inc(wt_psum, 1)

        @block.scalar
        def _(act):
            for q in range(NQ):
                act.wait_ge(wt_psum, q + 1)
                nc.scalar.copy(chip.w_hi[:, q * BANK:(q + 1) * BANK], chip.bank(q, P, BANK)).then_inc(wt_hi, 1)
            act.wait_ge(wt_psum, NQ + 1)
            nc.scalar.copy(keep["gate"][:], chip.bank(7, P, NE)).then_inc(gate_sb, 1)

        @block.vector
        def _(dve):
            for q in range(NQ):
                dve.wait_ge(wt_hi, q + 1)
                c = slice(q * BANK, (q + 1) * BANK)
                nc.vector.tensor_tensor(chip.w_lo[:, c], chip.bank(q, P, BANK), chip.w_hi[:, c].bitcast(F32),
                                        ALU.subtract).then_inc(wt_lo, 1)
            dve.wait_ge(small, 48)
            nc.vector.tensor_copy(keep["pairs"][:], sel[:]).then_inc(wt_lo, 1)


def moe0_stage(nc, chip, a):
    names = ("bn_done stats_done xc_done eps_done rstd_done xn_done xnT_psum xT_sb xT_hi xT_lo logit_psum act_sc router cw_done "
             "cwT_psum cwT_hi cwT_lo up_psum bc_psum relu_done sq_done h_done h_hi h_lo down_done yT_sb yo_psum "
             "x_upd half scan_zero").split()
    (bn_done, stats_done, xc_done, eps_done, rstd_done, xn_done, xnT_psum, xT_sb, xT_hi, xT_lo, logit_psum, act_sc, router, cw_done,
     cwT_psum, cwT_hi, cwT_lo, up_psum, bc_psum, relu_done, sq_done, h_done, h_hi, h_lo, down_done, yT_sb, yo_psum,
     x_upd, half_set, scan_zero) = (chip.sem("f0_" + n) for n in names)
    RING, LAG = 5, 3
    U, B, Y, XT, YT, LG, CW = 0, 2, 4, 5, 6, 6, 7
    with ExitStack() as own:
        def sb(name, shape, dt=F32):
            return own.enter_context(nc.sbuf_tensor("f0_" + name, shape, dt))

        keep = {"gate": sb("gate", [P, NE]), "bias": sb("bias", [P, NE]), "pairs": sb("pairs", [NE, CR * P], F32R),
                "before": sb("before", [P, 2 * NGRP * NGRP])}
        prepare_moe0(nc, chip, a, keep)
        bn = sb("bn", [P, G, 6])
        mv = sb("mv", [P, G, 2])
        rstd = sb("rstd", [P, G])
        var_eps = sb("var_eps", [P, G])
        minus_half = sb("minus_half", [P, G])
        eps = sb("eps", [P, G])
        xn = sb("xn", [P, G, P])
        xT = sb("xT", [P, GP])
        xh = sb("xh", [P, 2 * GP], F32R)
        xl = sb("xl", [P, 2 * GP], F32R)
        th = sb("th", [P, G, NE])
        ex = sb("ex", [P, G, NE])
        cwT_h = sb("cwT_h", [NE, 2 * GP], F32R)
        cwT_l = sb("cwT_l", [NE, 2 * GP], F32R)
        r = sb("r", [P, RING, GP])
        sq = sb("sq", [P, RING, GP])
        h = sb("h", [P, RING, GP])
        hh = sb("hh", [P, RING, GP], F32R)
        hl = sb("hl", [P, RING, GP], F32R)
        yT = sb("yT", [P, GP])
        sc = sb("sc", [P, G, NE])
        sig = sb("sig", [P, G, NE])
        pair_max = sb("pair_max", [P, G * NGRP, 2])
        pair_min = sb("pair_min", [P, G * NGRP, 2])
        best = sb("best", [P, G * NGRP])
        second = sb("second", [P, G * NGRP])
        other = sb("other", [P, G * NGRP])
        gs = sb("gs", [P, G, NGRP])
        ge = sb("ge", [P, G, NGRP, NGRP])
        gt4 = sb("gt4", [P, G, NGRP, NGRP])
        rank = sb("rank", [P, G, NGRP])
        masked = sb("masked", [P, G, NE])
        top8 = sb("top8", [P, G, 8])
        over = sb("over", [P, G, NE])
        n_over = sb("n_over", [P, G])
        PAD = 8
        scan = sb("scan", [P, 2, G, PAD + NE])
        same = sb("same", [P, G, NE])
        w_sum = sb("w_sum", [P, G])
        w_inv = sb("w_inv", [P, G])
        cw = sb("cw", [P, G, NE])
        gate, bias, pairs, before = keep["gate"], keep["bias"], keep["pairs"], keep["before"]
        block = own.enter_context(nc.Block())

        def chunk(s, c, late):
            return (s.has(0) if c >= late else s.has(-1)), (c - late) % CF, CF * s.g + c - late + 1

        def first(s):
            return isinstance(s.g, int) and s.g == -1

        @block.gpsimd
        def _(pool):
            nc.gpsimd.memset(minus_half[:], -0.5).then_inc(half_set, 1)
            nc.gpsimd.memset(eps[:], EPS).then_inc(half_set, 1)
            pool.wait_ge(half_set, 2)

            def centred(g, off):
                pool.wait_ge(stats_done, G * (g + off + 1))
                need(pool, xnT_psum, g + off)
                xg = chip.xt(G * (g + off), G).rearrange("p (b d) -> p b d", b=G)
                nc.gpsimd.tensor_tensor(xn[:], xg, mv[:, :, 0:1].broadcast_to([P, G, P]), ALU.subtract).then_inc(xc_done, 1)

            def rstds(g, off):
                nc.gpsimd.tensor_tensor(var_eps[:], mv[:, :, 1], eps[:], ALU.add).then_inc(eps_done, 1)
                pool.wait_ge(eps_done, g + off + 1)
                nc.gpsimd.tensor_tensor(rstd[:], var_eps[:], minus_half[:], ALU.pow).then_inc(rstd_done, 1)

            def normalised(g, off):
                pool.wait_ge(rstd_done, g + off + 1)
                pool.wait_ge(xc_done, g + off + 1)
                nc.gpsimd.tensor_tensor(xn[:], xn[:], rstd[:].unsqueeze(2).broadcast_to([P, G, P]), ALU.mult).then_inc(xn_done, 1)

            def step(s):
                g = s.g
                if first(s):
                    centred(g, 1)
                    rstds(g, 1)
                    normalised(g, 1)
                for c in range(CF):
                    ok, cc, t = chunk(s, c, 1)
                    if ok:
                        b = cc % RING
                        pool.wait_ge(h_hi, t)
                        need(pool, down_done, t - RING)
                        nc.gpsimd.tensor_tensor(hl[:, b], h[:, b], hh[:, b].bitcast(F32), ALU.subtract).then_inc(h_lo, 1)
                    if s.has(2):
                        if c == 2:
                            centred(g, 2)
                        if c == 3:
                            rstds(g, 2)
                        if c == 4:
                            normalised(g, 2)
            run_groups(pool, step, ahead=2)

        @block.tensor
        def _(pe):
            def step(s):
                g = s.g
                at = (g % 2) * GP if s.has(0) else 0

                def up(c, t):
                    if c == 0:
                        pe.wait_ge(xT_hi, g + 1)
                        pe.wait_ge(xT_lo, g + 1)
                    need(pe, relu_done, t - 2)
                    ws = slice(c * P, (c + 1) * P)
                    split3(nc.tensor, chip.bank(U + c % 2, P, GP), [(chip.w_hi[:, ws], chip.w_lo[:, ws], xh[:, bass.ds(at, GP)],
                                                                     xl[:, bass.ds(at, GP)])]).then_inc(up_psum, 1)

                def weights(c):
                    sel, bank = pairs[:, c * P:(c + 1) * P], chip.bank(B + c % 2, P, GP)
                    nc.tensor.matmul(bank, sel, cwT_h[:, bass.ds(at, GP)], start=True, stop=False)
                    nc.tensor.matmul(bank, sel, cwT_l[:, bass.ds(at, GP)], start=False, stop=True).then_inc(bc_psum, 1)

                def down(cc, t):
                    b = cc % RING
                    pe.wait_ge(h_hi, t)
                    pe.wait_ge(h_lo, t)
                    if cc == 0:
                        need(pe, yT_sb, g)
                    ws = slice((CF + cc) * P, (CF + cc + 1) * P)
                    last = split3(nc.tensor, chip.bank(Y, P, GP), [(chip.w_hi[:, ws], chip.w_lo[:, ws], hh[:, b], hl[:, b])],
                                  first=cc == 0, last=cc == CF - 1)
                    last.then_inc(down_done, 1)

                def transposes(off):
                    pe.wait_ge(xn_done, g + off + 1)
                    need(pe, xT_sb, g + off)
                    for b in range(G):
                        last = nc.tensor.transpose(chip.bank(XT, P, P, b * P), xn[:, b], chip.ident[:])
                    last.then_inc(xnT_psum, 1)

                def logits(off):
                    pe.wait_ge(xT_sb, g + off + 1)
                    need(pe, x_upd, g)
                    need(pe, act_sc, 2 * (g + off))
                    for b in range(G):
                        last = nc.tensor.matmul(chip.bank(LG, P, NE, b * NE), xT[:, b * P:(b + 1) * P], gate[:], start=True, stop=True)
                    last.then_inc(logit_psum, 1)

                if first(s):
                    transposes(1)
                    logits(1)
                for c in range(CF):
                    now, _, t = chunk(s, c, 0)
                    late, cc, td = chunk(s, c, LAG)
                    if now and c == 1:
                        pe.wait_ge(cwT_hi, g + 1)
                        pe.wait_ge(cwT_lo, g + 1)
                    if now and 0 < c < CR:
                        need(pe, h_done, CR * g + c - 1)
                    if now:
                        up(c, t)
                    if now and c == 1:
                        weights(0)
                    if now and 0 < c < CR:
                        weights(c)
                    if late:
                        down(cc, td)
                    if c == 6 and s.has(2):
                        transposes(2)
                    if c == 7 and s.has(2):
                        logits(2)
                    if c == 4 and s.has(-1):
                        pe.wait_ge(yT_sb, g)
                        pe.wait_ge(act_sc, 2 * cap(g + 1, NG))
                        for b in range(G):
                            last = nc.tensor.transpose(chip.bank(YT, P, P, b * P), yT[:, b * P:(b + 1) * P], chip.ident[:])
                        last.then_inc(yo_psum, 1)
                    if c == 8 and s.has(1):
                        pe.wait_ge(cw_done, g + 2)
                        need(pe, cwT_lo, g + 1)
                        for b in range(G):
                            last = nc.tensor.transpose(chip.bank(CW, NE, P, b * P), cw[:, b], chip.ident[:])
                        last.then_inc(cwT_psum, 1)
            run_groups(pe, step, ahead=2)

        @block.scalar
        def _(act):
            def xT_of(g, off):
                act.wait_ge(xnT_psum, g + off + 1)
                need(act, logit_psum, g + off)
                need(act, xT_lo, g + off)
                nc.scalar.copy(xT[:], chip.bank(XT, P, GP)).then_inc(xT_sb, 1)

            def sigmoids(g, off):
                act.wait_ge(logit_psum, g + off + 1)
                need(act, cw_done, g + off)
                lg = chip.bank(LG, P, G * NE).rearrange("p (b e) -> p b e", b=G)
                nc.scalar.activation(th[:], lg, ACT.Tanh, scale=0.5).then_inc(act_sc, 1)
                nc.scalar.activation(ex[:], lg, ACT.Exp, scale=-1.0).then_inc(act_sc, 1)

            def step(s):
                g = s.g
                nxt = ((g + 1) % 2) * GP
                if first(s):
                    xT_of(g, 1)
                    sigmoids(g, 1)
                for c in range(CF):
                    if c == LAG and s.has(-1):
                        act.wait_ge(down_done, CF * g)
                        nc.scalar.copy(yT[:], chip.bank(Y, P, GP)).then_inc(yT_sb, 1)
                    ok, cc, t = chunk(s, c, 0)
                    if ok:
                        b = cc % RING
                        act.wait_ge(up_psum, t)
                        nc.scalar.activation(r[:, b], chip.bank(U + c % 2, P, GP), ACT.Relu).then_inc(relu_done, 1)
                        act.wait_ge(relu_done, t)
                        if cc < CR:
                            need(act, h_done, CR * g + cc + 1 - RING)
                        else:
                            act.wait_ge(h_lo, t - RING)
                        nc.scalar.activation((sq if cc < CR else h)[:, b], r[:, b], ACT.Square).then_inc(sq_done, 1)
                    ok, cc, t = chunk(s, c, 1)
                    if ok:
                        b = cc % RING
                        if cc < CR:
                            act.wait_ge(h_done, CR * g + cc + 1)
                        else:
                            act.wait_ge(sq_done, t)
                        need(act, down_done, t - RING)
                        nc.scalar.copy(hh[:, b], h[:, b]).then_inc(h_hi, 1)
                    if c == 6 and s.has(2):
                        xT_of(g, 2)
                    if c == 8 and s.has(2):
                        sigmoids(g, 2)
                    if c == 8 and s.has(-1):
                        act.wait_ge(yo_psum, g)
                    if c == 8 and s.has(1):
                        act.wait_ge(cwT_psum, g + 2)
                        need(act, bc_psum, CR * g)
                        nc.scalar.copy(cwT_h[:, bass.ds(nxt, GP)], chip.bank(CW, NE, GP)).then_inc(cwT_hi, 1)
            run_groups(act, step, ahead=2)

        @block.vector
        def _(dve):
            for k in range(2):
                nc.vector.memset(scan[:, k], 0.0).then_inc(scan_zero, 1)
            dve.wait_ge(scan_zero, 2)
            chain = Chain(dve, router, 27)
            EARLY = 7
            V = nc.vector

            def over_experts(t):
                return t.unsqueeze(2).broadcast_to([P, G, NE])

            gi = gs[:].unsqueeze(3).broadcast_to([P, G, NGRP, NGRP])
            gj = gs[:].unsqueeze(2).broadcast_to([P, G, NGRP, NGRP])
            tie = before[:].rearrange("p (k i j) -> p k i j", k=2, i=NGRP)

            def router_scores(g, off):
                dve.wait_ge(act_sc, 2 * (g + off) + 2)
                V.tensor_scalar(ex[:], ex[:], 1.0, None, ALU.add)
                chain.link(V.tensor_scalar(sc[:], th[:], 0.5, 0.5, ALU.mult, ALU.add))
                chain.link(V.tensor_tensor(sc[:], sc[:], bias[:].unsqueeze(1).broadcast_to([P, G, NE]), ALU.add))
                s4 = sc[:].rearrange("p b (i e) -> p (b i) e", e=4)
                V.tensor_tensor(pair_max[:], s4[:, :, 0:2], s4[:, :, 2:4], ALU.max)
                chain.link(V.tensor_tensor(pair_min[:], s4[:, :, 0:2], s4[:, :, 2:4], ALU.min))

            def router_groups():
                V.tensor_tensor(best[:], pair_max[:, :, 0], pair_max[:, :, 1], ALU.max)
                V.tensor_tensor(second[:], pair_max[:, :, 0], pair_max[:, :, 1], ALU.min)
                chain.link(V.tensor_tensor(other[:], pair_min[:, :, 0], pair_min[:, :, 1], ALU.max))
                chain.link(V.tensor_tensor(second[:], second[:], other[:], ALU.max))
                chain.link(V.tensor_tensor(gs[:].rearrange("p b i -> p (b i)"), best[:], second[:], ALU.add))
                V.tensor_tensor(ge[:], gj, gi, ALU.is_ge)
                chain.link(V.tensor_tensor(gt4[:], gj, gi, ALU.is_gt))

            def router_choice():
                V.tensor_tensor(ge[:], ge[:], tie[:, 0].unsqueeze(1).broadcast_to([P, G, NGRP, NGRP]), ALU.mult)
                chain.link(V.tensor_tensor(gt4[:], gt4[:], tie[:, 1].unsqueeze(1).broadcast_to([P, G, NGRP, NGRP]), ALU.mult))
                chain.link(V.tensor_tensor(ge[:], ge[:], gt4[:], ALU.add))
                chain.link(V.tensor_reduce(rank[:], ge[:], AX_X, ALU.add))
                chain.link(V.tensor_scalar(rank[:], rank[:], 1.5, None, ALU.is_lt))
                chain.link(V.tensor_tensor(masked[:].rearrange("p b (i e) -> p b i e", e=4), sc[:].rearrange("p b (i e) -> p b i e", e=4),
                                           rank[:].unsqueeze(3).broadcast_to([P, G, NGRP, 4]), ALU.mult))

            def router_top():
                V.reciprocal(sig[:], ex[:])
                for b in range(G):
                    last = V.max(top8[:, b], masked[:, b])
                chain.link(last)
                fourth = over_experts(top8[:, :, TOP - 1])
                V.tensor_tensor(over[:], masked[:], fourth, ALU.is_gt)
                chain.link(V.tensor_tensor(scan[:, 0, :, PAD:], masked[:], fourth, ALU.is_equal))
                V.tensor_copy(same[:], scan[:, 0, :, PAD:])
                chain.link(V.tensor_reduce(n_over[:], over[:], AX_X, ALU.add))

            def router_ties():
                for k, d in enumerate((1, 2, 4, 8)):
                    src, dst = scan[:, k % 2], scan[:, 1 - k % 2]
                    chain.link(V.tensor_tensor(dst[:, :, PAD:], src[:, :, PAD:], src[:, :, PAD - d:PAD + NE - d], ALU.add))
                chain.link(V.tensor_tensor(masked[:], scan[:, 0, :, PAD:], over_experts(n_over[:]), ALU.add))
                chain.link(V.scalar_tensor_tensor(same[:], masked[:], TOP + 0.5, same[:], ALU.is_lt, ALU.mult))

            def router_weights():
                chain.link(V.tensor_tensor(over[:], over[:], same[:], ALU.add))
                chain.link(V.tensor_tensor(sig[:], sig[:], over[:], ALU.mult))
                chain.link(V.tensor_reduce(w_sum[:], sig[:], AX_X, ALU.add))
                chain.link(V.tensor_scalar(w_sum[:], w_sum[:], 1e-20, None, ALU.add))
                chain.link(V.reciprocal(w_inv[:], w_sum[:]))
                chain.link(V.tensor_tensor(sig[:], sig[:], over_experts(w_inv[:]), ALU.mult))

            def moments(g, off):
                for b in range(G):
                    V.bn_stats(bn[:, b], chip.xt(G * (g + off) + b)).then_inc(bn_done, 1)

            def stats():
                for b in range(G):
                    V.bn_aggr(mv[:, b], bn[:, b]).then_inc(stats_done, 1)

            def step(s):
                g = s.g
                nxt = ((g + 1) % 2) * GP
                if first(s):
                    moments(g, 1)
                    dve.wait_ge(bn_done, G * (g + 2))
                    stats()
                    chain.begin(g + 1)
                    router_scores(g, 1)
                    router_groups()
                for c in range(CF):
                    if c == 2 and s.has(2):
                        dve.wait_ge(bn_done, G * (g + 3))
                        dve.wait_ge(xn_done, g + 2)
                    ok, cc, t = chunk(s, c, 0)
                    if ok and cc < CR:
                        b = cc % RING
                        dve.wait_ge(bc_psum, CR * g + cc + 1)
                        dve.wait_ge(sq_done, t)
                        need(dve, h_lo, t - RING)
                        V.tensor_tensor(h[:, b], sq[:, b], chip.bank(B + c % 2, P, GP), ALU.mult).then_inc(h_done, 1)
                    if c == 1 and s.has(2):
                        moments(g, 2)
                    if c == 2 and s.has(2):
                        stats()
                    if c == 6 and s.has(-1):
                        dve.wait_ge(yo_psum, g)
                        xg = chip.xt(G * (g - 1), G)
                        V.tensor_tensor(xg, xg, chip.bank(YT, P, GP), ALU.add).then_inc(x_upd, 1)
                    if s.has(1):
                        if c == 0:
                            chain.begin(g + 1, EARLY)
                            router_choice()
                        if c == 2:
                            router_top()
                        if c == 3:
                            router_ties()
                        if c == 4:
                            dve.wait_ge(xT_sb, g + 2)
                            need(dve, up_psum, CF * g)
                            V.tensor_copy(xh[:, bass.ds(nxt, GP)], xT[:]).then_inc(xT_hi, 1)
                            dve.wait_ge(xT_hi, g + 2)
                            V.tensor_tensor(xl[:, bass.ds(nxt, GP)], xT[:], xh[:, bass.ds(nxt, GP)].bitcast(F32),
                                            ALU.subtract).then_inc(xT_lo, 1)
                        if c == 5:
                            router_weights()
                        if c == 6:
                            need(dve, cwT_psum, g + 1)
                            V.tensor_scalar(cw[:], sig[:], ROUTED_SCALE, None, ALU.mult).then_inc(cw_done, 1)
                            chain.end()
                    if c == 9 and s.has(2):
                        chain.begin(g + 2)
                        router_scores(g, 2)
                    if c == 9 and s.has(1):
                        dve.wait_ge(cwT_hi, g + 2)
                        V.tensor_tensor(cwT_l[:, bass.ds(nxt, GP)], chip.bank(CW, NE, GP), cwT_h[:, bass.ds(nxt, GP)].bitcast(F32),
                                        ALU.subtract).then_inc(cwT_lo, 1)
                    if c == 9 and s.has(2):
                        router_groups()
            run_groups(dve, step, ahead=2)



E1 = 8
D1 = 512
C1 = D1 // P
CI = E1 * C1


def prepare_moe1(nc, chip, a, w):
    big, small, t_psum, t_sb, hi_a, hi_b, lo = (chip.sem("m1_" + n) for n in "big small t_psum t_sb hi_a hi_b lo".split())
    big2 = chip.sem("m1_big2")
    with ExitStack() as own:
        def sb(name, shape, dt=F32):
            return own.enter_context(nc.sbuf_tensor("m1_" + name, shape, dt))

        w1 = sb("w1", [P, E1, D1])
        w2 = sb("w2", [P, CI, P])
        rows = sb("rows", [CI + 2, P])
        qk = sb("qk", [P, 2 * P])
        b2 = sb("b2", [E1, P])
        sel = sb("sel", [E1, E1 * P])
        block = own.enter_context(nc.Block())

        def row(name, n):
            return a[name].rearrange("(o d) -> o d", o=1).broadcast_to([n, a[name].shape[0]])

        @block.sync
        def _(sp):
            for dst, src in ((rows[0:CI], a["b1"].rearrange("e (c p) -> (e c) p", p=P)), (rows[CI:CI + 1], row("bq", 1)),
                             (rows[CI + 1:CI + 2], row("bk", 1)), (qk[:, 0:P], a["Wq"]), (qk[:, P:], a["Wk"]),
                             (w["wv"][:], a["Wv"]), (w["wo"][:], a["Wo"]), (w["wg"][:], a["Wg"]), (w["bv"][:], row("bv", P)),
                             (w["bo"][:], row("bo", P)), (w["bg"][:], row("bg", P)), (b2[:], a["b2"]), (sel[:], a["ones_rows"])):
                sp.dma_start(dst, src).then_inc(small, 16)
            sp.dma_start(w1[:], a["W1"].rearrange("e h d -> h e d")).then_inc(big, 16)
            sp.dma_start(w2[:], a["W2"].rearrange("e (c p) h -> p (e c) h", p=P)).then_inc(big2, 16)
            sp.wait_ge(small, 16 * 13)

        @block.tensor
        def _(pe):
            pe.wait_ge(small, 16 * 13)
            nc.tensor.transpose(chip.bank(0, P, CI + 2), rows[:], chip.ident[0:CI + 2, 0:CI + 2]).then_inc(t_psum, 1)

        @block.scalar
        def _(act):
            act.wait_ge(t_psum, 1)
            nc.scalar.copy(w["cols"][:], chip.bank(0, P, CI + 2)).then_inc(t_sb, 1)
            act.wait_ge(big, 16)
            nc.scalar.copy(chip.w_hi[:, 0:CI * P // 2], w1[:, 0:E1 // 2]).then_inc(hi_a, 1)
            nc.scalar.copy(chip.w_hi[:, CI * P // 2:], w1[:, E1 // 2:]).then_inc(hi_a, 1)
            act.wait_ge(big2, 16)
            nc.scalar.copy(w["w2h"][:, 0:CI // 2], w2[:, 0:CI // 2]).then_inc(hi_a, 1)
            nc.scalar.copy(w["w2h"][:, CI // 2:], w2[:, CI // 2:]).then_inc(hi_a, 1)

        @block.vector
        def _(dve):
            dve.wait_ge(small, 16 * 13)
            nc.vector.tensor_copy(w["qk_h"][:], qk[:]).then_inc(hi_b, 1)
            nc.vector.tensor_copy(w["b2h"][:], b2[:]).then_inc(hi_b, 1)
            nc.vector.tensor_copy(w["sel"][:], sel[:]).then_inc(hi_b, 1)
            dve.wait_ge(hi_b, 3)
            nc.vector.tensor_tensor(w["qk_l"][:], qk[:], w["qk_h"][:].bitcast(F32), ALU.subtract).then_inc(lo, 1)
            nc.vector.tensor_tensor(w["b2l"][:], b2[:], w["b2h"][:].bitcast(F32), ALU.subtract).then_inc(lo, 1)
            for k, (dst, src, hi) in enumerate((
                    (chip.w_lo[:, 0:CI * P // 2], w1[:, 0:E1 // 2].rearrange("p e d -> p (e d)"), chip.w_hi[:, 0:CI * P // 2]),
                    (chip.w_lo[:, CI * P // 2:], w1[:, E1 // 2:].rearrange("p e d -> p (e d)"), chip.w_hi[:, CI * P // 2:]),
                    (w["w2l"][:, 0:CI // 2], w2[:, 0:CI // 2], w["w2h"][:, 0:CI // 2]),
                    (w["w2l"][:, CI // 2:], w2[:, CI // 2:], w["w2h"][:, CI // 2:]))):
                dve.wait_ge(hi_a, k + 1)
                nc.vector.tensor_tensor(dst, src, hi.bitcast(F32), ALU.subtract).then_inc(lo, 1)


def ffn1_stage(nc, chip, a, out):
    names = ("bn_done stats_done eps_done rstd_done xn_done xnb_done xT_psum xT_sb xT_hi xT_lo q_psum k_psum v_psum qT_sb kT_sb v_sb "
             "s_psum s_max s_sub s_exp s_sum s_inv w_done wT_psum wT_sb aT_psum aT_sb o_psum x2_done res_done x2T_psum x2T_sb "
             "x2T_hi x2T_lo g_psum g_logit g_max g_sub g_exp g_sum g_inv gate_done gT_psum gT_hi gT_lo gb_psum gb_sb b2_psum acc_set "
             "up_psum relu_done hi_act hi_dve h_lo down_done scaled acc_done y_done yo_psum x_upd out_done half").split()
    S = {n: chip.sem("f1_" + n) for n in names}
    (bn_done, stats_done, eps_done, rstd_done, xn_done, xnb_done, xT_psum, xT_sb, xT_hi, xT_lo, q_psum, k_psum, v_psum, qT_sb,
     kT_sb, v_sb, s_psum, s_max, s_sub, s_exp, s_sum, s_inv, w_done, wT_psum, wT_sb, aT_psum, aT_sb, o_psum, x2_done, res_done,
     x2T_psum, x2T_sb, x2T_hi, x2T_lo, g_psum, g_logit, g_max, g_sub, g_exp, g_sum, g_inv, gate_done, gT_psum, gT_hi, gT_lo,
     gb_psum, gb_sb, b2_psum, acc_set, up_psum, relu_done, hi_act, hi_dve, h_lo, down_done, scaled, acc_done, y_done,
     yo_psum, x_upd, out_done, half_set) = (S[n] for n in names)
    RING, LAG = 4, 3
    END = C1 - 1 + LAG
    U, Y, GB, A, B, C = 0, 2, 4, 5, 6, 7
    with ExitStack() as own:
        def sb(name, shape, dt=F32):
            return own.enter_context(nc.sbuf_tensor("f1_" + name, shape, dt))

        w = {"wv": sb("wv", [P, P]), "wo": sb("wo", [P, P]), "wg": sb("wg", [P, E1]), "bv": sb("bv", [P, P]), "bo": sb("bo", [P, P]),
             "bg": sb("bg", [P, E1]), "cols": sb("cols", [P, CI + 2]), "qk_h": sb("qk_h", [P, 2 * P], F32R),
             "qk_l": sb("qk_l", [P, 2 * P], F32R), "b2h": sb("b2h", [E1, P], F32R), "b2l": sb("b2l", [E1, P], F32R),
             "sel": sb("sel", [E1, E1 * P], F32R), "w2h": sb("w2h", [P, CI, P], F32R), "w2l": sb("w2l", [P, CI, P], F32R)}
        prepare_moe1(nc, chip, a, w)
        bn = sb("bn", [P, G, 6])
        mv = sb("mv", [P, G, 2])
        rstd = sb("rstd", [P, G])
        var_eps = sb("var_eps", [P, G])
        minus_half = sb("minus_half", [P, G])
        eps = sb("eps", [P, G])
        xn = sb("xn", [P, G, P])
        xnb = sb("xnb", [P, G, P])
        xT = sb("xT", [P, GP])
        xTh = sb("xTh", [P, GP], F32R)
        xTl = sb("xTl", [P, GP], F32R)
        qT = sb("qT", [P, GP])
        kT = sb("kT", [P, GP])
        v = sb("v", [P, G, P])
        att = sb("att", [P, G, P])
        smax = sb("smax", [P, G])
        ssum = sb("ssum", [P, G])
        sinv = sb("sinv", [P, G])
        attT = sb("attT", [P, GP])
        aT = sb("aT", [P, GP])
        x2 = sb("x2", [P, G, P])
        x2T = sb("x2T", [P, GP])
        x2h = sb("x2h", [P, 2 * GP], F32R)
        x2l = sb("x2l", [P, 2 * GP], F32R)
        gates = sb("gates", [P, G, E1])
        gmax = sb("gmax", [P, G])
        gsum = sb("gsum", [P, G])
        ginv = sb("ginv", [P, G])
        gTh = sb("gTh", [E1, 2 * GP], F32R)
        gTl = sb("gTl", [E1, 2 * GP], F32R)
        gb = sb("gb", [P, 2, GP])
        h = sb("h", [P, RING, GP])
        hh = sb("hh", [P, RING, GP], F32R)
        hl = sb("hl", [P, RING, GP], F32R)
        part = sb("part", [P, 2, GP])
        acc = sb("acc", [P, GP])
        yT = sb("yT", [P, GP])
        block = own.enter_context(nc.Block())

        def item(s, u, late):
            return (s.has(0) if u >= late else s.has(-1)), (u - late) % CI, CI * s.g + u - late + 1

        def four(t):
            return t.rearrange("p (b d) -> p b d", b=G)

        def per_batch(t):
            return t.unsqueeze(2).broadcast_to([P, G, P])

        def all_batches(t, width):
            return t.unsqueeze(1).broadcast_to([P, G, width])

        @block.sync
        def _(sp):
            with sp.Fori(0, NG) as g:
                sp.wait_ge(x_upd, g + 1)
                sp.dma_start(out[bass.ds(g * G, G)].rearrange("b t d -> t b d"), four(chip.xt(g * G, G))).then_inc(out_done, 16)
            sp.wait_ge(out_done, 16 * NG)

        @block.gpsimd
        def _(pool):
            nc.gpsimd.memset(minus_half[:], -0.5).then_inc(half_set, 1)
            nc.gpsimd.memset(eps[:], EPS).then_inc(half_set, 1)
            pool.wait_ge(half_set, 2)

            def step(s):
                g = s.g
                for u in range(CI):
                    if (u - END - 1) % 4 == 0:
                        late = END + 1
                        e = (u - late) // 4 % E1
                        if s.has(0) if u >= late else s.has(-1):
                            m = E1 * g + (u - late) // 4 + 1
                            pool.wait_ge(scaled, m)
                            if e == 0:
                                pool.wait_ge(acc_set, g + 1)
                            else:
                                pool.wait_ge(acc_done, (E1 - 1) * (g if u >= late else g - 1) + e)
                            if e < E1 - 1:
                                nc.gpsimd.tensor_tensor(acc[:], acc[:], part[:, e % 2], ALU.add).then_inc(acc_done, 1)
                            else:
                                nc.gpsimd.tensor_tensor(yT[:], acc[:], part[:, e % 2], ALU.add).then_inc(y_done, 1)
                    if u == 13 and s.has(-1):
                        pool.wait_ge(yo_psum, g)
                    if u == 2 and s.has(1):
                        pool.wait_ge(stats_done, G * (g + 2))
                        nc.gpsimd.tensor_tensor(var_eps[:], mv[:, :, 1], eps[:], ALU.add).then_inc(eps_done, 1)
                        pool.wait_ge(eps_done, g + 2)
                        need(pool, xn_done, G * (g + 1))
                        nc.gpsimd.tensor_tensor(rstd[:], var_eps[:], minus_half[:], ALU.pow).then_inc(rstd_done, 1)
                    if u == 4 and s.has(1):
                        pool.wait_ge(xn_done, G * (g + 2))
                        need(pool, x2_done, g + 1)
                        nc.gpsimd.tensor_tensor(xnb[:], xn[:], all_batches(w["bo"][:], P), ALU.add).then_inc(xnb_done, 1)
                    if u == 23 and s.has(1):
                        pool.wait_ge(x2_done, g + 2)
                        xg = four(chip.xt(G * (g + 1), G))
                        nc.gpsimd.tensor_tensor(xg, xg, x2[:], ALU.add).then_inc(res_done, 1)
            run_groups(pool, step)

        @block.tensor
        def _(pe):
            T = nc.tensor

            def step(s):
                g = s.g
                at = (g % 2) * GP
                for u in range(CI):
                    ok, cc, t = item(s, u, 0)
                    if ok:
                        if u == 0:
                            pe.wait_ge(x2T_hi, g + 1)
                            pe.wait_ge(x2T_lo, g + 1)
                        if u % 4 == 3:
                            if u == 3:
                                pe.wait_ge(gT_hi, g + 1)
                                pe.wait_ge(gT_lo, g + 1)
                            need(pe, gb_sb, E1 * g + u // 4)
                            if u == 7:
                                pe.wait_ge(acc_set, g + 1)
                        if u == 5:
                            pe.wait_ge(gb_sb, E1 * g + 1)
                        need(pe, relu_done, t - 2)
                        ws = slice(u * P, (u + 1) * P)
                        split3(T, chip.bank(U + u % 2, P, GP),
                               [(chip.w_hi[:, ws], chip.w_lo[:, ws], x2h[:, bass.ds(at, GP)], x2l[:, bass.ds(at, GP)])]).then_inc(up_psum, 1)
                        if u % 4 == 3:
                            e = u // 4
                            es = slice(e * P, (e + 1) * P)
                            T.matmul(chip.bank(GB, P, GP), w["sel"][:, es], gTh[:, bass.ds(at, GP)], start=True, stop=False)
                            T.matmul(chip.bank(GB, P, GP), w["sel"][:, es], gTl[:, bass.ds(at, GP)], start=False, stop=True).then_inc(gb_psum, 1)
                        if u == 5:
                            split3(T, chip.bank(GB, P, GP), [(w["b2h"][:], w["b2l"][:], gTh[:, bass.ds(at, GP)], gTl[:, bass.ds(at, GP)])]).then_inc(b2_psum, 1)
                    ok, cc, t = item(s, u, LAG)
                    if ok:
                        b = cc % RING
                        pe.wait_ge(h_lo, t)
                        if cc % 4 == 0:
                            need(pe, scaled, E1 * (g if u >= LAG else g - 1) + cc // 4 - 1)
                        split3(T, chip.bank(Y + cc // 4 % 2, P, GP), [(w["w2h"][:, cc], w["w2l"][:, cc], hh[:, b], hl[:, b])],
                               first=cc % 4 == 0, last=cc % 4 == 3).then_inc(down_done, 1)
                    if u == 5 and s.has(1):
                        pe.wait_ge(xn_done, G * (g + 2))
                        need(pe, x2T_sb, g + 1)
                        for b in range(G):
                            last = T.transpose(chip.bank(A, P, P, b * P), xn[:, b], chip.ident[:])
                        last.then_inc(xT_psum, 1)
                    if u == 8 and s.has(1):
                        pe.wait_ge(xT_lo, g + 2)
                        need(pe, g_logit, g + 1)
                        split3(T, chip.bank(B, P, GP), [(w["qk_h"][:, 0:P], w["qk_l"][:, 0:P], xTh[:], xTl[:])]).then_inc(q_psum, 1)
                        need(pe, gT_lo, g + 1)
                        split3(T, chip.bank(C, P, GP), [(w["qk_h"][:, P:], w["qk_l"][:, P:], xTh[:], xTl[:])]).then_inc(k_psum, 1)
                    if u == 9 and s.has(1):
                        pe.wait_ge(xT_sb, g + 2)
                        for b in range(G):
                            last = T.matmul(chip.bank(A, P, P, b * P), xT[:, b * P:(b + 1) * P], w["wv"][:], start=True, stop=True)
                        last.then_inc(v_psum, 1)
                    if u == 12 and s.has(-1):
                        pe.wait_ge(y_done, g)
                        if s.has(1):
                            pe.wait_ge(qT_sb, g + 2)
                        for b in range(G):
                            last = T.transpose(chip.bank(B, P, P, b * P), yT[:, b * P:(b + 1) * P], chip.ident[:])
                        last.then_inc(yo_psum, 1)
                    if u == 10 and s.has(1):
                        pe.wait_ge(qT_sb, g + 2)
                        pe.wait_ge(kT_sb, g + 2)
                        for b in range(G):
                            bs = slice(b * P, (b + 1) * P)
                            last = T.matmul(chip.bank(C, P, P, b * P), qT[:, bs], kT[:, bs], start=True, stop=True)
                        last.then_inc(s_psum, 1)
                    if u == 17 and s.has(1):
                        pe.wait_ge(w_done, g + 2)
                        pe.wait_ge(v_sb, g + 2)
                        for b in range(G):
                            last = T.transpose(chip.bank(A, P, P, b * P), att[:, b], chip.ident[:])
                        last.then_inc(wT_psum, 1)
                    if u == 19 and s.has(1):
                        pe.wait_ge(wT_sb, g + 2)
                        need(pe, x_upd, g)
                        for b in range(G):
                            last = T.matmul(chip.bank(B, P, P, b * P), v[:, b], attT[:, b * P:(b + 1) * P], start=True, stop=True)
                        last.then_inc(aT_psum, 1)
                    if u == 21 and s.has(1):
                        pe.wait_ge(aT_sb, g + 2)
                        pe.wait_ge(s_sub, g + 2)
                        for b in range(G):
                            last = T.matmul(chip.bank(C, P, P, b * P), aT[:, b * P:(b + 1) * P], w["wo"][:], start=True, stop=True)
                        last.then_inc(o_psum, 1)
                    if u == 24 and s.has(1):
                        pe.wait_ge(x2_done, g + 2)
                        pe.wait_ge(wT_sb, g + 2)
                        for b in range(G):
                            last = T.transpose(chip.bank(A, P, P, b * P), x2[:, b], chip.ident[:])
                        last.then_inc(x2T_psum, 1)
                    if u == 26 and s.has(1):
                        pe.wait_ge(x2T_sb, g + 2)
                        pe.wait_ge(aT_sb, g + 2)
                        for b in range(G):
                            last = T.matmul(chip.bank(B, P, E1, b * E1), x2T[:, b * P:(b + 1) * P], w["wg"][:], start=True, stop=True)
                        last.then_inc(g_psum, 1)
                    if u == 31 and s.has(1):
                        pe.wait_ge(gate_done, g + 2)
                        pe.wait_ge(x2_done, g + 2)
                        for b in range(G):
                            last = T.transpose(chip.bank(C, E1, P, b * P), gates[:, b], chip.ident[:])
                        last.then_inc(gT_psum, 1)
            run_groups(pe, step)

        @block.scalar
        def _(act):
            cols = w["cols"]

            def step(s):
                g = s.g
                nxt = ((g + 1) % 2) * GP
                for u in range(CI):
                    ok, cc, t = item(s, u, 0)
                    if ok:
                        act.wait_ge(up_psum, t)
                        need(act, h_lo, t - RING)
                        nc.scalar.activation(h[:, cc % RING], chip.bank(U + u % 2, P, GP), ACT.Relu,
                                             bias=cols[:, cc:cc + 1]).then_inc(relu_done, 1)
                        if u % 2 == 0:
                            act.wait_ge(relu_done, t)
                            need(act, down_done, t - RING)
                            nc.scalar.copy(hh[:, cc % RING], h[:, cc % RING]).then_inc(hi_act, 1)
                        if u % 4 == 3:
                            e = u // 4
                            act.wait_ge(gb_psum, E1 * g + e + 1)
                            need(act, scaled, E1 * g + e - 1)
                            nc.scalar.copy(gb[:, e % 2], chip.bank(GB, P, GP)).then_inc(gb_sb, 1)
                        if u == 5:
                            act.wait_ge(b2_psum, g + 1)
                            need(act, y_done, g)
                            nc.scalar.copy(acc[:], chip.bank(GB, P, GP)).then_inc(acc_set, 1)
                    if not s.has(1):
                        continue
                    if u == 5:
                        act.wait_ge(xT_psum, g + 2)
                        need(act, xT_lo, g + 1)
                        need(act, v_psum, g + 1)
                        nc.scalar.copy(xT[:], chip.bank(A, P, GP)).then_inc(xT_sb, 1)
                    if u == 8:
                        act.wait_ge(q_psum, g + 2)
                        need(act, s_psum, g + 1)
                        nc.scalar.activation(qT[:], chip.bank(B, P, GP), ACT.Identity, bias=cols[:, CI:CI + 1]).then_inc(qT_sb, 1)
                        act.wait_ge(k_psum, g + 2)
                        nc.scalar.activation(kT[:], chip.bank(C, P, GP), ACT.Identity, bias=cols[:, CI + 1:CI + 2]).then_inc(kT_sb, 1)
                    if u == 12:
                        act.wait_ge(s_sub, g + 2)
                        nc.scalar.activation(att[:], att[:], ACT.Exp, scale=P ** -0.5).then_inc(s_exp, 1)
                    if u == 17:
                        act.wait_ge(wT_psum, g + 2)
                        need(act, aT_psum, g + 1)
                        nc.scalar.copy(attT[:], chip.bank(A, P, GP)).then_inc(wT_sb, 1)
                    if u == 19:
                        act.wait_ge(aT_psum, g + 2)
                        need(act, o_psum, g + 1)
                        nc.scalar.copy(aT[:], chip.bank(B, P, GP)).then_inc(aT_sb, 1)
                    if u == 24:
                        act.wait_ge(x2T_psum, g + 2)
                        need(act, g_psum, g + 1)
                        need(act, x2T_lo, g + 1)
                        nc.scalar.copy(x2T[:], chip.bank(A, P, GP)).then_inc(x2T_sb, 1)
                    if u == 28:
                        act.wait_ge(g_sub, g + 2)
                        nc.scalar.activation(gates[:], gates[:], ACT.Exp).then_inc(g_exp, 1)
                    if u == 31:
                        act.wait_ge(gT_psum, g + 2)
                        need(act, gb_psum, E1 * g)
                        need(act, b2_psum, g)
                        nc.scalar.copy(gTh[:, bass.ds(nxt, GP)], chip.bank(C, E1, GP)).then_inc(gT_hi, 1)
            run_groups(act, step)

        @block.vector
        def _(dve):
            V = nc.vector

            def step(s):
                g = s.g
                nxt = ((g + 1) % 2) * GP
                for u in range(CI):
                    if u == 1 and s.has(1):
                        dve.wait_ge(bn_done, G * (g + 2))
                    ok, cc, t = item(s, u, 0)
                    if ok:
                        b = cc % RING
                        if u % 2 == 0:
                            dve.wait_ge(hi_act, CI // 2 * g + u // 2 + 1)
                        else:
                            dve.wait_ge(relu_done, t)
                            need(dve, down_done, t - RING)
                            V.tensor_copy(hh[:, b], h[:, b]).then_inc(hi_dve, 1)
                            dve.wait_ge(hi_dve, CI // 2 * g + u // 2 + 1)
                        V.tensor_tensor(hl[:, b], h[:, b], hh[:, b].bitcast(F32), ALU.subtract).then_inc(h_lo, 1)
                    if (u - END) % 4 == 0 and (s.has(0) if u >= END else s.has(-1)):
                        e = (u - END) // 4 % E1
                        m = E1 * g + (u - END) // 4
                        dve.wait_ge(down_done, 4 * m + 4)
                        dve.wait_ge(gb_sb, m + 1)
                        if e >= 2:
                            dve.wait_ge(acc_done, (E1 - 1) * (g if u >= END else g - 1) + e - 1)
                        elif e == 1:
                            need(dve, y_done, g)
                        else:
                            need(dve, acc_done, (E1 - 1) * g)
                        V.tensor_tensor(part[:, e % 2], chip.bank(Y + e % 2, P, GP), gb[:, e % 2], ALU.mult).then_inc(scaled, 1)
                    if u == 13 and s.has(-1):
                        dve.wait_ge(yo_psum, g)
                        dve.wait_ge(res_done, g)
                        xg = chip.xt(G * (g - 1), G)
                        V.tensor_tensor(xg, xg, chip.bank(B, P, GP), ALU.add).then_inc(x_upd, 1)
                    if not s.has(1):
                        continue
                    if u == 0:
                        for b in range(G):
                            V.bn_stats(bn[:, b], chip.xt(G * (g + 1) + b)).then_inc(bn_done, 1)
                    if u == 1:
                        for b in range(G):
                            V.bn_aggr(mv[:, b], bn[:, b]).then_inc(stats_done, 1)
                    if u == 3:
                        dve.wait_ge(rstd_done, g + 2)
                        need(dve, xT_psum, g + 1)
                        need(dve, xnb_done, g + 1)
                        for b in range(G):
                            V.tensor_scalar(xn[:, b], chip.xt(G * (g + 1) + b), mv[:, b, 0:1], rstd[:, b:b + 1],
                                            ALU.subtract, ALU.mult).then_inc(xn_done, 1)
                    if u == 6:
                        dve.wait_ge(xT_sb, g + 2)
                        need(dve, k_psum, g + 1)
                        V.tensor_copy(xTh[:], xT[:]).then_inc(xT_hi, 1)
                        dve.wait_ge(xT_hi, g + 2)
                        V.tensor_tensor(xTl[:], xT[:], xTh[:].bitcast(F32), ALU.subtract).then_inc(xT_lo, 1)
                    if u == 10:
                        dve.wait_ge(v_psum, g + 2)
                        need(dve, aT_psum, g + 1)
                        V.tensor_tensor(v[:], four(chip.bank(A, P, GP)), all_batches(w["bv"][:], P), ALU.add).then_inc(v_sb, 1)
                    if u == 11:
                        dve.wait_ge(s_psum, g + 2)
                        V.tensor_reduce(smax[:], four(chip.bank(C, P, GP)), AX_X, ALU.max).then_inc(s_max, 1)
                        dve.wait_ge(s_max, g + 2)
                        need(dve, wT_psum, g + 1)
                        V.tensor_tensor(att[:], four(chip.bank(C, P, GP)), per_batch(smax[:]), ALU.subtract).then_inc(s_sub, 1)
                    if u == 13:
                        dve.wait_ge(s_exp, g + 2)
                        V.tensor_reduce(ssum[:], att[:], AX_X, ALU.add).then_inc(s_sum, 1)
                        dve.wait_ge(s_sum, g + 2)
                        V.reciprocal(sinv[:], ssum[:]).then_inc(s_inv, 1)
                        dve.wait_ge(s_inv, g + 2)
                        V.tensor_tensor(att[:], att[:], per_batch(sinv[:]), ALU.mult).then_inc(w_done, 1)
                    if u == 22:
                        dve.wait_ge(o_psum, g + 2)
                        dve.wait_ge(xnb_done, g + 2)
                        need(dve, x2T_psum, g + 1)
                        need(dve, res_done, g + 1)
                        V.tensor_tensor(x2[:], xnb[:], four(chip.bank(C, P, GP)), ALU.add).then_inc(x2_done, 1)
                    if u == 25:
                        dve.wait_ge(x2T_sb, g + 2)
                        need(dve, up_psum, CI * g)
                        V.tensor_copy(x2h[:, bass.ds(nxt, GP)], x2T[:]).then_inc(x2T_hi, 1)
                        dve.wait_ge(x2T_hi, g + 2)
                        V.tensor_tensor(x2l[:, bass.ds(nxt, GP)], x2T[:], x2h[:, bass.ds(nxt, GP)].bitcast(F32), ALU.subtract).then_inc(x2T_lo, 1)
                    if u == 27:
                        gl = chip.bank(B, P, G * E1).rearrange("p (b e) -> p b e", b=G)
                        dve.wait_ge(g_psum, g + 2)
                        need(dve, gT_psum, g + 1)
                        V.tensor_tensor(gates[:], gl, all_batches(w["bg"][:], E1), ALU.add).then_inc(g_logit, 1)
                        dve.wait_ge(g_logit, g + 2)
                        V.tensor_reduce(gmax[:], gates[:], AX_X, ALU.max).then_inc(g_max, 1)
                        dve.wait_ge(g_max, g + 2)
                        V.tensor_tensor(gates[:], gates[:], gmax[:].unsqueeze(2).broadcast_to([P, G, E1]), ALU.subtract).then_inc(g_sub, 1)
                    if u == 29:
                        dve.wait_ge(g_exp, g + 2)
                        V.tensor_reduce(gsum[:], gates[:], AX_X, ALU.add).then_inc(g_sum, 1)
                        dve.wait_ge(g_sum, g + 2)
                        V.reciprocal(ginv[:], gsum[:]).then_inc(g_inv, 1)
                        dve.wait_ge(g_inv, g + 2)
                        V.tensor_tensor(gates[:], gates[:], ginv[:].unsqueeze(2).broadcast_to([P, G, E1]), ALU.mult).then_inc(gate_done, 1)
                    if u == 31:
                        dve.wait_ge(gT_hi, g + 2)
                        V.tensor_tensor(gTl[:, bass.ds(nxt, GP)], chip.bank(C, E1, GP), gTh[:, bass.ds(nxt, GP)].bitcast(F32),
                                        ALU.subtract).then_inc(gT_lo, 1)
            run_groups(dve, step)


def network(nc, a, out):
    with ExitStack() as ctx:
        chip = Chip(nc, ctx)
        x_in = (chip.x[:].rearrange("p (b d) -> p b d", b=NB), a["x"].rearrange("b t d -> t b d"))
        prep_sems, xattn_sems = {}, {}
        for L in range(2):
            names = {n: a[f"L{L}_xattn_{n}"] for n in ("Wq", "Wk", "Wv", "Wo", "bo")}
            prepare_xattn(nc, chip, L, {**names, "ident": a["ident"]}, prep_sems, loads=[x_in] if L == 0 else [])
            xattn_stage(nc, chip, L, a["ctx_768"], xattn_sems)
            ffn = {n[len("L0_ffn_"):]: t for n, t in a.items() if n.startswith(f"L{L}_ffn_")}
            if L == 0:
                moe0_stage(nc, chip, {**ffn, "pairs": a["pairs"], "before": a["before"]})
            else:
                ffn1_stage(nc, chip, {**ffn, "ones_rows": a["ones_rows"]}, out)


_OUT = (NB, P, P)


def kernel(**inputs):
    import numpy as np
    import concourse.bacc as bacc
    from concourse import mybir as _mybir
    from concourse.bass_utils import run_bass_kernel_spmd

    f = np.float32
    rows = np.arange(NGRP)[:, None], np.arange(NGRP)[None]
    constants = {
        "ident": np.eye(P, dtype=f),
        "pairs": (np.arange(NE)[:, None] == np.arange(CR * P)[None] // FI).astype(f),
        "ones_rows": (np.arange(E1)[:, None] == np.arange(E1 * P)[None] // P).astype(f),
        "before": np.stack([rows[1] < rows[0], rows[1] > rows[0]]).astype(f).reshape(-1),
    }
    nc = bacc.Bacc("TRN2", target_bir_lowering=False, num_devices=1)
    arrays, a = {}, {}
    for name, t in {**inputs, **constants}.items():
        t = np.ascontiguousarray(t)
        arrays[f"in_{name}"] = t
        a[name] = nc.dram_tensor(f"in_{name}", t.shape, _mybir.dt.from_np(t.dtype), kind="ExternalInput").ap()
    out = nc.dram_tensor("out_0", _OUT, F32, kind="ExternalOutput").ap()
    network(nc, a, out)
    r = run_bass_kernel_spmd(nc, [arrays], core_ids=[0])
    return r.results[0]["out_0"]
```

```python
from contextlib import ExitStack

import concourse.bass as bass
from concourse import mybir

F32 = mybir.dt.float32
F32R = mybir.dt.float32r
ALU = mybir.AluOpType
ACT = mybir.ActivationFunctionType
AX_X = mybir.AxisListType.X

P = 128
BANK = 512
NB = 32
G = 4
NG = NB // G
NK = 77
CD = 96
H = 16
DH = 64
INNER = H * DH
NC = INNER // P
HS = [(0, 6), (6, 12), (12, 16)]
EPS = 1e-5
LOW = 32


def need(eng, sem, value):
    if isinstance(value, int) and value <= 0:
        return
    eng.wait_ge(sem, value)


def split3(pe, out, pairs, first=True, last=True, **kw):
    n = 0
    for a_hi, a_lo, b_hi, b_lo in pairs:
        for a, b in ((a_hi, b_hi), (a_hi, b_lo), (a_lo, b_hi)):
            n += 1
            ins = pe.matmul(out, a, b, start=first and n == 1, stop=last and n == 3 * len(pairs), **kw)
    return ins


def cap(value, most):
    return min(value, most) if isinstance(value, int) else value


class Step:

    def __init__(self, g, i):
        self.g, self.i, self.n = g, i, g * G + i

    def has(self, off):
        return not isinstance(self.n, int) or 0 <= self.n + off < NB


def run_steps(eng, step):
    for n in range(-3, G):
        step(Step(n // G, n % G))
    with eng.Fori(1, NG - 1) as g:
        for i in range(G):
            step(Step(g, i))
    for n in range(NB - G, NB + 1):
        step(Step(n // G, n % G))


class Chip:

    def __init__(self, nc, ctx):
        self.nc, self.ctx = nc, ctx
        self.x = self.sb("x_res", [P, NB * P])
        self.ident = self.sb("identity", [P, P])
        self.fused = self.sb("fused", [P, 2 * H * P], F32R)
        self.fused_hi = self.fused[0:CD, 0:H * P]
        self.fused_lo = self.fused[0:CD, H * P:]
        self.wq = self.sb("wq", [P, INNER])
        self.wk = self.sb("wk", [P, INNER])
        self.wv = self.sb("wv", [P, INNER])
        self.wv_hi = self.sb("wv_hi", [CD, INNER], F32R)
        self.wv_lo = self.sb("wv_lo", [CD, INNER], F32R)
        self.wo = self.sb("wo", [P, NC * P])
        self.bo = self.sb("bo", [P, P])
        self.w_hi = self.sb("w_hi", [P, 4096], F32R)
        self.w_lo = self.sb("w_lo", [P, 4096], F32R)
        self.ps = ctx.enter_context(nc.psum_tensor("banks", [P, 8 * BANK], F32))

    def sb(self, name, shape, dt=F32):
        return self.ctx.enter_context(self.nc.sbuf_tensor(name, shape, dt))

    def sem(self, name):
        return self.ctx.enter_context(self.nc.semaphore(name))

    def xt(self, n, k=1):
        return self.x[:, bass.ds(n * P, k * P)]

    def bank(self, b, rows, width, at=0):
        return self.ps[0:rows, b * BANK + at:b * BANK + at + width]


def start_loads(sp, loads):
    for dst, src, sem in loads:
        sp.dma_start(dst, src).then_inc(sem, 16)


def all_rows(t, n):
    return t.rearrange("(o d) -> o d", o=1).broadcast_to([n, t.shape[0]])


def xattn_loads(chip, a, sems):
    return [(chip.wq[:], a["Wq"], sems["w_loaded"]), (chip.wk[0:CD], a["Wk"], sems["w_loaded"]), (chip.wv[0:CD], a["Wv"], sems["v_loaded"]),
            (chip.wo[:].rearrange("p (c d) -> p c d", c=NC), a["Wo"].rearrange("(c p) d -> p c d", p=P), sems["o_loaded"]),
            (chip.bo[:], all_rows(a["bo"], P), sems["o_loaded"])]


def xattn_prep_sems(chip):
    return {n: chip.sem("p_" + n) for n in "w_loaded v_loaded o_loaded wT_psum wT_act wT_dve f_psum f_hi f_lo v_hi v_lo".split()}


def prepare_xattn(nc, chip, L, sems, loads=()):
    pre = f"p{L}_"
    w_loaded, v_loaded, o_loaded, wT_psum, wT_act, wT_dve, f_psum, f_hi, f_lo, v_hi, v_lo = sems.values()
    base = {n: k * L for n, k in (("w_loaded", 48), ("v_loaded", 16), ("o_loaded", 48), ("wT_psum", 4), ("wT", 2), ("f", 4), ("v", 1))}
    n_w, n_o = (3, 3) if L == 0 else (2, 2)
    wq, wk, wv = chip.wq[:], chip.wk[0:CD], chip.wv[0:CD]
    with ExitStack() as own:
        def sb(name, shape, dt=F32):
            return own.enter_context(nc.sbuf_tensor(pre + name, shape, dt))

        wqT = sb("wqT", [P, NC * P])
        wkT = sb("wkT", [P, NC * CD])
        block = own.enter_context(nc.Block())

        F_ORDER = (0, 2, 1, 3)

        def heads(t, q):
            return t.rearrange("c (m r d) -> c r m d", r=2, d=P)[:, q // 2, 4 * (q % 2):4 * (q % 2) + 4]

        @block.sync
        def _(sp):
            start_loads(sp, loads)
            sp.wait_ge(o_loaded, base["o_loaded"] + 16 * n_o)

        @block.tensor
        def _(pe):
            pe.wait_ge(w_loaded, base["w_loaded"] + 16 * n_w)
            for w, rows, at in ((wq, P, 0), (wk, CD, 2)):
                for c in range(NC):
                    t = nc.tensor.transpose(chip.bank(at + c // 4, P, rows, (c % 4) * rows),
                                            w[:, c * P:(c + 1) * P], chip.ident[0:rows, 0:rows])
                    if c % 4 == 3:
                        t.then_inc(wT_psum, 1)
            pe.wait_ge(wT_act, base["wT"] + 2)
            pe.wait_ge(wT_dve, base["wT"] + 2)
            for m in range(NC):
                for odd in range(2):
                    r = slice(DH * odd, DH * (odd + 1))
                    f = nc.tensor.matmul(chip.bank(4 + 2 * odd + m // 4, CD, P, (m % 4) * P),
                                         wkT[r, m * CD:(m + 1) * CD], wqT[r, m * P:(m + 1) * P], start=True, stop=True)
                    if m % 4 == 3:
                        f.then_inc(f_psum, 1)

        @block.scalar
        def _(act):
            for q in range(2):
                act.wait_ge(wT_psum, base["wT_psum"] + q + 1)
                nc.scalar.copy(wqT[:, q * BANK:(q + 1) * BANK], chip.bank(q, P, BANK)).then_inc(wT_act, 1)
            act.wait_ge(v_loaded, base["v_loaded"] + 16)
            nc.scalar.copy(chip.wv_hi[:], wv).then_inc(v_hi, 1)
            for k, q in enumerate(F_ORDER):
                act.wait_ge(f_psum, base["f"] + k + 1)
                nc.scalar.copy(heads(chip.fused_hi, q), chip.bank(4 + q, CD, BANK).rearrange("c (m d) -> c m d", m=4)).then_inc(f_hi, 1)

        @block.vector
        def _(dve):
            for q in range(2):
                dve.wait_ge(wT_psum, base["wT_psum"] + q + 3)
                nc.vector.tensor_copy(wkT[:, q * 4 * CD:(q + 1) * 4 * CD], chip.bank(2 + q, P, 4 * CD)).then_inc(wT_dve, 1)
            dve.wait_ge(v_hi, base["v"] + 1)
            nc.vector.tensor_tensor(chip.wv_lo[:], wv, chip.wv_hi[:].bitcast(F32), ALU.subtract).then_inc(v_lo, 1)
            for k, q in enumerate(F_ORDER):
                dve.wait_ge(f_hi, base["f"] + k + 1)
                nc.vector.tensor_tensor(heads(chip.fused_lo, q), chip.bank(4 + q, CD, BANK).rearrange("c (m d) -> c m d", m=4),
                                        heads(chip.fused_hi, q).bitcast(F32), ALU.subtract).then_inc(f_lo, 1)


def xattn_stage(nc, chip, L, context, sems, ahead, x_rest):
    pre = f"x{L}_"
    names = ("ctx_loaded bn_done stats_done eps_done rstd_done xn_done xnT_psum xnT_hi xnT_lo bo_added "
             "ctxT_psum ctxT_hi ctxT_lo kp_psum kp_hi kp_lo sim_done max_done sub_done exp_done sum_done recip_done "
             "norm_done v_psum v_sb t_psum t_sb pv_psum oT_sb wo_psum x_upd half").split()
    if not sems:
        sems.update({n: chip.sem("x_" + n) for n in names})
    (ctx_loaded, bn_done, stats_done, eps_done, rstd_done, xn_done, xnT_psum, xnT_hi, xnT_lo, bo_added,
     ctxT_psum, ctxT_hi, ctxT_lo, kp_psum, kp_hi, kp_lo, sim_done, max_done, sub_done, exp_done, sum_done, recip_done,
     norm_done, v_psum, v_sb, t_psum, t_sb, pv_psum, oT_sb, wo_psum, x_upd, half_set) = (sems[n] for n in names)
    KW = G * NK
    with ExitStack() as own:
        def sb(name, shape, dt=F32):
            return own.enter_context(nc.sbuf_tensor(pre + name, shape, dt))

        ctx_raw = sb("ctx_raw", [NK, G, CD])
        ctxT_h = sb("ctxT_h", [CD, KW], F32R)
        ctxT_l = sb("ctxT_l", [CD, KW], F32R)
        kp_h = sb("kp_h", [P, G, H * NK], F32R)
        kp_l = sb("kp_l", [P, G, H * NK], F32R)
        bn = sb("bn", [P, 2, 6])
        mv = sb("mv", [P, 4, 2])
        rstd = sb("rstd", [P, 4])
        var_eps = sb("var_eps", [P, 4])
        minus_half = sb("minus_half", [P, 1])
        eps = sb("eps", [P, 1])
        xn = sb("xn", [P, 2, P])
        xnT_h = sb("xnT_h", [P, 2, P], F32R)
        xnT_l = sb("xnT_l", [P, 2, P], F32R)
        prob = sb("prob", [P, 2, H, NK])
        mx = sb("mx", [P, 2, H])
        rs = sb("rs", [P, 2, H])
        ri = sb("ri", [P, 2, H])
        v = sb("v", [NK, 2, INNER])
        pT = sb("pT", [NK, H, P])
        oT = sb("oT", [P, NC, P])
        SIM, MISC = 0, 7
        V_BANK, T_BANK, PV_BANK = (3, 4), (5, 6, 3, 4), (5, 6)
        KP_BANK = (3, 5, 0)
        CTX_AT, WO_AT = P, BANK - P

        def sim_ps(part):
            if part == 0:
                return chip.ps[:, 0:2 * BANK].rearrange("p (b c) -> p b c", b=2)[:, :, 0:6 * NK].rearrange(
                    "p b (h k) -> p b h k", h=6)
            return chip.bank(2, P, 4 * NK).rearrange("p (h k) -> p h k", h=4)

        def pair_ps(p):
            at = KP_BANK[p % 3] * BANK
            return chip.ps[:, at:at + 2 * BANK].rearrange("p (h c) -> p h c", h=2)[:, :, 0:KW].rearrange(
                "p h (b k) -> p h b k", b=G)

        def pair_sb(t, p):
            return t[:, :, 2 * p * NK:2 * (p + 1) * NK].rearrange("p b (h k) -> p h b k", h=2)

        def part_of(t, par, part):
            if part == 0:
                return t[:, par, 0:12].rearrange("p (b h) k -> p b h k", b=2) if len(t.shape) == 4 else \
                    t[:, par, 0:12].rearrange("p (b h) -> p b h", b=2)
            return t[:, par, 12:16]

        block = own.enter_context(nc.Block())

        @block.sync
        def _(sp):
            sp.dma_start(ctx_raw[:], context[0:G].rearrange("b k d -> k b d")).then_inc(ctx_loaded, 16)
            start_loads(sp, ahead)
            with sp.Fori(1, NG) as g:
                sp.wait_ge(ctxT_psum, g + NG * L)
                sp.dma_start(ctx_raw[:], context[bass.ds(g * G, G)].rearrange("b k d -> k b d")).then_inc(ctx_loaded, 16)

        @block.gpsimd
        def _(pool):
            nc.gpsimd.memset(minus_half[:], -0.5).then_inc(half_set, 1)
            nc.gpsimd.memset(eps[:], EPS).then_inc(half_set, 1)
            pool.wait_ge(half_set, 2 * L + 2)

            def step(s):
                n, i = s.n, s.i
                m = n + NB * L
                if s.has(2):
                    pool.wait_ge(xn_done, m + 3)
                    xb = chip.xt(n + 2)
                    nc.gpsimd.tensor_tensor(xb, xb, chip.bo[:], ALU.add).then_inc(bo_added, 1)
                if s.has(3):
                    b = (i + 3) % 4
                    pool.wait_ge(stats_done, m + 4)
                    need(pool, xn_done, m)
                    nc.gpsimd.tensor_tensor(var_eps[:, b:b + 1], mv[:, b, 1:2], eps[:], ALU.add).then_inc(eps_done, 1)
                    pool.wait_ge(eps_done, m + 4)
                    nc.gpsimd.tensor_tensor(rstd[:, b:b + 1], var_eps[:, b:b + 1], minus_half[:], ALU.pow).then_inc(rstd_done, 1)
                if s.has(1):
                    b = (i + 1) % 2
                    pool.wait_ge(recip_done, m + 2)
                    for q in range(4):
                        hq = slice(4 * q, 4 * q + 4)
                        nc.gpsimd.tensor_tensor(prob[:, b, hq], prob[:, b, hq],
                                                ri[:, b, hq].unsqueeze(2).broadcast_to([P, 4, NK]),
                                                ALU.mult).then_inc(norm_done, 1)
            run_steps(pool, step)

        @block.tensor
        def _(pe):
            def step(s):
                n, g, i = s.n, s.g, s.i
                m, gm = n + NB * L, g + NG * L
                b1 = (i + 1) % 2

                def weights(j):
                    if j < 2:
                        need(pe, oT_sb, 2 * m - 1 + j)
                    else:
                        pe.wait_ge(v_sb, cap(2 * m + 1 + j, 2 * NB * (L + 1)))
                    pe.wait_ge(norm_done, 4 * m + j + 1)
                    for h in range(4 * j, 4 * j + 4):
                        last = nc.tensor.transpose(chip.bank(T_BANK[j], NK, P, (h % 4) * P), prob[:, i % 2, h], chip.ident[:])
                    last.then_inc(t_psum, 1)

                def outputs(j):
                    pe.wait_ge(v_sb, 2 * m + 2)
                    pe.wait_ge(t_sb, 4 * m + 2 * j + 2)
                    for r in range(4):
                        for half in range(2):
                            h = 8 * j + 2 * r + half
                            at = PV_BANK[j] * BANK + r * P
                            last = nc.tensor.matmul(chip.ps[DH * half:DH * (half + 1), at:at + P],
                                                    v[:, i % 2, h * DH:(h + 1) * DH], pT[:, h], start=True, stop=True)
                    last.then_inc(pv_psum, 1)

                def scores():
                    pe.wait_ge(xnT_hi, m + 2)
                    pe.wait_ge(xnT_lo, m + 2)
                    need(pe, sub_done, 2 * m + 2)
                    if i == 3:
                        pe.wait_ge(kp_lo, 8 * gm + 16)
                    for q, (h0, h1) in enumerate(HS):
                        c = slice(h0 * NK, h1 * NK)
                        last = split3(nc.tensor, chip.bank(SIM + q, P, (h1 - h0) * NK),
                                      [(xnT_h[:, b1], xnT_l[:, b1], kp_h[:, (i + 1) % G, c], kp_l[:, (i + 1) % G, c])])
                    last.then_inc(sim_done, 1)

                def projection():
                    pe.wait_ge(oT_sb, 2 * m)
                    pe.wait_ge(xnT_lo, cap(m + 2, NB * (L + 1)))
                    if i == 3 and s.has(1):
                        pe.wait_ge(ctxT_lo, gm + 2)
                    for c in range(NC):
                        last = nc.tensor.matmul(chip.bank(MISC, P, P, WO_AT), oT[:, c], chip.wo[:, c * P:(c + 1) * P],
                                                start=c == 0, stop=c == NC - 1)
                    last.then_inc(wo_psum, 1)

                if i == 3 and s.has(1):
                    pe.wait_ge(ctxT_hi, gm + 2)
                    pe.wait_ge(ctxT_lo, gm + 2)
                    for p in range(H // 2):
                        if p >= 3:
                            pe.wait_ge(kp_lo, 8 * gm + 8 + p - 2)
                        elif p == 1:
                            need(pe, oT_sb, 2 * m)
                        elif p == 2:
                            need(pe, sub_done, 2 * m + 2)
                        for h in (2 * p, 2 * p + 1):
                            hs = slice(h * P, (h + 1) * P)
                            last = split3(nc.tensor, chip.bank(KP_BANK[p % 3] + h % 2, P, KW),
                                          [(chip.fused_hi[:, hs], chip.fused_lo[:, hs], ctxT_h[:], ctxT_l[:])])
                        last.then_inc(kp_psum, 1)
                if s.has(1) and i != 3:
                    scores()
                if s.has(-1):
                    projection()
                if s.has(1) and i == 3:
                    scores()
                if s.has(1):
                    cs = slice(((i + 1) % G) * NK, ((i + 1) % G + 1) * NK)
                    need(pe, t_sb, 4 * m)
                    for q in range(2):
                        c = slice(q * BANK, (q + 1) * BANK)
                        split3(nc.tensor, chip.bank(V_BANK[q], NK, BANK),
                               [(ctxT_h[:, cs], ctxT_l[:, cs], chip.wv_hi[:, c], chip.wv_lo[:, c])]).then_inc(v_psum, 1)
                if s.has(0):
                    for j in range(4):
                        weights(j)
                if i == 2 and s.has(2):
                    pe.wait_ge(ctx_loaded, 16 * gm + 32)
                    need(pe, x_upd, m)
                    for b in range(G):
                        last = nc.tensor.transpose(chip.bank(MISC, CD, NK, CTX_AT + b * NK), ctx_raw[:, b],
                                                   chip.ident[0:NK, 0:NK])
                    last.then_inc(ctxT_psum, 1)
                if s.has(2):
                    pe.wait_ge(xn_done, m + 3)
                    need(pe, x_upd, m)
                    nc.tensor.transpose(chip.bank(MISC, P, P), xn[:, i % 2], chip.ident[:]).then_inc(xnT_psum, 1)
                if s.has(0):
                    outputs(0)
                    outputs(1)
            run_steps(pe, step)

        @block.scalar
        def _(act):
            def step(s):
                n, g, i = s.n, s.g, s.i
                m, gm = n + NB * L, g + NG * L
                b1 = (i + 1) % 2

                def exps(part):
                    act.wait_ge(sub_done, 2 * m + 3 + part)
                    hp = slice(0, 12) if part == 0 else slice(12, 16)
                    nc.scalar.activation(prob[:, b1, hp], prob[:, b1, hp], ACT.Exp, scale=DH ** -0.5).then_inc(exp_done, 1)

                def weights(j):
                    act.wait_ge(t_psum, 4 * m + j + 1)
                    nc.scalar.copy(pT[:, 4 * j:4 * j + 4], chip.bank(T_BANK[j], NK, BANK)).then_inc(t_sb, 1)

                if i == 3 and s.has(1):
                    for p in range(H // 2):
                        act.wait_ge(kp_psum, 8 * gm + 9 + p)
                        nc.scalar.copy(pair_sb(kp_h, p), pair_ps(p)).then_inc(kp_hi, 1)
                if s.has(1):
                    for q in range(2):
                        act.wait_ge(v_psum, 2 * m + 3 + q)
                        nc.scalar.copy(v[:, b1, q * BANK:(q + 1) * BANK], chip.bank(V_BANK[q], NK, BANK)).then_inc(v_sb, 1)
                if s.has(0):
                    weights(0)
                    weights(1)
                    weights(2)
                    weights(3)
                if s.has(2):
                    act.wait_ge(xnT_psum, m + 3)
                    nc.scalar.copy(xnT_h[:, i % 2], chip.bank(MISC, P, P)).then_inc(xnT_hi, 1)
                if i == 2 and s.has(2):
                    act.wait_ge(ctxT_psum, gm + 2)
                    nc.scalar.copy(ctxT_h[:], chip.bank(MISC, CD, KW, CTX_AT)).then_inc(ctxT_hi, 1)
                if s.has(1):
                    exps(0)
                    exps(1)
            run_steps(act, step)

        @block.vector
        def _(dve):
            def step(s):
                n, g, i = s.n, s.g, s.i
                m, gm = n + NB * L, g + NG * L
                b1 = (i + 1) % 2

                def sums(off):
                    b = (i + off) % 2
                    dve.wait_ge(exp_done, 2 * (m + off) + 2)
                    nc.vector.tensor_reduce(rs[:, b], prob[:, b], AX_X, ALU.add).then_inc(sum_done, 1)
                    dve.wait_ge(sum_done, m + off + 1)
                    nc.vector.reciprocal(ri[:, b], rs[:, b]).then_inc(recip_done, 1)

                def outputs(j):
                    dve.wait_ge(pv_psum, 2 * m + j + 1)
                    nc.vector.tensor_copy(oT[:, 4 * j:4 * j + 4], chip.bank(PV_BANK[j], P, BANK)).then_inc(oT_sb, 1)

                if i == 3 and s.has(1):
                    for p in range(H // 2):
                        dve.wait_ge(kp_hi, 8 * gm + 9 + p)
                        nc.vector.tensor_tensor(pair_sb(kp_l, p), pair_ps(p), pair_sb(kp_h, p).bitcast(F32),
                                                ALU.subtract).then_inc(kp_lo, 1)
                    if s.has(0):
                        sums(0)
                if s.has(2):
                    b = (i + 2) % 4
                    dve.wait_ge(rstd_done, m + 3)
                    need(dve, xnT_psum, m + 1)
                    nc.vector.tensor_scalar(xn[:, i % 2], chip.xt(n + 2), mv[:, b, 0:1], rstd[:, b:b + 1],
                                            ALU.subtract, ALU.mult).then_inc(xn_done, 1)
                if s.has(1):
                    dve.wait_ge(sim_done, m + 2)
                    need(dve, t_psum, 4 * m)
                    for part in range(2):
                        nc.vector.tensor_reduce(part_of(mx, b1, part), sim_ps(part), AX_X, ALU.max).then_inc(max_done, 1)
                if s.has(3):
                    if L == 0 and isinstance(n, int) and n + 3 == G:
                        dve.wait_ge(x_rest, 16)
                    nc.vector.bn_stats(bn[:, b1], chip.xt(n + 3)).then_inc(bn_done, 1)
                    dve.wait_ge(bn_done, m + 4)
                if s.has(-1):
                    dve.wait_ge(wo_psum, m)
                    dve.wait_ge(bo_added, m)
                    xb = chip.xt(n - 1)
                    nc.vector.tensor_tensor(xb, xb, chip.bank(MISC, P, P, WO_AT), ALU.add).then_inc(x_upd, 1)
                if s.has(1):
                    for part in range(2):
                        sp_ = sim_ps(part)
                        dve.wait_ge(max_done, 2 * m + 3 + part)
                        nc.vector.tensor_tensor(part_of(prob, b1, part), sp_,
                                                part_of(mx, b1, part).unsqueeze(len(sp_.shape) - 1).broadcast_to(list(sp_.shape)),
                                                ALU.subtract).then_inc(sub_done, 1)
                if s.has(3):
                    nc.vector.bn_aggr(mv[:, (i + 3) % 4], bn[:, b1]).then_inc(stats_done, 1)
                if s.has(2):
                    dve.wait_ge(xnT_hi, m + 3)
                    if i == 2:
                        dve.wait_ge(ctxT_hi, gm + 2)
                    nc.vector.tensor_tensor(xnT_l[:, i % 2], chip.bank(MISC, P, P), xnT_h[:, i % 2].bitcast(F32),
                                            ALU.subtract).then_inc(xnT_lo, 1)
                if i == 2 and s.has(2):
                    dve.wait_ge(ctxT_hi, gm + 2)
                    nc.vector.tensor_tensor(ctxT_l[:], chip.bank(MISC, CD, KW, CTX_AT), ctxT_h[:].bitcast(F32),
                                            ALU.subtract).then_inc(ctxT_lo, 1)
                if s.has(0):
                    outputs(0)
                    outputs(1)
                if s.has(1) and not (i == 2 and s.has(2)):
                    sums(1)
            run_steps(dve, step)



NE = 16
FI = 64
TOP = 4
NGRP = 4
CR = NE * FI // P
CS = 2
CF = CR + CS
ROUTED_SCALE = 2.5
GP = G * P


class GroupStep:

    def __init__(self, g):
        self.g = g

    def has(self, off):
        return not isinstance(self.g, int) or 0 <= self.g + off < NG


def run_groups(eng, step, ahead=1):
    step(GroupStep(-1))
    step(GroupStep(0))
    with eng.Fori(1, NG - ahead) as g:
        step(GroupStep(g))
    for g in range(NG - ahead, NG + 1):
        step(GroupStep(g))


class Chain:

    def __init__(self, eng, sem, per_group):
        self.eng, self.sem, self.per = eng, sem, per_group

    def begin(self, g, done=0):
        self.base, self.n = self.per * g, done

    def link(self, ins):
        self.n += 1
        ins.then_inc(self.sem, 1)
        self.eng.wait_ge(self.sem, self.base + self.n)

    def end(self):
        assert self.n == self.per, self.n


class Moe0Weights:

    def __init__(self, nc, chip, scope, a):
        def sb(name, shape, dt=F32):
            return scope.enter_context(nc.sbuf_tensor("m0_" + name, shape, dt))

        self.up_loaded, self.dn_loaded, self.small = (chip.sem("m0_" + n) for n in "up_loaded dn_loaded small".split())
        self.up, self.dn = sb("up", [P, CF, P]), sb("dn", [P, CF, P])
        self.gw, self.sel = sb("gw", [NE, P]), sb("sel", [LOW + NE, CR * P])
        self.gate, self.bias = sb("gate", [P, NE]), sb("bias", [P, NE])
        self.pairs, self.before = sb("pairs", [LOW + NE, CR * P], F32R), sb("before", [P, 2 * NGRP * NGRP])
        self.cwT = sb("cwT", [LOW + NE, 2 * GP], F32R)
        self.loads = [
            (self.up[:, 0:CR], a["up_w"].rearrange("(c e) f d -> (e f) c d", e=2), self.up_loaded),
            (self.up[:, CR:CF], a["shared_up"].rearrange("(c f) d -> f c d", f=P), self.up_loaded),
            (self.gw[:], a["gate_w"], self.up_loaded),
            (self.dn[:, 0:CR].rearrange("d c (e f) -> d (c e) f", e=2), a["down_w"].rearrange("e d f -> d e f"), self.dn_loaded),
            (self.dn[:, CR:CF].rearrange("d c f -> d (c f)"), a["shared_down"], self.dn_loaded),
            (self.sel[:], a["pairs"], self.small), (self.bias[:], all_rows(a["bias_e"], P), self.small),
            (self.before[:], all_rows(a["before"], P), self.small)]


class PrepareMoe0:

    N_LOW = 2 * CF // 4 + 2

    def __init__(self, nc, chip, m):
        self.nc, self.chip, self.m = nc, chip, m
        self.wt_psum, self.wt_hi, self.wt_lo, self.gate_sb = (chip.sem("m0_" + n) for n in "wt_psum wt_hi wt_lo gate_sb".split())

    def tensor(self, pe):
        chip, m = self.chip, self.m
        pe.wait_ge(m.up_loaded, 48)
        for c in range(2 * CF):
            if c == CF:
                pe.wait_ge(m.dn_loaded, 32)
            src = m.up[:, c] if c < CF else m.dn[:, c - CF]
            t = self.nc.tensor.transpose(chip.bank(c // 4, P, P, (c % 4) * P), src, chip.ident[:])
            if c % 4 == 3:
                t.then_inc(self.wt_psum, 1)
        self.nc.tensor.transpose(chip.bank(7, P, NE), m.gw[:], chip.ident[0:NE, 0:NE]).then_inc(self.wt_psum, 1)

    def scalar(self, act):
        chip = self.chip
        for q in range(2 * CF // 4):
            act.wait_ge(self.wt_psum, q + 1)
            self.nc.scalar.copy(chip.w_hi[:, q * BANK:(q + 1) * BANK], chip.bank(q, P, BANK)).then_inc(self.wt_hi, 1)
        act.wait_ge(self.wt_psum, 2 * CF // 4 + 1)
        self.nc.scalar.copy(self.m.gate[:], chip.bank(7, P, NE)).then_inc(self.gate_sb, 1)

    def vector(self, dve):
        chip, m = self.chip, self.m
        for q in range(2 * CF // 4):
            dve.wait_ge(self.wt_hi, q + 1)
            c = slice(q * BANK, (q + 1) * BANK)
            self.nc.vector.tensor_tensor(chip.w_lo[:, c], chip.bank(q, P, BANK), chip.w_hi[:, c].bitcast(F32),
                                         ALU.subtract).then_inc(self.wt_lo, 1)
        dve.wait_ge(m.small, 48)
        self.nc.vector.tensor_copy(m.pairs[:], m.sel[:]).then_inc(self.wt_lo, 1)
        self.nc.vector.tensor_scalar(m.cwT[:], m.sel[:], 0.0, None, ALU.mult).then_inc(self.wt_lo, 1)


def moe0_stage(nc, chip, weights, ahead):
    names = ("bn_done stats_done xc_done eps_done rstd_done xn_done xnT_psum xT_sb xT_hi xT_lo logit_psum act_sc router cw_done "
             "cwT_psum cwT_hi cwT_lo up_psum bc_psum relu_done sq_done h_done h_hi h_lo down_done yT_sb yo_psum "
             "x_upd half scan_zero").split()
    (bn_done, stats_done, xc_done, eps_done, rstd_done, xn_done, xnT_psum, xT_sb, xT_hi, xT_lo, logit_psum, act_sc, router, cw_done,
     cwT_psum, cwT_hi, cwT_lo, up_psum, bc_psum, relu_done, sq_done, h_done, h_hi, h_lo, down_done, yT_sb, yo_psum,
     x_upd, half_set, scan_zero) = (chip.sem("f0_" + n) for n in names)
    RING = 5
    HI, LAG = 2, 4
    U, B, Y, XT, YT, LG, CW = 0, 2, 4, 5, 6, 7, 7
    with ExitStack() as own:
        def sb(name, shape, dt=F32):
            return own.enter_context(nc.sbuf_tensor("f0_" + name, shape, dt))

        prepare = PrepareMoe0(nc, chip, weights)
        bn = sb("bn", [P, G, 6])
        mv = sb("mv", [P, G, 2])
        rstd = sb("rstd", [P, G])
        var_eps = sb("var_eps", [P, G])
        minus_half = sb("minus_half", [P, G])
        eps = sb("eps", [P, G])
        xn = sb("xn", [P, G, P])
        xT = sb("xT", [P, GP])
        xh = sb("xh", [P, 2 * GP], F32R)
        xl = sb("xl", [P, 2 * GP], F32R)
        th = sb("th", [P, G, NE])
        ex = sb("ex", [P, G, NE])
        cwT = weights.cwT
        r = sb("r", [P, RING, GP])
        sq = sb("sq", [P, RING, GP])
        h = sb("h", [P, RING, GP])
        hh = sb("hh", [P, RING, GP], F32R)
        hl = sb("hl", [P, RING, GP], F32R)
        yT = sb("yT", [P, GP])
        sc = sb("sc", [P, G, NE])
        sig = sb("sig", [P, G, NE])
        pair_max = sb("pair_max", [P, G * NGRP, 2])
        pair_min = sb("pair_min", [P, G * NGRP, 2])
        best = sb("best", [P, G * NGRP])
        second = sb("second", [P, G * NGRP])
        other = sb("other", [P, G * NGRP])
        gs = sb("gs", [P, G, NGRP])
        ge = sb("ge", [P, G, NGRP, NGRP])
        gt4 = sb("gt4", [P, G, NGRP, NGRP])
        rank = sb("rank", [P, G, NGRP])
        masked = sb("masked", [P, G, NE])
        top8 = sb("top8", [P, G, 8])
        over = sb("over", [P, G, NE])
        n_over = sb("n_over", [P, G])
        PAD = 8
        scan = sb("scan", [P, 2, G, PAD + NE])
        same = sb("same", [P, G, NE])
        w_sum = sb("w_sum", [P, G])
        w_inv = sb("w_inv", [P, G])
        cw = sb("cw", [P, G, NE])
        gate, bias, pairs, before = weights.gate, weights.bias, weights.pairs, weights.before
        block = own.enter_context(nc.Block())

        def chunk(s, c, late):
            return (s.has(0) if c >= late else s.has(-1)), (c - late) % CF, CF * s.g + c - late + 1

        def first(s):
            return isinstance(s.g, int) and s.g == -1

        @block.sync
        def _(sp):
            start_loads(sp, ahead)

        @block.gpsimd
        def _(pool):
            nc.gpsimd.memset(minus_half[:], -0.5).then_inc(half_set, 1)
            nc.gpsimd.memset(eps[:], EPS).then_inc(half_set, 1)
            pool.wait_ge(half_set, 2)

            def centred(g, off):
                pool.wait_ge(stats_done, G * (g + off + 1))
                need(pool, xnT_psum, g + off)
                xg = chip.xt(G * (g + off), G).rearrange("p (b d) -> p b d", b=G)
                nc.gpsimd.tensor_tensor(xn[:], xg, mv[:, :, 0:1].broadcast_to([P, G, P]), ALU.subtract).then_inc(xc_done, 1)

            def rstds(g, off):
                nc.gpsimd.tensor_tensor(var_eps[:], mv[:, :, 1], eps[:], ALU.add).then_inc(eps_done, 1)
                pool.wait_ge(eps_done, g + off + 1)
                nc.gpsimd.tensor_tensor(rstd[:], var_eps[:], minus_half[:], ALU.pow).then_inc(rstd_done, 1)

            def normalised(g, off):
                pool.wait_ge(rstd_done, g + off + 1)
                pool.wait_ge(xc_done, g + off + 1)
                nc.gpsimd.tensor_tensor(xn[:], xn[:], rstd[:].unsqueeze(2).broadcast_to([P, G, P]), ALU.mult).then_inc(xn_done, 1)

            def step(s):
                g = s.g
                if first(s):
                    centred(g, 1)
                    rstds(g, 1)
                    normalised(g, 1)
                for c in range(CF):
                    ok, cc, t = chunk(s, c, HI)
                    if ok:
                        b = cc % RING
                        pool.wait_ge(h_hi, t)
                        need(pool, down_done, t - RING)
                        nc.gpsimd.tensor_tensor(hl[:, b], h[:, b], hh[:, b].bitcast(F32), ALU.subtract).then_inc(h_lo, 1)
                    if s.has(2):
                        if c == 2:
                            centred(g, 2)
                        if c == 3:
                            rstds(g, 2)
                        if c == 4:
                            normalised(g, 2)
            run_groups(pool, step, ahead=2)

        @block.tensor
        def _(pe):
            def step(s):
                g = s.g
                at = (g % 2) * GP if s.has(0) else 0

                def up(c, t):
                    if c == 0 and isinstance(g, int) and g == 0:
                        pe.wait_ge(prepare.wt_lo, prepare.N_LOW)
                    if c == 0:
                        pe.wait_ge(xT_hi, g + 1)
                        pe.wait_ge(xT_lo, g + 1)
                    need(pe, relu_done, t - 2)
                    ws = slice(c * P, (c + 1) * P)
                    split3(nc.tensor, chip.bank(U + c % 2, P, GP), [(chip.w_hi[:, ws], chip.w_lo[:, ws], xh[:, bass.ds(at, GP)],
                                                                     xl[:, bass.ds(at, GP)])]).then_inc(up_psum, 1)

                def weights(c):
                    sel, bank = pairs[:, c * P:(c + 1) * P], chip.bank(B + c % 2, P, GP)
                    nc.tensor.matmul(bank, sel, cwT[:, bass.ds(at, GP)], start=True, stop=True).then_inc(bc_psum, 1)

                def down(cc, t):
                    b = cc % RING
                    pe.wait_ge(h_hi, t)
                    pe.wait_ge(h_lo, t)
                    if cc == 0:
                        need(pe, yT_sb, g)
                    ws = slice((CF + cc) * P, (CF + cc + 1) * P)
                    last = split3(nc.tensor, chip.bank(Y, P, GP), [(chip.w_hi[:, ws], chip.w_lo[:, ws], hh[:, b], hl[:, b])],
                                  first=cc == 0, last=cc == CF - 1)
                    last.then_inc(down_done, 1)

                def transposes(off):
                    pe.wait_ge(xn_done, g + off + 1)
                    need(pe, xT_sb, g + off)
                    for b in range(G):
                        last = nc.tensor.transpose(chip.bank(XT, P, P, b * P), xn[:, b], chip.ident[:])
                    last.then_inc(xnT_psum, 1)

                def logits(off):
                    pe.wait_ge(xT_sb, g + off + 1)
                    need(pe, cwT_lo, g + off - 1)
                    for b in range(G):
                        last = nc.tensor.matmul(chip.bank(LG, P, NE, b * NE), xT[:, b * P:(b + 1) * P], gate[:], start=True, stop=True)
                    last.then_inc(logit_psum, 1)

                if first(s):
                    prepare.tensor(pe)
                    transposes(1)
                    pe.wait_ge(prepare.gate_sb, 1)
                    logits(1)
                for c in range(CF):
                    now, _, t = chunk(s, c, 0)
                    late, cc, td = chunk(s, c, LAG)
                    if now:
                        up(c, t)
                    if now and c == 1:
                        pe.wait_ge(cwT_hi, g + 1)
                        pe.wait_ge(cwT_lo, g + 1)
                    if now and 0 < c < CR:
                        need(pe, h_done, CR * g + c - 1)
                    if late:
                        down(cc, td)
                    if now and c == 1:
                        weights(0)
                    if now and 0 < c < CR:
                        weights(c)
                    if c == 6 and s.has(2):
                        transposes(2)
                    if c == 7 and s.has(2):
                        logits(2)
                    if c == LAG and s.has(-1):
                        pe.wait_ge(yT_sb, g)
                        for b in range(G):
                            last = nc.tensor.transpose(chip.bank(YT, P, P, b * P), yT[:, b * P:(b + 1) * P], chip.ident[:])
                        last.then_inc(yo_psum, 1)
                    if c == 8 and s.has(1):
                        pe.wait_ge(cw_done, g + 2)
                        pe.wait_ge(act_sc, 2 * cap(g + 3, NG))
                        for b in range(G):
                            last = nc.tensor.transpose(chip.bank(CW, NE, P, b * P), cw[:, b], chip.ident[:])
                        last.then_inc(cwT_psum, 1)
            run_groups(pe, step, ahead=2)

        @block.scalar
        def _(act):
            def xT_of(g, off):
                act.wait_ge(xnT_psum, g + off + 1)
                need(act, logit_psum, g + off)
                need(act, xT_lo, g + off)
                nc.scalar.copy(xT[:], chip.bank(XT, P, GP)).then_inc(xT_sb, 1)

            def sigmoids(g, off):
                act.wait_ge(logit_psum, g + off + 1)
                need(act, cw_done, g + off)
                lg = chip.bank(LG, P, G * NE).rearrange("p (b e) -> p b e", b=G)
                nc.scalar.activation(th[:], lg, ACT.Tanh, scale=0.5).then_inc(act_sc, 1)
                nc.scalar.activation(ex[:], lg, ACT.Exp, scale=-1.0).then_inc(act_sc, 1)

            def step(s):
                g = s.g
                nxt = ((g + 1) % 2) * GP
                if first(s):
                    prepare.scalar(act)
                    xT_of(g, 1)
                    sigmoids(g, 1)
                for c in range(CF):
                    if c == LAG and s.has(-1):
                        act.wait_ge(down_done, CF * g)
                        nc.scalar.copy(yT[:], chip.bank(Y, P, GP)).then_inc(yT_sb, 1)
                    ok, cc, t = chunk(s, c, 0)
                    if ok:
                        b = cc % RING
                        act.wait_ge(up_psum, t)
                        nc.scalar.activation(r[:, b], chip.bank(U + c % 2, P, GP), ACT.Relu).then_inc(relu_done, 1)
                    ok, cc, t = chunk(s, c, HI)
                    if ok:
                        b = cc % RING
                        if cc < CR:
                            act.wait_ge(h_done, CR * g + cc + 1)
                        else:
                            act.wait_ge(sq_done, t)
                        need(act, down_done, t - RING)
                        nc.scalar.copy(hh[:, b], h[:, b]).then_inc(h_hi, 1)
                    ok, cc, t = chunk(s, c, 0)
                    if ok:
                        b = cc % RING
                        act.wait_ge(relu_done, t)
                        if cc < CR:
                            need(act, h_done, CR * g + cc + 1 - RING)
                        else:
                            act.wait_ge(h_lo, t - RING)
                        nc.scalar.activation((sq if cc < CR else h)[:, b], r[:, b], ACT.Square).then_inc(sq_done, 1)
                    if c == 6 and s.has(2):
                        xT_of(g, 2)
                    if c == 7 and s.has(2):
                        sigmoids(g, 2)
                    if c == 8 and s.has(-1):
                        act.wait_ge(yo_psum, g)
                    if c == 8 and s.has(1):
                        act.wait_ge(cwT_psum, g + 2)
                        need(act, bc_psum, CR * g)
                        nc.scalar.copy(cwT[0:NE, bass.ds(nxt, GP)], chip.bank(CW, NE, GP)).then_inc(cwT_hi, 1)
            run_groups(act, step, ahead=2)

        @block.vector
        def _(dve):
            for k in range(2):
                nc.vector.memset(scan[:, k], 0.0).then_inc(scan_zero, 1)
            dve.wait_ge(scan_zero, 2)
            chain = Chain(dve, router, 27)
            EARLY = 7
            V = nc.vector

            def over_experts(t):
                return t.unsqueeze(2).broadcast_to([P, G, NE])

            gi = gs[:].unsqueeze(3).broadcast_to([P, G, NGRP, NGRP])
            gj = gs[:].unsqueeze(2).broadcast_to([P, G, NGRP, NGRP])
            tie = before[:].rearrange("p (k i j) -> p k i j", k=2, i=NGRP)

            def router_scores(g, off):
                dve.wait_ge(act_sc, 2 * (g + off) + 2)
                V.tensor_scalar(ex[:], ex[:], 1.0, None, ALU.add)
                chain.link(V.tensor_scalar(sc[:], th[:], 0.5, 0.5, ALU.mult, ALU.add))
                chain.link(V.tensor_tensor(sc[:], sc[:], bias[:].unsqueeze(1).broadcast_to([P, G, NE]), ALU.add))
                s4 = sc[:].rearrange("p b (i e) -> p (b i) e", e=4)
                V.tensor_tensor(pair_max[:], s4[:, :, 0:2], s4[:, :, 2:4], ALU.max)
                chain.link(V.tensor_tensor(pair_min[:], s4[:, :, 0:2], s4[:, :, 2:4], ALU.min))

            def router_groups():
                V.tensor_tensor(best[:], pair_max[:, :, 0], pair_max[:, :, 1], ALU.max)
                V.tensor_tensor(second[:], pair_max[:, :, 0], pair_max[:, :, 1], ALU.min)
                chain.link(V.tensor_tensor(other[:], pair_min[:, :, 0], pair_min[:, :, 1], ALU.max))
                chain.link(V.tensor_tensor(second[:], second[:], other[:], ALU.max))
                chain.link(V.tensor_tensor(gs[:].rearrange("p b i -> p (b i)"), best[:], second[:], ALU.add))
                V.tensor_tensor(ge[:], gj, gi, ALU.is_ge)
                chain.link(V.tensor_tensor(gt4[:], gj, gi, ALU.is_gt))

            def router_choice():
                V.tensor_tensor(ge[:], ge[:], tie[:, 0].unsqueeze(1).broadcast_to([P, G, NGRP, NGRP]), ALU.mult)
                chain.link(V.tensor_tensor(gt4[:], gt4[:], tie[:, 1].unsqueeze(1).broadcast_to([P, G, NGRP, NGRP]), ALU.mult))
                chain.link(V.tensor_tensor(ge[:], ge[:], gt4[:], ALU.add))
                chain.link(V.tensor_reduce(rank[:], ge[:], AX_X, ALU.add))
                chain.link(V.tensor_scalar(rank[:], rank[:], 1.5, None, ALU.is_lt))
                chain.link(V.tensor_tensor(masked[:].rearrange("p b (i e) -> p b i e", e=4), sc[:].rearrange("p b (i e) -> p b i e", e=4),
                                           rank[:].unsqueeze(3).broadcast_to([P, G, NGRP, 4]), ALU.mult))

            def router_top():
                V.reciprocal(sig[:], ex[:])
                for b in range(G):
                    last = V.max(top8[:, b], masked[:, b])
                chain.link(last)
                fourth = over_experts(top8[:, :, TOP - 1])
                V.tensor_tensor(over[:], masked[:], fourth, ALU.is_gt)
                chain.link(V.tensor_tensor(scan[:, 0, :, PAD:], masked[:], fourth, ALU.is_equal))
                V.tensor_copy(same[:], scan[:, 0, :, PAD:])
                chain.link(V.tensor_reduce(n_over[:], over[:], AX_X, ALU.add))

            def router_ties():
                for k, d in enumerate((1, 2, 4, 8)):
                    src, dst = scan[:, k % 2], scan[:, 1 - k % 2]
                    chain.link(V.tensor_tensor(dst[:, :, PAD:], src[:, :, PAD:], src[:, :, PAD - d:PAD + NE - d], ALU.add))
                chain.link(V.tensor_tensor(masked[:], scan[:, 0, :, PAD:], over_experts(n_over[:]), ALU.add))
                chain.link(V.scalar_tensor_tensor(same[:], masked[:], TOP + 0.5, same[:], ALU.is_lt, ALU.mult))

            def router_weights():
                chain.link(V.tensor_tensor(over[:], over[:], same[:], ALU.add))
                chain.link(V.tensor_tensor(sig[:], sig[:], over[:], ALU.mult))
                chain.link(V.tensor_reduce(w_sum[:], sig[:], AX_X, ALU.add))
                chain.link(V.tensor_scalar(w_sum[:], w_sum[:], 1e-20, None, ALU.add))
                chain.link(V.reciprocal(w_inv[:], w_sum[:]))
                chain.link(V.tensor_tensor(sig[:], sig[:], over_experts(w_inv[:]), ALU.mult))

            def moments(g, off):
                for b in range(G):
                    V.bn_stats(bn[:, b], chip.xt(G * (g + off) + b)).then_inc(bn_done, 1)

            def stats():
                for b in range(G):
                    V.bn_aggr(mv[:, b], bn[:, b]).then_inc(stats_done, 1)

            def step(s):
                g = s.g
                nxt = ((g + 1) % 2) * GP
                if first(s):
                    moments(g, 1)
                    dve.wait_ge(bn_done, G * (g + 2))
                    stats()
                    prepare.vector(dve)
                    chain.begin(g + 1)
                    router_scores(g, 1)
                    router_groups()
                for c in range(CF):
                    if c == 1 and s.has(2):
                        dve.wait_ge(bn_done, G * (g + 3))
                        dve.wait_ge(xn_done, g + 2)
                    ok, cc, t = chunk(s, c, 0)
                    if ok and cc < CR:
                        b = cc % RING
                        dve.wait_ge(bc_psum, CR * g + cc + 1)
                        dve.wait_ge(sq_done, t)
                        need(dve, h_lo, t - RING)
                        V.tensor_tensor(h[:, b], sq[:, b], chip.bank(B + c % 2, P, GP), ALU.mult).then_inc(h_done, 1)
                    if c == 0 and s.has(2):
                        moments(g, 2)
                    if c == 1 and s.has(2):
                        stats()
                    if c == 6 and s.has(-1):
                        dve.wait_ge(yo_psum, g)
                        xg = chip.xt(G * (g - 1), G)
                        V.tensor_tensor(xg, xg, chip.bank(YT, P, GP), ALU.add).then_inc(x_upd, 1)
                    if s.has(1):
                        if c == 2:
                            chain.begin(g + 1, EARLY)
                            router_choice()
                            router_top()
                        if c == 4:
                            dve.wait_ge(xT_sb, g + 2)
                            need(dve, up_psum, CF * g)
                            V.tensor_copy(xh[:, bass.ds(nxt, GP)], xT[:]).then_inc(xT_hi, 1)
                            dve.wait_ge(xT_hi, g + 2)
                            V.tensor_tensor(xl[:, bass.ds(nxt, GP)], xT[:], xh[:, bass.ds(nxt, GP)].bitcast(F32),
                                            ALU.subtract).then_inc(xT_lo, 1)
                        if c == 5:
                            router_ties()
                            router_weights()
                            need(dve, cwT_psum, g + 1)
                            V.tensor_scalar(cw[:], sig[:], ROUTED_SCALE, None, ALU.mult).then_inc(cw_done, 1)
                            chain.end()
                    if c == 7 and s.has(2):
                        chain.begin(g + 2)
                        router_scores(g, 2)
                        router_groups()
                    if c == 9 and s.has(1):
                        dve.wait_ge(cwT_hi, g + 2)
                        V.tensor_tensor(cwT[LOW:, bass.ds(nxt, GP)], chip.bank(CW, NE, GP), cwT[0:NE, bass.ds(nxt, GP)].bitcast(F32),
                                        ALU.subtract).then_inc(cwT_lo, 1)
            run_groups(dve, step, ahead=2)



E1 = 8
D1 = 512
C1 = D1 // P
CI = E1 * C1


class Moe1Weights:

    def __init__(self, nc, chip, scope, a):
        def sb(name, shape, dt=F32):
            return scope.enter_context(nc.sbuf_tensor("m1_" + name, shape, dt))

        self.w1_loaded, self.w2_loaded, self.small = (chip.sem("m1_" + n) for n in "w1_loaded w2_loaded small".split())
        self.w2h = chip.fused[:].rearrange("p (c d) -> p c d", c=CI)
        self.spare = sb("spare", [P, CI * P + INNER])
        self.w2_raw = [self.spare[:, CI * P:], chip.wq[:], chip.wk[:], chip.wv[:]]
        self.wv, self.wo, self.wg = sb("wv", [P, P]), sb("wo", [P, P]), sb("wg", [P, E1])
        self.bv, self.bo, self.bg = sb("bv", [P, P]), sb("bo", [P, P]), sb("bg", [P, E1])
        self.wvT = sb("wvT", [P, 2 * P])
        self.vo = sb("vo", [P, 2 * P])
        self.cols = sb("cols", [P, CI + 2])
        self.qk_h, self.qk_l = sb("qk_h", [P, 2 * P], F32R), sb("qk_l", [P, 2 * P], F32R)
        self.b2h, self.b2l = sb("b2h", [LOW + E1, P], F32R), sb("b2l", [E1, P], F32R)
        self.sel = sb("sel", [LOW + E1, E1 * P], F32R)
        self.gT = sb("gT", [LOW + E1, 2 * GP], F32R)
        self.rows, self.qk, self.b2, self.sel_raw = sb("rows", [CI + 2, P]), sb("qk", [P, 2 * P]), sb("b2", [E1, P]), sb("sel_raw", [LOW + E1, E1 * P])
        smalls = [
            (self.rows[0:CI], a["b1"].rearrange("e (c p) -> (e c) p", p=P)), (self.rows[CI:CI + 1], all_rows(a["bq"], 1)),
            (self.rows[CI + 1:CI + 2], all_rows(a["bk"], 1)), (self.qk[:, 0:P], a["Wq"]), (self.qk[:, P:], a["Wk"]),
            (self.wv[:], a["Wv"]), (self.wo[:], a["Wo"]), (self.wg[:], a["Wg"]), (self.bv[:], all_rows(a["bv"], P)),
            (self.bo[:], all_rows(a["bo"], P)), (self.bg[:], all_rows(a["bg"], P)), (self.b2[:], a["b2"]), (self.sel_raw[:], a["ones_rows"])]
        self.n_small = len(smalls)
        self.loads = [(dst, src, self.small) for dst, src in smalls] + [
            (self.spare[:, 0:CI * P].rearrange("p (e d) -> p e d", e=E1), a["W1"].rearrange("e h d -> h e d"), self.w1_loaded)] + [
            (t.rearrange("p (c d) -> p c d", d=P), a["W2"].rearrange("e (c p) h -> p (e c) h", p=P)[:, k * NC:(k + 1) * NC], self.w2_loaded)
            for k, t in enumerate(self.w2_raw)]


class PrepareMoe1:

    def __init__(self, nc, chip, w):
        self.nc, self.chip, self.w = nc, chip, w
        self.t_psum, self.t_sb, self.hi, self.lo = (chip.sem("m1_" + n) for n in "t_psum t_sb hi lo".split())

    def tensor(self, pe):
        chip, w = self.chip, self.w
        pe.wait_ge(w.small, 16 * w.n_small)
        T = self.nc.tensor
        T.transpose(chip.bank(0, P, CI + 2), w.rows[:], chip.ident[0:CI + 2, 0:CI + 2]).then_inc(self.t_psum, 1)
        T.transpose(chip.bank(1, P, P), w.wv[:], chip.ident[:])
        T.transpose(chip.bank(1, P, P, P), w.bv[:], chip.ident[:]).then_inc(self.t_psum, 1)
        pe.wait_ge(self.t_sb, 2)
        T.matmul(chip.bank(2, P, P), w.wvT[:, 0:P], w.wo[:], start=True, stop=True)
        T.matmul(chip.bank(2, P, P, P), w.wvT[:, P:], w.wo[:], start=True, stop=True).then_inc(self.t_psum, 1)

    def scalar(self, act):
        for k, (dst, width) in enumerate(((self.w.cols, CI + 2), (self.w.wvT, 2 * P), (self.w.vo, 2 * P))):
            act.wait_ge(self.t_psum, k + 1)
            self.nc.scalar.copy(dst[:], self.chip.bank(k, P, width)).then_inc(self.t_sb, 1)
        act.wait_ge(self.t_sb, 1)

    def vector(self, dve):
        V, w, hi, lo = self.nc.vector, self.w, self.hi, self.lo
        dve.wait_ge(w.small, 16 * w.n_small)
        V.tensor_copy(w.qk_h[:], w.qk[:]).then_inc(hi, 1)
        dve.wait_ge(hi, 1)
        V.tensor_tensor(w.qk_l[:], w.qk[:], w.qk_h[:].bitcast(F32), ALU.subtract).then_inc(lo, 1)
        V.tensor_scalar(w.b2h[:], w.sel_raw[:, 0:P], 0.0, None, ALU.mult).then_inc(hi, 1)
        V.tensor_scalar(w.gT[:], w.sel_raw[:], 0.0, None, ALU.mult).then_inc(hi, 1)
        V.tensor_copy(w.sel[:], w.sel_raw[:]).then_inc(hi, 1)
        dve.wait_ge(hi, 4)
        V.tensor_copy(w.b2h[0:E1], w.b2[:]).then_inc(hi, 1)
        V.tensor_copy(w.b2h[LOW:], w.b2[:]).then_inc(hi, 1)
        dve.wait_ge(hi, 6)
        V.tensor_tensor(w.b2l[:], w.b2[:], w.b2h[0:E1].bitcast(F32), ALU.subtract).then_inc(lo, 1)


def ffn1_stage(nc, chip, w, out):
    names = ("bn_done stats_done eps_done rstd_done xn_done xnb_done xT_psum xT_sb xT_hi xT_lo q_psum k_psum v_psum qT_sb kT_sb v_sb "
             "s_psum s_max s_sub s_exp s_sum s_inv w_done wT_psum wT_sb o_psum x2_done res_done x2T_psum x2T_sb "
             "x2T_hi x2T_lo g_psum g_logit g_max g_sub g_exp g_sum g_inv gate_done gT_psum gT_hi gT_lo gb_psum gb_sb b2_psum acc_set "
             "up_psum relu_done hi_act hi_dve h_lo down_done scaled acc_done y_done yo_psum x_upd out_done half").split()
    S = {n: chip.sem("f1_" + n) for n in names}
    (bn_done, stats_done, eps_done, rstd_done, xn_done, xnb_done, xT_psum, xT_sb, xT_hi, xT_lo, q_psum, k_psum, v_psum, qT_sb,
     kT_sb, v_sb, s_psum, s_max, s_sub, s_exp, s_sum, s_inv, w_done, wT_psum, wT_sb, o_psum, x2_done, res_done,
     x2T_psum, x2T_sb, x2T_hi, x2T_lo, g_psum, g_logit, g_max, g_sub, g_exp, g_sum, g_inv, gate_done, gT_psum, gT_hi, gT_lo,
     gb_psum, gb_sb, b2_psum, acc_set, up_psum, relu_done, hi_act, hi_dve, h_lo, down_done, scaled, acc_done, y_done,
     yo_psum, x_upd, out_done, half_set) = (S[n] for n in names)
    RING, LAG = 4, 3
    END = C1 - 1 + LAG
    U, Y, GB, A, B, C = 0, 2, 4, 5, 6, 7
    with ExitStack() as own:
        def sb(name, shape, dt=F32):
            return own.enter_context(nc.sbuf_tensor("f1_" + name, shape, dt))

        prepare = PrepareMoe1(nc, chip, w)
        w2l = sb("w2l", [P, CI, P], F32R)
        w2l_flat = w2l[:].rearrange("p c d -> p (c d)")
        w_hi_done, w_lo_done = chip.sem("m1_w_hi_done"), chip.sem("m1_w_lo_done")
        pieces = [(w.spare[:, k:k + BANK], chip.w_hi[:, k:k + BANK], chip.w_lo[:, k:k + BANK]) for k in range(0, CI * P, BANK)] + [
            (w.w2_raw[k // INNER][:, k % INNER:k % INNER + BANK], chip.fused[:, k:k + BANK], w2l_flat[:, k:k + BANK])
            for k in range(0, CI * P, BANK)]
        bn = sb("bn", [P, G, 6])
        mv = sb("mv", [P, G, 2])
        rstd = sb("rstd", [P, G])
        var_eps = sb("var_eps", [P, G])
        minus_half = sb("minus_half", [P, G])
        eps = sb("eps", [P, G])
        xn = sb("xn", [P, G, P])
        xnb = sb("xnb", [P, G, P])
        xT = sb("xT", [P, GP])
        xTh = sb("xTh", [P, GP], F32R)
        xTl = sb("xTl", [P, GP], F32R)
        qT = sb("qT", [P, GP])
        kT = sb("kT", [P, GP])
        v = sb("v", [P, G, P])
        att = sb("att", [P, G, P])
        smax = sb("smax", [P, G])
        ssum = sb("ssum", [P, G])
        sinv = sb("sinv", [P, G])
        attT = sb("attT", [P, GP])
        x2 = sb("x2", [P, G, P])
        x2T = sb("x2T", [P, GP])
        x2h = sb("x2h", [P, 2 * GP], F32R)
        x2l = sb("x2l", [P, 2 * GP], F32R)
        gates = sb("gates", [P, G, E1])
        gmax = sb("gmax", [P, G])
        gsum = sb("gsum", [P, G])
        ginv = sb("ginv", [P, G])
        gT = w.gT
        hh = sb("hh", [P, RING, GP], F32R)
        hl = sb("hl", [P, RING, GP], F32R)
        spare = w.spare[:].rearrange("p (k c) -> p k c", c=GP)
        h, gb, part = spare[:, 0:RING], spare[:, RING:RING + 2], spare[:, RING + 2:RING + 4]
        acc, yT = spare[:, RING + 4], spare[:, RING + 5]
        block = own.enter_context(nc.Block())

        def item(s, u, late):
            return (s.has(0) if u >= late else s.has(-1)), (u - late) % CI, CI * s.g + u - late + 1

        def four(t):
            return t.rearrange("p (b d) -> p b d", b=G)

        def per_batch(t):
            return t.unsqueeze(2).broadcast_to([P, G, P])

        def all_batches(t, width):
            return t.unsqueeze(1).broadcast_to([P, G, width])

        def first(s):
            return isinstance(s.g, int) and s.g == -1

        def piece(s, u, late):
            return u - late if first(s) and 0 <= u - late < len(pieces) else None

        @block.sync
        def _(sp):
            with sp.Fori(0, NG) as g:
                sp.wait_ge(x_upd, g + 1)
                sp.dma_start(out[bass.ds(g * G, G)].rearrange("b t d -> t b d"), four(chip.xt(g * G, G))).then_inc(out_done, 16)
            sp.wait_ge(out_done, 16 * NG)

        @block.gpsimd
        def _(pool):
            nc.gpsimd.memset(minus_half[:], -0.5).then_inc(half_set, 1)
            nc.gpsimd.memset(eps[:], EPS).then_inc(half_set, 1)
            pool.wait_ge(half_set, 2)

            def step(s):
                g = s.g
                for u in range(CI):
                    if (u - END - 1) % 4 == 0:
                        late = END + 1
                        e = (u - late) // 4 % E1
                        if s.has(0) if u >= late else s.has(-1):
                            m = E1 * g + (u - late) // 4 + 1
                            pool.wait_ge(scaled, m)
                            if e == 0:
                                pool.wait_ge(acc_set, g + 1)
                            else:
                                pool.wait_ge(acc_done, (E1 - 1) * (g if u >= late else g - 1) + e)
                            if e < E1 - 1:
                                nc.gpsimd.tensor_tensor(acc, acc, part[:, e % 2], ALU.add).then_inc(acc_done, 1)
                            else:
                                nc.gpsimd.tensor_tensor(yT, acc, part[:, e % 2], ALU.add).then_inc(y_done, 1)
                    if u == 12 and s.has(-1):
                        pool.wait_ge(yo_psum, g)
                    if u == 2 and s.has(1):
                        pool.wait_ge(stats_done, G * (g + 2))
                        nc.gpsimd.tensor_tensor(var_eps[:], mv[:, :, 1], eps[:], ALU.add).then_inc(eps_done, 1)
                        pool.wait_ge(eps_done, g + 2)
                        need(pool, xn_done, G * (g + 1))
                        nc.gpsimd.tensor_tensor(rstd[:], var_eps[:], minus_half[:], ALU.pow).then_inc(rstd_done, 1)
                    if u == 4 and s.has(1):
                        pool.wait_ge(xn_done, G * (g + 2))
                        need(pool, x2_done, g + 1)
                        nc.gpsimd.tensor_tensor(xnb[:], xn[:], all_batches(w.bo[:], P), ALU.add).then_inc(xnb_done, 1)
                    if u == 22 and s.has(1):
                        pool.wait_ge(x2_done, g + 2)
                        xg = four(chip.xt(G * (g + 1), G))
                        nc.gpsimd.tensor_tensor(xg, xg, x2[:], ALU.add).then_inc(res_done, 1)
            run_groups(pool, step)

        @block.tensor
        def _(pe):
            T = nc.tensor

            def step(s):
                g = s.g
                at = (g % 2) * GP
                if first(s):
                    prepare.tensor(pe)
                for u in range(CI):
                    ok, cc, t = item(s, u, 0)
                    if ok:
                        if u == 0 and isinstance(g, int) and g == 0:
                            pe.wait_ge(w_lo_done, len(pieces))
                            pe.wait_ge(prepare.t_sb, 3)
                            pe.wait_ge(prepare.lo, 2)
                        if u == 0:
                            pe.wait_ge(x2T_hi, g + 1)
                            pe.wait_ge(x2T_lo, g + 1)
                        if u % 4 == 3:
                            if u == 3:
                                pe.wait_ge(gT_hi, g + 1)
                                pe.wait_ge(gT_lo, g + 1)
                            need(pe, gb_sb, E1 * g + u // 4)
                            if u == 7:
                                pe.wait_ge(acc_set, g + 1)
                        if u == 5:
                            pe.wait_ge(gb_sb, E1 * g + 1)
                        need(pe, relu_done, t - 2)
                        ws = slice(u * P, (u + 1) * P)
                        split3(T, chip.bank(U + u % 2, P, GP),
                               [(chip.w_hi[:, ws], chip.w_lo[:, ws], x2h[:, bass.ds(at, GP)], x2l[:, bass.ds(at, GP)])]).then_inc(up_psum, 1)
                        if u % 4 == 3:
                            e = u // 4
                            es = slice(e * P, (e + 1) * P)
                            T.matmul(chip.bank(GB, P, GP), w.sel[:, es], gT[:, bass.ds(at, GP)], start=True, stop=True).then_inc(gb_psum, 1)
                        if u == 5:
                            T.matmul(chip.bank(GB, P, GP), w.b2h[:], gT[:, bass.ds(at, GP)], start=True, stop=False)
                            T.matmul(chip.bank(GB, P, GP), w.b2l[:], gT[0:E1, bass.ds(at, GP)], start=False, stop=True).then_inc(b2_psum, 1)
                    ok, cc, t = item(s, u, LAG)
                    if ok:
                        b = cc % RING
                        pe.wait_ge(h_lo, t)
                        if cc % 4 == 0:
                            need(pe, scaled, E1 * (g if u >= LAG else g - 1) + cc // 4 - 1)
                        split3(T, chip.bank(Y + cc // 4 % 2, P, GP), [(w.w2h[:, cc], w2l[:, cc], hh[:, b], hl[:, b])],
                               first=cc % 4 == 0, last=cc % 4 == 3).then_inc(down_done, 1)
                    if u == 7 and s.has(1):
                        pe.wait_ge(xn_done, G * (g + 2))
                        need(pe, x2T_sb, g + 1)
                        for b in range(G):
                            last = T.transpose(chip.bank(A, P, P, b * P), xn[:, b], chip.ident[:])
                        last.then_inc(xT_psum, 1)
                    if u == 9 and first(s):
                        pe.wait_ge(prepare.lo, 1)
                    if u == 9 and s.has(1):
                        pe.wait_ge(xT_lo, g + 2)
                        need(pe, g_logit, g + 1)
                        split3(T, chip.bank(B, P, GP), [(w.qk_h[:, 0:P], w.qk_l[:, 0:P], xTh[:], xTl[:])]).then_inc(q_psum, 1)
                        need(pe, gT_lo, g + 1)
                        split3(T, chip.bank(C, P, GP), [(w.qk_h[:, P:], w.qk_l[:, P:], xTh[:], xTl[:])]).then_inc(k_psum, 1)
                    if u == 10 and first(s):
                        pe.wait_ge(prepare.t_sb, 3)
                    if u == 10 and s.has(1):
                        pe.wait_ge(xT_sb, g + 2)
                        for b in range(G):
                            last = T.matmul(chip.bank(A, P, P, b * P), xT[:, b * P:(b + 1) * P], w.vo[:, 0:P], start=True, stop=True)
                        last.then_inc(v_psum, 1)
                    if u == 12 and s.has(-1):
                        pe.wait_ge(y_done, g)
                        if s.has(1):
                            pe.wait_ge(qT_sb, g + 2)
                        for b in range(G):
                            last = T.transpose(chip.bank(B, P, P, b * P), yT[:, b * P:(b + 1) * P], chip.ident[:])
                        last.then_inc(yo_psum, 1)
                    if u == 11 and s.has(1):
                        pe.wait_ge(qT_sb, g + 2)
                        pe.wait_ge(kT_sb, g + 2)
                        for b in range(G):
                            bs = slice(b * P, (b + 1) * P)
                            last = T.matmul(chip.bank(C, P, P, b * P), qT[:, bs], kT[:, bs], start=True, stop=True)
                        last.then_inc(s_psum, 1)
                    if u == 16 and s.has(1):
                        pe.wait_ge(w_done, g + 2)
                        pe.wait_ge(v_sb, g + 2)
                        for b in range(G):
                            last = T.transpose(chip.bank(A, P, P, b * P), att[:, b], chip.ident[:])
                        last.then_inc(wT_psum, 1)
                    if u == 19 and s.has(1):
                        pe.wait_ge(wT_sb, g + 2)
                        pe.wait_ge(s_sub, g + 2)
                        for b in range(G):
                            last = T.matmul(chip.bank(C, P, P, b * P), attT[:, b * P:(b + 1) * P], v[:, b], start=True, stop=True)
                        last.then_inc(o_psum, 1)
                    if u == 24 and s.has(1):
                        pe.wait_ge(x2_done, g + 2)
                        pe.wait_ge(wT_sb, g + 2)
                        for b in range(G):
                            last = T.transpose(chip.bank(A, P, P, b * P), x2[:, b], chip.ident[:])
                        last.then_inc(x2T_psum, 1)
                    if u == 26 and s.has(1):
                        pe.wait_ge(x2T_sb, g + 2)
                        need(pe, x_upd, g)
                        for b in range(G):
                            last = T.matmul(chip.bank(B, P, E1, b * E1), x2T[:, b * P:(b + 1) * P], w.wg[:], start=True, stop=True)
                        last.then_inc(g_psum, 1)
                    if u == 31 and s.has(1):
                        pe.wait_ge(gate_done, g + 2)
                        pe.wait_ge(x2_done, g + 2)
                        for b in range(G):
                            last = T.transpose(chip.bank(C, E1, P, b * P), gates[:, b], chip.ident[:])
                        last.then_inc(gT_psum, 1)
            run_groups(pe, step)

        @block.scalar
        def _(act):
            cols = w.cols

            def step(s):
                g = s.g
                nxt = ((g + 1) % 2) * GP
                if first(s):
                    prepare.scalar(act)
                for u in range(CI):
                    ok, cc, t = item(s, u, 0)
                    if ok:
                        act.wait_ge(up_psum, t)
                        need(act, h_lo, t - RING)
                        nc.scalar.activation(h[:, cc % RING], chip.bank(U + u % 2, P, GP), ACT.Relu,
                                             bias=cols[:, cc:cc + 1]).then_inc(relu_done, 1)
                        if u % 2 == 0:
                            act.wait_ge(relu_done, t)
                            need(act, down_done, t - RING)
                            nc.scalar.copy(hh[:, cc % RING], h[:, cc % RING]).then_inc(hi_act, 1)
                        if u % 4 == 3:
                            e = u // 4
                            act.wait_ge(gb_psum, E1 * g + e + 1)
                            need(act, scaled, E1 * g + e - 1)
                            nc.scalar.copy(gb[:, e % 2], chip.bank(GB, P, GP)).then_inc(gb_sb, 1)
                        if u == 5:
                            act.wait_ge(b2_psum, g + 1)
                            need(act, y_done, g)
                            nc.scalar.copy(acc, chip.bank(GB, P, GP)).then_inc(acc_set, 1)
                    k = piece(s, u, 0)
                    if k is not None:
                        if k < len(pieces) // 2:
                            act.wait_ge(w.w1_loaded, 16)
                        else:
                            act.wait_ge(w.w2_loaded, 16 * len(w.w2_raw))
                        nc.scalar.copy(pieces[k][1], pieces[k][0]).then_inc(w_hi_done, 1)
                    if not s.has(1):
                        continue
                    if u == 7:
                        act.wait_ge(xT_psum, g + 2)
                        need(act, xT_lo, g + 1)
                        need(act, v_psum, g + 1)
                        nc.scalar.copy(xT[:], chip.bank(A, P, GP)).then_inc(xT_sb, 1)
                    if u == 10:
                        act.wait_ge(q_psum, g + 2)
                        need(act, s_psum, g + 1)
                        nc.scalar.activation(qT[:], chip.bank(B, P, GP), ACT.Identity, bias=cols[:, CI:CI + 1]).then_inc(qT_sb, 1)
                        act.wait_ge(k_psum, g + 2)
                        nc.scalar.activation(kT[:], chip.bank(C, P, GP), ACT.Identity, bias=cols[:, CI + 1:CI + 2]).then_inc(kT_sb, 1)
                    if u == 12:
                        act.wait_ge(s_sub, g + 2)
                        nc.scalar.activation(att[:], att[:], ACT.Exp, scale=P ** -0.5).then_inc(s_exp, 1)
                    if u == 16:
                        act.wait_ge(wT_psum, g + 2)
                        need(act, o_psum, g + 1)
                        nc.scalar.copy(attT[:], chip.bank(A, P, GP)).then_inc(wT_sb, 1)
                    if u == 24:
                        act.wait_ge(x2T_psum, g + 2)
                        need(act, g_psum, g + 1)
                        need(act, x2T_lo, g + 1)
                        nc.scalar.copy(x2T[:], chip.bank(A, P, GP)).then_inc(x2T_sb, 1)
                    if u == 28:
                        act.wait_ge(g_sub, g + 2)
                        nc.scalar.activation(gates[:], gates[:], ACT.Exp).then_inc(g_exp, 1)
                    if u == 31:
                        act.wait_ge(gT_psum, g + 2)
                        need(act, gb_psum, E1 * g)
                        need(act, b2_psum, g)
                        nc.scalar.copy(gT[0:E1, bass.ds(nxt, GP)], chip.bank(C, E1, GP)).then_inc(gT_hi, 1)
            run_groups(act, step)

        @block.vector
        def _(dve):
            V = nc.vector

            def step(s):
                g = s.g
                nxt = ((g + 1) % 2) * GP
                for u in range(CI):
                    if u == 1 and s.has(1):
                        dve.wait_ge(bn_done, G * (g + 2))
                    ok, cc, t = item(s, u, 0)
                    if ok:
                        b = cc % RING
                        if u % 2 == 0:
                            dve.wait_ge(hi_act, CI // 2 * g + u // 2 + 1)
                        else:
                            dve.wait_ge(relu_done, t)
                            need(dve, down_done, t - RING)
                            V.tensor_copy(hh[:, b], h[:, b]).then_inc(hi_dve, 1)
                            dve.wait_ge(hi_dve, CI // 2 * g + u // 2 + 1)
                        V.tensor_tensor(hl[:, b], h[:, b], hh[:, b].bitcast(F32), ALU.subtract).then_inc(h_lo, 1)
                    if (u - END) % 4 == 0 and (s.has(0) if u >= END else s.has(-1)):
                        e = (u - END) // 4 % E1
                        m = E1 * g + (u - END) // 4
                        dve.wait_ge(down_done, 4 * m + 4)
                        dve.wait_ge(gb_sb, m + 1)
                        if e >= 2:
                            dve.wait_ge(acc_done, (E1 - 1) * (g if u >= END else g - 1) + e - 1)
                        elif e == 1:
                            need(dve, y_done, g)
                        else:
                            need(dve, acc_done, (E1 - 1) * g)
                        V.tensor_tensor(part[:, e % 2], chip.bank(Y + e % 2, P, GP), gb[:, e % 2], ALU.mult).then_inc(scaled, 1)
                    if u == 12 and s.has(-1):
                        dve.wait_ge(yo_psum, g)
                        dve.wait_ge(res_done, g)
                        xg = chip.xt(G * (g - 1), G)
                        V.tensor_tensor(xg, xg, chip.bank(B, P, GP), ALU.add).then_inc(x_upd, 1)
                    k = piece(s, u, 1)
                    if k is not None:
                        dve.wait_ge(w_hi_done, k + 1)
                        V.tensor_tensor(pieces[k][2], pieces[k][0], pieces[k][1].bitcast(F32), ALU.subtract).then_inc(w_lo_done, 1)
                    if not s.has(1):
                        continue
                    if u == 0:
                        for b in range(G):
                            V.bn_stats(bn[:, b], chip.xt(G * (g + 1) + b)).then_inc(bn_done, 1)
                    if u == 1:
                        for b in range(G):
                            V.bn_aggr(mv[:, b], bn[:, b]).then_inc(stats_done, 1)
                        if first(s):
                            prepare.vector(dve)
                    if u == 3:
                        dve.wait_ge(rstd_done, g + 2)
                        need(dve, xT_psum, g + 1)
                        need(dve, xnb_done, g + 1)
                        for b in range(G):
                            V.tensor_scalar(xn[:, b], chip.xt(G * (g + 1) + b), mv[:, b, 0:1], rstd[:, b:b + 1],
                                            ALU.subtract, ALU.mult).then_inc(xn_done, 1)
                    if u == 6:
                        dve.wait_ge(xT_sb, g + 2)
                        need(dve, k_psum, g + 1)
                        V.tensor_copy(xTh[:], xT[:]).then_inc(xT_hi, 1)
                        dve.wait_ge(xT_hi, g + 2)
                        V.tensor_tensor(xTl[:], xT[:], xTh[:].bitcast(F32), ALU.subtract).then_inc(xT_lo, 1)
                    if u == 11:
                        if first(s):
                            dve.wait_ge(prepare.t_sb, 3)
                        dve.wait_ge(v_psum, g + 2)
                        need(dve, o_psum, g + 1)
                        V.tensor_tensor(v[:], four(chip.bank(A, P, GP)), all_batches(w.vo[:, P:], P), ALU.add).then_inc(v_sb, 1)
                    if u == 11:
                        dve.wait_ge(s_psum, g + 2)
                        V.tensor_reduce(smax[:], four(chip.bank(C, P, GP)), AX_X, ALU.max).then_inc(s_max, 1)
                        dve.wait_ge(s_max, g + 2)
                        need(dve, wT_psum, g + 1)
                        V.tensor_tensor(att[:], four(chip.bank(C, P, GP)), per_batch(smax[:]), ALU.subtract).then_inc(s_sub, 1)
                    if u == 12:
                        dve.wait_ge(s_exp, g + 2)
                        V.tensor_reduce(ssum[:], att[:], AX_X, ALU.add).then_inc(s_sum, 1)
                        dve.wait_ge(s_sum, g + 2)
                        V.reciprocal(sinv[:], ssum[:]).then_inc(s_inv, 1)
                        dve.wait_ge(s_inv, g + 2)
                        V.tensor_tensor(att[:], att[:], per_batch(sinv[:]), ALU.mult).then_inc(w_done, 1)
                    if u == 21:
                        dve.wait_ge(o_psum, g + 2)
                        dve.wait_ge(xnb_done, g + 2)
                        need(dve, x2T_psum, g + 1)
                        need(dve, res_done, g + 1)
                        V.tensor_tensor(x2[:], xnb[:], four(chip.bank(C, P, GP)), ALU.add).then_inc(x2_done, 1)
                    if u == 25:
                        dve.wait_ge(x2T_sb, g + 2)
                        need(dve, up_psum, CI * g)
                        V.tensor_copy(x2h[:, bass.ds(nxt, GP)], x2T[:]).then_inc(x2T_hi, 1)
                        dve.wait_ge(x2T_hi, g + 2)
                        V.tensor_tensor(x2l[:, bass.ds(nxt, GP)], x2T[:], x2h[:, bass.ds(nxt, GP)].bitcast(F32), ALU.subtract).then_inc(x2T_lo, 1)
                    if u == 27:
                        gl = chip.bank(B, P, G * E1).rearrange("p (b e) -> p b e", b=G)
                        dve.wait_ge(g_psum, g + 2)
                        need(dve, gT_psum, g + 1)
                        V.tensor_tensor(gates[:], gl, all_batches(w.bg[:], E1), ALU.add).then_inc(g_logit, 1)
                        dve.wait_ge(g_logit, g + 2)
                        V.tensor_reduce(gmax[:], gates[:], AX_X, ALU.max).then_inc(g_max, 1)
                        dve.wait_ge(g_max, g + 2)
                        V.tensor_tensor(gates[:], gates[:], gmax[:].unsqueeze(2).broadcast_to([P, G, E1]), ALU.subtract).then_inc(g_sub, 1)
                    if u == 29:
                        dve.wait_ge(g_exp, g + 2)
                        V.tensor_reduce(gsum[:], gates[:], AX_X, ALU.add).then_inc(g_sum, 1)
                        dve.wait_ge(g_sum, g + 2)
                        V.reciprocal(ginv[:], gsum[:]).then_inc(g_inv, 1)
                        dve.wait_ge(g_inv, g + 2)
                        V.tensor_tensor(gates[:], gates[:], ginv[:].unsqueeze(2).broadcast_to([P, G, E1]), ALU.mult).then_inc(gate_done, 1)
                    if u == 31:
                        dve.wait_ge(gT_hi, g + 2)
                        V.tensor_tensor(gT[LOW:, bass.ds(nxt, GP)], chip.bank(C, E1, GP), gT[0:E1, bass.ds(nxt, GP)].bitcast(F32),
                                        ALU.subtract).then_inc(gT_lo, 1)
            run_groups(dve, step)


def network(nc, a, out):
    with ExitStack() as ctx:
        chip = Chip(nc, ctx)
        prep_sems, xattn_sems = xattn_prep_sems(chip), {}
        x_rest = chip.sem("x_rest")
        x_sb, x_in = chip.x[:].rearrange("p (b d) -> p b d", b=NB), a["x"].rearrange("b t d -> t b d")
        of_layer = [{n[len("L0_xattn_"):]: t for n, t in a.items() if n.startswith(f"L{L}_xattn_")} for L in range(2)]
        wq, wk, wv, wo, bo = xattn_loads(chip, of_layer[0], prep_sems)
        first = [(chip.ident[:], a["ident"], prep_sems["w_loaded"]), wq, wk, wv,
                 (x_sb[:, 0:G], x_in[:, 0:G], prep_sems["o_loaded"]), wo, bo, (x_sb[:, G:], x_in[:, G:], x_rest)]
        for L in range(2):
            ffn = {n[len("L0_ffn_"):]: t for n, t in a.items() if n.startswith(f"L{L}_ffn_")}
            with ExitStack() as scope:
                weights = (Moe0Weights(nc, chip, scope, {**ffn, "pairs": a["pairs"], "before": a["before"]}) if L == 0 else
                           Moe1Weights(nc, chip, scope, {**ffn, "ones_rows": a["ones_rows"]}))
                prepare_xattn(nc, chip, L, prep_sems, loads=first if L == 0 else [])
                xattn_stage(nc, chip, L, a["ctx_768"], xattn_sems, weights.loads, x_rest)
                if L == 0:
                    moe0_stage(nc, chip, weights, xattn_loads(chip, of_layer[1], prep_sems))
                else:
                    ffn1_stage(nc, chip, weights, out)


_OUT = (NB, P, P)


def kernel(**inputs):
    import numpy as np
    import concourse.bacc as bacc
    from concourse import mybir as _mybir
    from concourse.bass_utils import run_bass_kernel_spmd

    f = np.float32
    rows = np.arange(NGRP)[:, None], np.arange(NGRP)[None]
    constants = {
        "ident": np.eye(P, dtype=f),
        "pairs": (np.arange(LOW + NE)[:, None] % LOW == np.arange(CR * P)[None] // FI).astype(f),
        "ones_rows": (np.arange(LOW + E1)[:, None] % LOW == np.arange(E1 * P)[None] // P).astype(f),
        "before": np.stack([rows[1] < rows[0], rows[1] > rows[0]]).astype(f).reshape(-1),
    }
    nc = bacc.Bacc("TRN2", target_bir_lowering=False, num_devices=1)
    arrays, a = {}, {}
    for name, t in {**inputs, **constants}.items():
        t = np.ascontiguousarray(t)
        arrays[f"in_{name}"] = t
        a[name] = nc.dram_tensor(f"in_{name}", t.shape, _mybir.dt.from_np(t.dtype), kind="ExternalInput").ap()
    out = nc.dram_tensor("out_0", _OUT, F32, kind="ExternalOutput").ap()
    network(nc, a, out)
    r = run_bass_kernel_spmd(nc, [arrays], core_ids=[0])
    return r.results[0]["out_0"]
```
